# Optimizing a Trainium2 kernel written in Bass

```python
import numpy as np
import jax
import jax.numpy as jnp

def _softmax(x, axis=-1):
    return jax.nn.softmax(x, axis=axis)

def _gelu(x):
    return jax.nn.gelu(x, approximate=True)

def _silu(x):
    return jax.nn.silu(x)

def _sigmoid(x):
    return jax.nn.sigmoid(x)

def _layernorm(x, axis=-1, eps=1e-05):
    m = jnp.mean(x, axis=axis, keepdims=True)
    v = jnp.var(x, axis=axis, keepdims=True)
    return (x - m) / jnp.sqrt(v + eps)

def _scatter_add(tgt, idx, src, axis=0):
    return tgt.at[idx].add(src)

def _segment_sum(src, seg, n):
    return jax.ops.segment_sum(src, seg, n)
kernel_name = 'mk_cond_seq_d2_seqx_r4_9dc53d'

def setup_inputs(seed: int=0):
    np.random.seed(seed)
    _w = jnp.asarray

    def _rec_inputs():
        import jax
        import jax.numpy as jnp
        _rk = jax.random.key(seed)
        x = -0.0003929 + 0.9999 * jax.random.normal(jax.random.fold_in(_rk, 1), (2, 1024, 256), jnp.float32)
        _lenS = 1024 - jax.random.randint(jax.random.fold_in(_rk, 7), (2,), 0, max(1, 1024 // 4) + 1, jnp.int32)
        _lenS2 = 1024 - jax.random.randint(jax.random.fold_in(_rk, 8), (2,), 0, max(1, 1024 // 4) + 1, jnp.int32)
        cond_1024 = 0.00782532 + 1.00527 * jax.random.normal(jax.random.fold_in(_rk, 11), (2, 256), jnp.float32)
        pos_S = jnp.arange(1024, dtype=jnp.int32)
        return (x, cond_1024, pos_S)
    x, cond_1024, pos_S = _rec_inputs()

    def _L0_cond_setup():
        import jax, jax.numpy as jnp
        import numpy as np
        B, L, D, P = (8, 512, 256, 64)

        def _ln(x):
            m = x.mean(-1, keepdims=True)
            v = x.var(-1, keepdims=True)
            return (x - m) * jax.lax.rsqrt(v + 1e-05)

        def _s5(u, Lam_re, Lam_im, B_re, B_im, C_re, C_im, D_diag, log_step):
            Lam = Lam_re + 1j * Lam_im
            dt = jnp.exp(log_step)
            Lam_bar = jnp.exp(Lam * dt)
            Bc = B_re + 1j * B_im
            B_bar = ((Lam_bar - 1.0) / Lam)[:, None] * Bc
            Bu = jnp.einsum('bld,pd->blp', u.astype(B_bar.dtype), B_bar)
            A = jnp.broadcast_to(Lam_bar, Bu.shape)

            def binop(e1, e2):
                a1, b1 = e1
                a2, b2 = e2
                return (a1 * a2, a2 * b1 + b2)
            _, xs = jax.lax.associative_scan(binop, (A, Bu), axis=1)
            Cc = C_re + 1j * C_im
            return 2.0 * jnp.einsum('blp,dp->bld', xs, Cc).real + D_diag * u
        key = jax.random.key(seed)
        ks = jax.random.split(key, 16)
        inp = {'y': jax.random.normal(ks[0], (B, L, D), jnp.float32), 't': jax.random.normal(ks[1], (B, D), jnp.float32), 'Wm': jax.random.normal(ks[2], (D, 6 * D), jnp.float32) * 0.02, 'bm': jax.random.normal(ks[3], (6 * D,), jnp.float32) * 0.02, 'Lam_re': -0.5 * jnp.ones((P,), jnp.float32), 'Lam_im': jnp.pi * jnp.arange(P, dtype=jnp.float32), 'B_re': jax.random.normal(ks[4], (P, D), jnp.float32) / np.sqrt(D), 'B_im': jax.random.normal(ks[5], (P, D), jnp.float32) / np.sqrt(D), 'C_re': jax.random.normal(ks[6], (D, P), jnp.float32) / np.sqrt(P), 'C_im': jax.random.normal(ks[7], (D, P), jnp.float32) / np.sqrt(P), 'D_diag': jax.random.normal(ks[8], (D,), jnp.float32), 'log_step': jax.random.uniform(ks[9], (P,), jnp.float32, np.log(0.001), np.log(0.1)), 'Wc': jax.random.normal(ks[10], (D, 2 * D), jnp.float32) * 0.02, 'bc': jax.random.normal(ks[11], (2 * D,), jnp.float32) * 0.02, 'W1': jax.random.normal(ks[12], (D, 4 * D), jnp.float32) / np.sqrt(D), 'b1': jnp.zeros((4 * D,), jnp.float32), 'W2': jax.random.normal(ks[13], (4 * D, D), jnp.float32) / np.sqrt(4 * D) * 0.1, 'b2': jnp.zeros((D,), jnp.float32)}
        return inp
    _L0_cond_all = _L0_cond_setup()
    _L0_cond_in = {k: v for k, v in _L0_cond_all.items() if k in ('Wm', 'bm', 'Lam_re', 'Lam_im', 'B_re', 'B_im', 'C_re', 'C_im', 'D_diag', 'log_step', 'Wc', 'bc', 'W1', 'b1', 'W2', 'b2')}
    del _L0_cond_all

    def _L1_cond_setup():
        import jax, jax.numpy as jnp
        import numpy as np
        EPS = 1e-06
        NUM_HEADS = 16

        def _rms(x, w=None):
            y = x * jax.lax.rsqrt(jnp.mean(x * x, axis=-1, keepdims=True) + EPS)
            return y if w is None else y * w

        def _rope(q, k, pos):
            dh = q.shape[-1]
            half = dh // 2
            freqs = 1.0 / 10000.0 ** (jnp.arange(half, dtype=jnp.float32) / half)
            ang = pos.astype(jnp.float32)[:, None] * freqs[None, :]
            cos = jnp.concatenate([jnp.cos(ang), jnp.cos(ang)], -1)
            sin = jnp.concatenate([jnp.sin(ang), jnp.sin(ang)], -1)

            def rot(v):
                v1, v2 = jnp.split(v, 2, axis=-1)
                return jnp.concatenate([-v2, v1], -1)
            return (q * cos + rot(q) * sin, k * cos + rot(k) * sin)
        key = jax.random.key(seed)
        ks = jax.random.split(key, 12)
        B, T, D, H = (2, 512, 256, NUM_HEADS)
        Dh = D // H
        Hm = 704
        s = lambda fan_in: 1.0 / np.sqrt(fan_in)
        return {'x': jax.random.normal(ks[0], (B, T, D), jnp.float32), 'c': jax.random.normal(ks[1], (B, D), jnp.float32), 'pos': jnp.arange(T, dtype=jnp.int32), 'adaln_w': jax.random.normal(ks[2], (D, 6 * D), jnp.float32) * s(D) * 0.1, 'adaln_b': jax.random.normal(ks[3], (6 * D,), jnp.float32) * 0.02, 'qkv_w': jax.random.normal(ks[4], (D, 3 * D), jnp.float32) * s(D), 'lnq_w': jnp.ones((Dh,), jnp.float32), 'lnk_w': jnp.ones((Dh,), jnp.float32), 'proj_w': jax.random.normal(ks[5], (D, D), jnp.float32) * s(D), 'proj_b': jnp.zeros((D,), jnp.float32), 'w1_w': jax.random.normal(ks[6], (D, Hm), jnp.float32) * s(D), 'w3_w': jax.random.normal(ks[7], (D, Hm), jnp.float32) * s(D), 'w2_w': jax.random.normal(ks[8], (Hm, D), jnp.float32) * s(Hm)}
    _L1_cond_all = _L1_cond_setup()
    _L1_cond_in = {k: v for k, v in _L1_cond_all.items() if k in ('adaln_w', 'adaln_b', 'qkv_w', 'lnq_w', 'lnk_w', 'proj_w', 'proj_b', 'w1_w', 'w3_w', 'w2_w')}
    del _L1_cond_all
    return {'x': x, 'cond_1024': cond_1024, 'pos_S': pos_S, 'L0_cond_Wm': _L0_cond_in['Wm'], 'L0_cond_bm': _L0_cond_in['bm'], 'L0_cond_Lam_re': _L0_cond_in['Lam_re'], 'L0_cond_Lam_im': _L0_cond_in['Lam_im'], 'L0_cond_B_re': _L0_cond_in['B_re'], 'L0_cond_B_im': _L0_cond_in['B_im'], 'L0_cond_C_re': _L0_cond_in['C_re'], 'L0_cond_C_im': _L0_cond_in['C_im'], 'L0_cond_D_diag': _L0_cond_in['D_diag'], 'L0_cond_log_step': _L0_cond_in['log_step'], 'L0_cond_Wc': _L0_cond_in['Wc'], 'L0_cond_bc': _L0_cond_in['bc'], 'L0_cond_W1': _L0_cond_in['W1'], 'L0_cond_b1': _L0_cond_in['b1'], 'L0_cond_W2': _L0_cond_in['W2'], 'L0_cond_b2': _L0_cond_in['b2'], 'L1_cond_adaln_w': _L1_cond_in['adaln_w'], 'L1_cond_adaln_b': _L1_cond_in['adaln_b'], 'L1_cond_qkv_w': _L1_cond_in['qkv_w'], 'L1_cond_lnq_w': _L1_cond_in['lnq_w'], 'L1_cond_lnk_w': _L1_cond_in['lnk_w'], 'L1_cond_proj_w': _L1_cond_in['proj_w'], 'L1_cond_proj_b': _L1_cond_in['proj_b'], 'L1_cond_w1_w': _L1_cond_in['w1_w'], 'L1_cond_w3_w': _L1_cond_in['w3_w'], 'L1_cond_w2_w': _L1_cond_in['w2_w']}

def reference(x, cond_1024, pos_S, L0_cond_Wm, L0_cond_bm, L0_cond_Lam_re, L0_cond_Lam_im, L0_cond_B_re, L0_cond_B_im, L0_cond_C_re, L0_cond_C_im, L0_cond_D_diag, L0_cond_log_step, L0_cond_Wc, L0_cond_bc, L0_cond_W1, L0_cond_b1, L0_cond_W2, L0_cond_b2, L1_cond_adaln_w, L1_cond_adaln_b, L1_cond_qkv_w, L1_cond_lnq_w, L1_cond_lnk_w, L1_cond_proj_w, L1_cond_proj_b, L1_cond_w1_w, L1_cond_w3_w, L1_cond_w2_w):
    import jax
    import jax.numpy as jnp

    def _L0_cond_ref(y, t, Wm, bm, Lam_re, Lam_im, B_re, B_im, C_re, C_im, D_diag, log_step, Wc, bc, W1, b1, W2, b2):
        import jax, jax.numpy as jnp
        import numpy as np
        B, L, D, P = (8, 512, 256, 64)

        def _ln(x):
            m = x.mean(-1, keepdims=True)
            v = x.var(-1, keepdims=True)
            return (x - m) * jax.lax.rsqrt(v + 1e-05)

        def _s5(u, Lam_re, Lam_im, B_re, B_im, C_re, C_im, D_diag, log_step):
            Lam = Lam_re + 1j * Lam_im
            dt = jnp.exp(log_step)
            Lam_bar = jnp.exp(Lam * dt)
            Bc = B_re + 1j * B_im
            B_bar = ((Lam_bar - 1.0) / Lam)[:, None] * Bc
            Bu = jnp.einsum('bld,pd->blp', u.astype(B_bar.dtype), B_bar)
            A = jnp.broadcast_to(Lam_bar, Bu.shape)

            def binop(e1, e2):
                a1, b1 = e1
                a2, b2 = e2
                return (a1 * a2, a2 * b1 + b2)
            _, xs = jax.lax.associative_scan(binop, (A, Bu), axis=1)
            Cc = C_re + 1j * C_im
            return 2.0 * jnp.einsum('blp,dp->bld', xs, Cc).real + D_diag * u
        mod = t @ Wm + bm
        shift_a, scale_a, gate_a, shift_ff, scale_ff, gate_ff = jnp.split(mod, 6, axis=-1)
        y_mod = _ln(y) * (1 + scale_a[:, None]) + shift_a[:, None]
        a_y = _s5(y_mod, Lam_re, Lam_im, B_re, B_im, C_re, C_im, D_diag, log_step)
        y = y + gate_a[:, None] * a_y
        cond = t @ Wc + bc
        scale_c, shift_c = jnp.split(cond, 2, axis=-1)
        y_norm = _ln(y) * (1 + scale_c[:, None]) + shift_c[:, None]
        y_mod = y_norm * (1 + scale_ff[:, None]) + shift_ff[:, None]
        h = jax.nn.gelu(y_mod @ W1 + b1)
        ff_y = h @ W2 + b2
        return y + gate_ff[:, None] * ff_y

    def _L1_cond_ref(x, c, pos, adaln_w, adaln_b, qkv_w, lnq_w, lnk_w, proj_w, proj_b, w1_w, w3_w, w2_w):
        import jax, jax.numpy as jnp
        import numpy as np
        EPS = 1e-06
        NUM_HEADS = 16

        def _rms(x, w=None):
            y = x * jax.lax.rsqrt(jnp.mean(x * x, axis=-1, keepdims=True) + EPS)
            return y if w is None else y * w

        def _rope(q, k, pos):
            dh = q.shape[-1]
            half = dh // 2
            freqs = 1.0 / 10000.0 ** (jnp.arange(half, dtype=jnp.float32) / half)
            ang = pos.astype(jnp.float32)[:, None] * freqs[None, :]
            cos = jnp.concatenate([jnp.cos(ang), jnp.cos(ang)], -1)
            sin = jnp.concatenate([jnp.sin(ang), jnp.sin(ang)], -1)

            def rot(v):
                v1, v2 = jnp.split(v, 2, axis=-1)
                return jnp.concatenate([-v2, v1], -1)
            return (q * cos + rot(q) * sin, k * cos + rot(k) * sin)
        B, T, D = x.shape
        H = NUM_HEADS
        Dh = D // H
        mods = jax.nn.silu(c) @ adaln_w + adaln_b
        shift_msa, scale_msa, gate_msa, shift_mlp, scale_mlp, gate_mlp = jnp.split(mods, 6, axis=-1)
        x_mod = _rms(x) * (1.0 + scale_msa[:, None, :]) + shift_msa[:, None, :]
        qkv = x_mod @ qkv_w
        q, k, v = jnp.split(qkv, 3, axis=-1)
        q = q.reshape(B, T, H, Dh).transpose(0, 2, 1, 3)
        k = k.reshape(B, T, H, Dh).transpose(0, 2, 1, 3)
        v = v.reshape(B, T, H, Dh).transpose(0, 2, 1, 3)
        q = _rms(q, lnq_w)
        k = _rms(k, lnk_w)
        q, k = _rope(q, k, pos)
        scores = jnp.einsum('bhqd,bhkd->bhqk', q, k) / jnp.sqrt(jnp.float32(Dh))
        attn = jax.nn.softmax(scores, axis=-1)
        attn_out = jnp.einsum('bhqk,bhkd->bhqd', attn, v)
        attn_out = attn_out.transpose(0, 2, 1, 3).reshape(B, T, D)
        x = x + gate_msa[:, None, :] * (attn_out @ proj_w + proj_b)
        h = _rms(x) * (1.0 + scale_mlp[:, None, :]) + shift_mlp[:, None, :]
        mlp = jax.nn.silu(h @ w1_w) * (h @ w3_w) @ w2_w
        x = x + gate_mlp[:, None, :] * mlp
        return x
    x = _L0_cond_ref(x, cond_1024, L0_cond_Wm, L0_cond_bm, L0_cond_Lam_re, L0_cond_Lam_im, L0_cond_B_re, L0_cond_B_im, L0_cond_C_re, L0_cond_C_im, L0_cond_D_diag, L0_cond_log_step, L0_cond_Wc, L0_cond_bc, L0_cond_W1, L0_cond_b1, L0_cond_W2, L0_cond_b2)
    x = _L1_cond_ref(x, cond_1024, pos_S, L1_cond_adaln_w, L1_cond_adaln_b, L1_cond_qkv_w, L1_cond_lnq_w, L1_cond_lnk_w, L1_cond_proj_w, L1_cond_proj_b, L1_cond_w1_w, L1_cond_w3_w, L1_cond_w2_w)
    return x

_drawn_inputs = setup_inputs


def setup_inputs(seed=0):
    import zlib

    import numpy as np

    out = dict(_drawn_inputs(seed))
    spreads = {'L0_cond_Lam_re': (-0.5, 0.6),
     'L0_cond_b1': (0.0, 0.8),
     'L0_cond_b2': (0.0, 0.312),
     'L1_cond_lnq_w': (1.0, 0.6),
     'L1_cond_lnk_w': (1.0, 0.6),
     'L1_cond_proj_b': (0.0, 0.8)}
    factors = {'L0_cond_Wc': 5.808,
     'L0_cond_bc': 8.0,
     'L0_cond_W1': 2.715,
     'L1_cond_adaln_b': 4.804,
     'L1_cond_qkv_w': 5.642,
     'L1_cond_proj_w': 5.384}
    for name, (base, spread) in spreads.items():
        noise = np.random.default_rng([zlib.crc32(name.encode()), seed]).standard_normal(out[name].shape)
        drawn = base * np.exp(spread * noise) if base else spread * noise
        out[name] = jnp.asarray(drawn.astype(out[name].dtype))
    for name, factor in factors.items():
        out[name] = (out[name] * factor).astype(out[name].dtype)
    return out
```

```python
from contextlib import ExitStack

import numpy as np
import concourse.bass as bass
from concourse import mybir

F32 = mybir.dt.float32
BF16 = mybir.dt.bfloat16
I32 = mybir.dt.int32
ACT = mybir.ActivationFunctionType
ALU = mybir.AluOpType
AX = mybir.AxisListType

B, T, D = 2, 1024, 256
P = 128
CH = 512
HC = T // CH
TT = CH // P
NT = T // P
KD = D // P
S = 64
F = 4 * D
FC = F // P
NH, DH = 16, 16
HM = 704
MC = (HM + P - 1) // P
QD = 4
NQ = NH // QD
SP_ROWS = 6 * DH
ST_ROWS = SP_ROWS + 3
LN_EPS, RMS_EPS = 1e-5, 1e-6
MAGIC = 12582912.0
INV2PI = float(np.float32(1.0 / (2 * np.pi)))
TWO_PI_HI = 6.28125
TWO_PI_LO = float(np.float32(2 * np.pi - 6.28125))
LN2_HI = 0.693359375
LN2_LO = float(np.float32(np.log(2.0) - 0.693359375))


def build(nc, A):
    es = ExitStack()
    with es:
        def sb(name, shape, dt=F32):
            return es.enter_context(nc.sbuf_tensor(name, shape, dt))

        def sem(name):
            return es.enter_context(nc.semaphore(name))

        P01, P23, P45, P67 = [es.enter_context(nc.psum_tensor(n, [P, 2 * CH], F32)) for n in ("P01", "P23", "P45", "P67")]

        x_tok = sb("x_tok", [P, B * NT, D])
        xn = sb("xn", [P, TT, D])
        uT = [sb(f"uT{h}", [P, KD, CH]) for h in range(2)]
        w_ff1 = sb("w_ff1", [P, KD, F])
        w_ff2 = sb("w_ff2", [P, FC, D])
        w_qkv = sb("w_qkv", [P, KD, 3 * D])
        w_proj = sb("w_proj", [P, KD, D])
        w_g1 = sb("w_g1", [P, KD, HM])
        w_g3 = sb("w_g3", [P, KD, HM])
        w_g2 = sb("w_g2", [P, MC, D])
        b_ff1 = sb("b_ff1", [P, FC])
        row_b2 = sb("row_b2", [1, D])
        row_pb = sb("row_pb", [1, D])
        ones_row = sb("ones_row", [1, P])
        ident = sb("ident", [P, P])
        ident_bf = sb("ident_bf", [P, P], BF16)
        gate = sb("gate", [P, 4, B, D])
        scal = sb("scal", [P, 8, KD, B])
        SH_A, SC_A, SC_FF, SH_FF, SH_MSA, SC_MSA, SH_MLP, SC_MLP = range(8)
        tmp = [sb(f"tmp{q}", [P, 2, D]) for q in range(2)]
        qnm = sb("qnm", [P, 5, 2 * NH])
        bn6 = sb("bn6", [P, TT, 6])
        mv = sb("mv", [P, TT, 2])
        nrm = sb("nrm", [P, 5, TT])
        ropeA = sb("ropeA", [P, NT, 2, DH])
        ropeB = sb("ropeB", [P, NT, 2, DH])
        v_tok = sb("v_tok", [P, NT, D])
        v_quad = sb("v_quad", [P, NT, QD, 32])
        attn = sb("attn", [P, NT, D])
        work = sb("work", [P, 8192])
        stacks = sb("stacks", [P, 2, NH, T], BF16)
        q_st = stacks[:, 0]
        k_st = stacks[:, 1]

        def carve(base, at, shape, dt=F32):
            n = int(np.prod(shape[1:])) * (2 if dt == BF16 else 4) // 4
            ap = base[0:shape[0], at:at + n]
            if dt != F32:
                ap = ap.bitcast(dt)
            if len(shape) == 3:
                ap = ap.rearrange("p (a b) -> p a b", a=shape[1])
            if len(shape) == 4:
                ap = ap.rearrange("p (a b c) -> p a b c", a=shape[1], b=shape[2])
            return ap, at + n

        at = 0
        w_mod, at = carve(work, at, [P, KD, 6 * D])
        w_cond, at = carve(work, at, [P, KD, 2 * D])
        w_ada, at = carve(work, at, [P, KD, 6 * D])
        row_gate, at = carve(work, at, [1, 4, D])
        hT, _ = carve(work, 0, [P, FC, CH])
        gT, _ = carve(work, 0, [P, MC, CH])
        sil, _ = carve(work, MC * CH, [P, 2, CH])
        at = 0
        sq, at = carve(work, at, [P, 2, CH])
        qn, at = carve(work, at, [P, 2, CH])
        ra, at = carve(work, at, [P, 2, CH])
        rb, at = carve(work, at, [P, CH])
        r1, at = carve(work, at, [P, CH])
        hb, at = carve(work, at, [P, 2, CH], BF16)
        mb, at = carve(work, at, [P, 2, CH], BF16)
        split, at = carve(work, at, [P, 2, 2 * NH * SP_ROWS], BF16)
        assert at <= 8192
        probs = work[:, :].rearrange("p (s h q) -> p s h q", s=2, h=QD)
        sreg = stacks[:, :, :, :].rearrange("p a h t -> p (a h t)").bitcast(F32)
        at = 0
        cosT, at = carve(sreg, at, [P, T])
        sinT, at = carve(sreg, at, [P, T])
        scr0, at = carve(sreg, at, [P, T])
        scr1, at = carve(sreg, at, [P, T])
        iota, at = carve(sreg, at, [P, T])
        decay, at = carve(sreg, at, [P, CH])
        b_nat, at = carve(sreg, at, [P, 2, D])
        b_T, at = carve(sreg, at, [P, 2, KD, P])
        c_nat, at = carve(sreg, at, [P, 2, KD, P])
        c_T, at = carve(sreg, at, [P, 2, D])
        c_w, at = carve(sreg, at, [P, 2, D])
        c_gated, at = carve(sreg, at, [P, B, 2, D])
        d_diag, at = carve(sreg, at, [P, B, KD, P])
        d_vec, at = carve(sreg, at, [P, KD])
        d_gate, at = carve(sreg, at, [P, KD, B])
        s_cos, at = carve(sreg, at, [P, CH])
        s_sin, at = carve(sreg, at, [P, CH])
        s_in, at = carve(sreg, at, [P, CH])
        s_y, at = carve(sreg, at, [P, 2, CH])
        s_z, at = carve(sreg, at, [P, 2, CH])
        condT, at = carve(sreg, at, [P, KD, B])
        csilu, at = carve(sreg, at, [P, KD, B])
        cond_b, at = carve(sreg, at, [P, KD, B, P])
        silu_b, at = carve(sreg, at, [P, KD, B, P])
        bias28, at = carve(sreg, at, [P, 28])
        mods, at = carve(sreg, at, [P, 28, B])
        prm, at = carve(sreg, at, [P, 48])
        pos_i, at = carve(sreg, at, [P, NT])
        ang, at = carve(sreg, at, [P, 6, NT * 8])
        freq, at = carve(sreg, at, [P, 8])
        lnw, at = carve(sreg, at, [P, 2, DH])
        assert at <= NH * T, at
        pmax = sb("pmax", [P, QD, NT, 2])
        negm = sb("negm", [P, 3, QD * NT])
        shift3 = sb("shift3", [P, 3 * QD * NT], BF16)
        shiftT = sb("shiftT", [3 * QD * NT, P], BF16)
        pv_sb = uT[0][:, :, :].rearrange("p k n -> p (k n)")
        rden = sb("rden", [P, NT, QD])

        ld_x = sem("ld_x")
        ld_cond = sem("ld_cond")
        ld_adaln = sem("ld_adaln")
        ld_s5 = sem("ld_s5")
        ld_ffn = sem("ld_ffn")
        ld_blk = sem("ld_blk")
        passed = sem("passed")
        ones_set = sem("ones_set")
        consts = sem("consts")
        dve_pre = sem("dve_pre")
        act_silu = sem("act_silu")
        act_trig = sem("act_trig")
        trig_ready = sem("trig_ready")
        cond_ready = sem("cond_ready")
        mods_mm = sem("mods_mm")
        gates_mm = sem("gates_mm")
        bneg = sem("bneg")
        bc_T = sem("bc_T")
        s5_w = sem("s5_w")
        xn_ready = sem("xn_ready")
        tr_ready = sem("tr_ready")
        u_ready = sem("u_ready")
        u_used = sem("u_used")
        out_ready = sem("out_ready")
        out_used = sem("out_used")
        x_upd = sem("x_upd")
        nstep = sem("nstep")
        sstep = sem("sstep")
        bu_ready = sem("bu_ready")
        z_ready = sem("z_ready")
        h_ready = sem("h_ready")
        gelu_done = sem("gelu_done")
        qk_ready = sem("qk_ready")
        v_ready = sem("v_ready")
        sq_ready = sem("sq_ready")
        qn_done = sem("qn_done")
        v_copied = sem("v_copied")
        rope_done = sem("rope_done")
        qnstep = sem("qnstep")
        qsstep = sem("qsstep")
        part_ready = sem("part_ready")
        split_act = sem("split_act")
        stkT_act = sem("stkT_act")
        stkT_dve = sem("stkT_dve")
        stk_act = sem("stk_act")
        stk_dve = sem("stk_dve")
        mx_ready = sem("mx_ready")
        mx_used = sem("mx_used")
        mstep = sem("mstep")
        shT_ready = sem("shT_ready")
        shT_copied = sem("shT_copied")
        shift_dma = sem("shift_dma")
        st_ready = sem("st_ready")
        p_ready = sem("p_ready")
        pv_step = sem("pv_step")
        vq_ready = sem("vq_ready")
        pv_copied = sem("pv_copied")
        pvT_ready = sem("pvT_ready")
        astep = sem("astep")
        attn_done = sem("attn_done")
        g_ready = sem("g_ready")
        sil_ready = sem("sil_ready")
        gm_done = sem("gm_done")
        st_out = sem("st_out")

        class Steps:
            def __init__(self, eng, s, base=0):
                self.eng, self.s, self.base, self.n = eng, s, base, 0

            def __call__(self, ins):
                ins.then_inc(self.s, 1)
                self.n += 1

            def wait(self):
                self.eng.wait_ge(self.s, self.base + self.n)

        LN_STEPS, RMS_STEPS = 21, 22
        SCAN_STEPS = 5
        QN_STEPS, QS_STEPS = 14, 2
        SHIFT_STEPS = 6

        def settle(eng):
            eng.sem_inc(passed, 1)

        def tok(c):
            return bass.ds(TT * c, TT)

        es.enter_context(nc.allow_non_contiguous_dma(reason="small vectors, one element a partition"))
        block = es.enter_context(nc.Block())

        @block.sync
        def _(sp):
            d = sp.dma_start
            for k in range(KD):
                d(condT[:, k, :], A["cond_1024"][:, k * P:(k + 1) * P].rearrange("b p -> p b")).then_inc(ld_cond, 16)
            d(w_mod, A["L0_cond_Wm"].rearrange("(k p) n -> p k n", p=P)).then_inc(ld_adaln, 16)
            d(w_cond, A["L0_cond_Wc"].rearrange("(k p) n -> p k n", p=P)).then_inc(ld_adaln, 16)
            d(w_ada, A["L1_cond_adaln_w"].rearrange("(k p) n -> p k n", p=P)).then_inc(ld_adaln, 16)
            for i, (n, lo) in enumerate((("L0_cond_bm", 2), ("L0_cond_bm", 5), ("L1_cond_adaln_b", 2), ("L1_cond_adaln_b", 5))):
                d(row_gate[:, i, :], A[n][lo * D:(lo + 1) * D].unsqueeze(0)).then_inc(ld_adaln, 16)
            for n, lo, w in (("L0_cond_bm", 0, 12), ("L0_cond_bc", 12, 4), ("L1_cond_adaln_b", 16, 12)):
                d(bias28[:, lo:lo + w], A[n].rearrange("(m p) -> p m", p=P)).then_inc(ld_adaln, 16)
            d(x_tok[:, :, :], A["x"].rearrange("(t p) d -> p t d", p=P)).then_inc(ld_x, 16)
            d(w_ff1[:, :, :], A["L0_cond_W1"].rearrange("(k p) n -> p k n", p=P)).then_inc(ld_ffn, 16)
            d(w_ff2[:, :, :], A["L0_cond_W2"].rearrange("(k p) n -> p k n", p=P)).then_inc(ld_ffn, 16)
            d(b_ff1[:, :], A["L0_cond_b1"].rearrange("(m p) -> p m", p=P)).then_inc(ld_ffn, 16)
            d(row_b2[:, :], A["L0_cond_b2"].unsqueeze(0)).then_inc(ld_ffn, 16)
            d(w_qkv[:, :, :], A["L1_cond_qkv_w"].rearrange("(k p) n -> p k n", p=P)).then_inc(ld_blk, 16)
            d(w_proj[:, :, :], A["L1_cond_proj_w"].rearrange("(k p) n -> p k n", p=P)).then_inc(ld_blk, 16)
            d(row_pb[:, :], A["L1_cond_proj_b"].unsqueeze(0)).then_inc(ld_blk, 16)
            d(w_g1[:, :, :], A["L1_cond_w1_w"].rearrange("(k p) n -> p k n", p=P)).then_inc(ld_blk, 16)
            d(w_g3[:, :, :], A["L1_cond_w3_w"].rearrange("(k p) n -> p k n", p=P)).then_inc(ld_blk, 16)
            full = HM // P
            d(w_g2[:, 0:full, :], A["L1_cond_w2_w"][0:full * P].rearrange("(k p) n -> p k n", p=P)).then_inc(ld_blk, 16)
            d(w_g2[0:HM - full * P, full, :], A["L1_cond_w2_w"][full * P:HM]).then_inc(ld_blk, 16)

            def send_shift(b, m):
                sp.wait_ge(shT_copied, 4 * b + m + 1)
                for s in range(3):
                    dst = q_st[SP_ROWS + s:SP_ROWS + s + 1, bass.ds(QD * m, QD), :].rearrange("s h (t q) -> s (h t) q", q=P)
                    d(dst, shiftT[QD * NT * s:QD * NT * (s + 1), :]).then_inc(shift_dma, 16)

            with sp.Fori(0, B) as b:
                send_shift(b, 0)
                with sp.Fori(0, NQ - 1) as n:
                    send_shift(b, n + 1)
                for h in range(HC):
                    c = HC * b + h
                    sp.wait_ge(x_upd, 2 * (4 + 4 * b + 2 * h + 2))
                    d(A["out"].rearrange("(t p) d -> p t d", p=P)[:, tok(c), :], x_tok[:, tok(c), :]).then_inc(st_out, 16)
            sp.wait_ge(st_out, 16 * B * HC)

        @block.gpsimd
        def _(pool):
            d = pool.dma_start
            for i, n in enumerate(("L0_cond_Lam_re", "L0_cond_Lam_im", "L0_cond_log_step")):
                for z in range(2):
                    d(prm[z * S:(z + 1) * S, i:i + 1], A[n].unsqueeze(1)).then_inc(ld_s5, 16)
            for z, (top, bot) in enumerate((("re", "im"), ("im", "re"))):
                d(b_nat[0:S, z, :], A[f"L0_cond_B_{top}"]).then_inc(ld_s5, 16)
                d(b_nat[S:P, z, :], A[f"L0_cond_B_{bot}"]).then_inc(ld_s5, 16)
                d(c_nat[:, z, :, 0:S], A[f"L0_cond_C_{top}"].rearrange("(k p) s -> p k s", p=P)).then_inc(ld_s5, 16)
                d(c_nat[:, z, :, S:P], A[f"L0_cond_C_{bot}"].rearrange("(k p) s -> p k s", p=P)).then_inc(ld_s5, 16)
            d(d_vec, A["L0_cond_D_diag"].rearrange("(k p) -> p k", p=P)).then_inc(ld_s5, 16)
            d(pos_i.bitcast(I32), A["pos_S"].rearrange("(t p) -> p t", p=P)).then_inc(ld_s5, 16)
            d(lnw[:, 0, :], A["L1_cond_lnq_w"].partition_broadcast(P)).then_inc(ld_s5, 16)
            d(lnw[:, 1, :], A["L1_cond_lnk_w"].partition_broadcast(P)).then_inc(ld_s5, 16)

            g = nc.gpsimd
            g.memset(ident[:, :], 0.0).then_inc(consts, 1)
            g.iota(scr1.bitcast(I32), pattern=[[1, T]], base=0, channel_multiplier=0).then_inc(consts, 1)
            pool.wait_ge(consts, 2)
            g.affine_select(out=ident[:, :], in_=ident[:, :], compare_op=ALU.not_equal, fill=1.0,
                            base=0, pattern=[[-1, P]], channel_multiplier=1).then_inc(consts, 1)
            g.tensor_copy(iota, scr1.bitcast(I32)).then_inc(consts, 1)
            pool.wait_ge(consts, 4)
            g.tensor_copy(ident_bf[:, :], ident[:, :]).then_inc(consts, 1)
            g.memset(ones_row[:, :], 1.0).then_inc(consts, 1)
            g.memset(v_quad[:, :, :, :], 0.0).then_inc(consts, 1)
            pool.wait_ge(consts, 7)
            g.memset(v_quad[:, :, :, DH:DH + 1], 1.0).then_inc(consts, 1)

            def rotate(b, t):
                i = NT * b + t
                z = t % 2
                pool.wait_ge(qn_done, i + 2)
                pool.wait_ge(rope_done, 4 * i)
                if t >= 2:
                    pool.wait_ge(part_ready, 3 * (i - 1))
                src = qn[:, z, :].rearrange("p (a h d) -> p a h d", a=2, h=NH)
                dst_a = ra[:, z, :].rearrange("p (a h d) -> p a h d", a=2, h=NH)
                dst_b = rb.rearrange("p (a h d) -> p a h d", a=2, h=NH)
                ca = ropeA[:, t, :, :].unsqueeze(2).to_broadcast([P, 2, NH, DH])
                g.tensor_tensor(out=dst_a, in0=src, in1=ca, op=ALU.mult).then_inc(rope_done, 1)
                e = DH // 2
                for lo, hi in ((0, e), (e, 0)):
                    cb = ropeB[:, t, :, lo:lo + e].unsqueeze(2).to_broadcast([P, 2, NH, e])
                    g.tensor_tensor(out=dst_b[:, :, :, lo:lo + e], in0=src[:, :, :, hi:hi + e], in1=cb,
                                    op=ALU.mult).then_inc(rope_done, 1)
                pool.wait_ge(rope_done, 4 * i + 3)
                g.tensor_tensor(out=ra[:, z, :], in0=ra[:, z, :], in1=rb, op=ALU.add).then_inc(rope_done, 1)

            def stage_v(b, n):
                pool.wait_ge(v_copied, NT * (b + 1) + 1)
                pool.wait_ge(pv_step, NT * (4 * b + n) + 1)
                g.tensor_copy(v_quad[:, :, :, 0:DH],
                              v_tok[:, :, bass.ds(QD * DH * n, QD * DH)].rearrange("p t (h d) -> p t h d", h=QD))\
                 .then_inc(vq_ready, 1)

            pool.wait_ge(s5_w, 1)
            pool.wait_ge(out_used, 1 + 2 * B * HC)
            one_pair = float(np.array([0x3F803F80], np.uint32).view(np.float32)[0])
            g.memset(k_st[SP_ROWS:P, :, :].bitcast(F32), one_pair).then_inc(ones_set, 1)
            with pool.Fori(0, B) as b:
                for t in range(NT):
                    rotate(b, t)
                with pool.Fori(0, NQ) as n:
                    stage_v(b, n)

        @block.vector
        def _(dve):
            v = nc.vector
            pre = Steps(dve, dve_pre)

            def ts(out, in0, s1, s2, op0, op1=None):
                if op1 is None:
                    pre(v.tensor_scalar(out, in0, s1, None, op0))
                else:
                    pre(v.tensor_scalar(out, in0, s1, s2, op0, op1))
                pre.wait()

            def tt(out, a, b, op):
                pre(v.tensor_tensor(out=out, in0=a, in1=b, op=op))
                pre.wait()

            def stt(out, a, s, b, op0, op1):
                pre(v.scalar_tensor_tensor(out=out, in0=a, scalar=s, in1=b, op0=op0, op1=op1))
                pre.wait()

            def cp(out, a):
                pre(v.tensor_copy(out, a))
                pre.wait()

            M, AD, SU = ALU.mult, ALU.add, ALU.subtract

            dve.wait_ge(ld_cond, 32)
            dve.wait_ge(act_silu, 1)
            cp(cond_b, condT.unsqueeze(3).to_broadcast([P, KD, B, P]))
            v.tensor_copy(silu_b, csilu.unsqueeze(3).to_broadcast([P, KD, B, P])).then_inc(cond_ready, 1)

            dve.wait_ge(ld_s5, 16 * 18)
            col = lambda i: prm[:, i:i + 1]
            (LRE, LIM, LS, DT, TH, N_, R_, PO, E_, MAG, PHI, PHH, PHL, LR, LI, DEN, CR, CI, SGN,
             X1, X2, S1, S2, S3, S4, TC, TS_, RD, AR) = range(29)
            pre(v.memset(prm[0:S, SGN:SGN + 1], 1.0))
            pre(v.memset(prm[S:P, SGN:SGN + 1], -1.0))
            v.tensor_scalar(b_nat[S:P, 1, :], b_nat[S:P, 1, :], -1.0, None, M).then_inc(bneg, 1)

            def exp_of(out, x):
                ts(col(X1), col(x), 88.0, -87.0, ALU.min, ALU.max)
                ts(col(N_), col(X1), 1.4426950408889634, MAGIC, M, AD)
                ts(col(N_), col(N_), MAGIC, None, SU)
                stt(col(R_), col(N_), -LN2_HI, col(X1), M, AD)
                stt(col(R_), col(N_), -LN2_LO, col(R_), M, AD)
                pre(v.memset(col(PO), 1.0 / 5040))
                pre.wait()
                for cf in (1.0 / 720, 1.0 / 120, 1.0 / 24, 1.0 / 6, 0.5, 1.0, 1.0):
                    ts(col(PO), col(PO), col(R_), cf, M, AD)
                ts(col(X2), col(N_), 127.0, None, AD)
                cp(col(E_).bitcast(I32), col(X2))
                pre(v.tensor_scalar(col(E_).bitcast(I32), col(E_).bitcast(I32), 23, None, ALU.logical_shift_left))
                pre.wait()
                tt(col(out), col(PO), col(E_), M)

            exp_of(DT, LS)
            tt(col(AR), col(LRE), col(DT), M)
            tt(col(TH), col(LIM), col(DT), M)
            exp_of(MAG, AR)
            ts(col(N_), col(TH), INV2PI, MAGIC, M, AD)
            ts(col(N_), col(N_), MAGIC, None, SU)
            stt(col(R_), col(N_), -TWO_PI_HI, col(TH), M, AD)
            stt(col(R_), col(N_), -TWO_PI_LO, col(R_), M, AD)
            ts(col(PHI), col(R_), INV2PI, None, M)
            ts(col(X1), col(PHI), 4096.0, MAGIC, M, AD)
            ts(col(PHH), col(X1), MAGIC, 1.0 / 4096, SU, M)
            tt(col(PHL), col(PHI), col(PHH), SU)

            dve.wait_ge(consts, 8)
            ts(scr0, iota, col(PHH), None, M)
            ts(scr1, scr0, MAGIC, MAGIC, AD, SU)
            tt(scr0, scr0, scr1, SU)
            stt(scr0, iota, col(PHL), scr0, M, AD)
            ts(scr1, scr0, MAGIC, MAGIC, AD, SU)
            tt(sinT, scr0, scr1, SU)
            ts(scr0, scr0, 0.25, None, AD)
            ts(scr1, scr0, MAGIC, MAGIC, AD, SU)
            tt(cosT, scr0, scr1, SU)
            cp(col(TS_), col(PHI))
            ts(col(X1), col(PHI), 0.25, None, AD)
            ts(col(X2), col(X1), MAGIC, MAGIC, AD, SU)
            tt(col(TC), col(X1), col(X2), SU)
            for i in range(8):
                f = float(np.float32(1.0) / np.float32(10000.0 ** (i / 8)))
                pre(v.memset(freq[:, i:i + 1], f))
            cp(ang[:, 5, 0:NT], pos_i.bitcast(I32))
            a3 = lambda r: ang[:, r, :].rearrange("p (t f) -> p t f", f=8)
            tt(a3(0), ang[:, 5, 0:NT].unsqueeze(2).to_broadcast([P, NT, 8]),
               freq.unsqueeze(1).to_broadcast([P, NT, 8]), M)

            def reduce_angle(out, a, s):
                ts(s, a, INV2PI, MAGIC, M, AD)
                ts(s, s, MAGIC, None, SU)
                stt(out, s, -TWO_PI_HI, a, M, AD)
                stt(out, s, -TWO_PI_LO, out, M, AD)

            reduce_angle(ang[:, 1, :], ang[:, 0, :], ang[:, 3, :])
            ts(ang[:, 2, :], ang[:, 1, :], float(np.pi / 2), None, AD)
            reduce_angle(ang[:, 2, :], ang[:, 2, :], ang[:, 3, :])
            for r in (1, 2):
                v.tensor_scalar(ang[:, r, :], ang[:, r, :], 3.1415925, -3.1415925, ALU.min, ALU.max).then_inc(trig_ready, 1)

            dve.wait_ge(mods_mm, 1)
            dve.wait_ge(ld_adaln, 16 * 10)
            tt(mods, P01[:, 0:56].rearrange("p (m b) -> p m b", b=B), bias28.unsqueeze(2).to_broadcast([P, 28, B]), AD)
            m2 = lambda i: mods[:, i:i + 2, :]
            pre(v.tensor_copy(scal[:, SH_A], m2(0)))
            pre(v.tensor_scalar(scal[:, SC_A], m2(2), 1.0, None, AD))
            pre(v.tensor_copy(scal[:, SH_MSA], m2(16)))
            pre(v.tensor_scalar(scal[:, SC_MSA], m2(18), 1.0, None, AD))
            pre(v.tensor_copy(scal[:, SH_MLP], m2(22)))
            pre(v.tensor_scalar(scal[:, SC_MLP], m2(24), 1.0, None, AD))
            pre(v.tensor_scalar(m2(8), m2(8), 1.0, None, AD))
            pre.wait()
            stt(scal[:, SC_FF], m2(12), 1.0, m2(8), AD, M)
            tt(scal[:, SH_FF], m2(14), m2(8), M)
            tt(scal[:, SH_FF], scal[:, SH_FF], m2(6), AD)
            dve.wait_ge(gates_mm, 1)
            pre(v.tensor_copy(gate[:, 0:2], P45[:, :].rearrange("p (g b d) -> p g b d", g=2, b=B)))
            pre(v.tensor_copy(gate[:, 2:4], P67[:, :].rearrange("p (g b d) -> p g b d", g=2, b=B)))
            pre.wait()
            dve.wait_ge(bc_T, 1)
            pre(v.tensor_copy(b_T, P23[:, 0:CH].rearrange("p (z k m) -> p z k m", z=2, k=KD)))
            pre(v.tensor_copy(c_T, P23[:, CH:2 * CH].rearrange("p (z m) -> p z m", z=2)))
            dve.wait_ge(act_trig, 6)
            tt(col(LR), col(MAG), col(TC), M)
            ts(col(LR), col(LR), 1.0, None, SU)
            tt(col(LI), col(MAG), col(TS_), M)
            tt(col(DEN), col(LRE), col(LRE), M)
            tt(col(X1), col(LIM), col(LIM), M)
            tt(col(DEN), col(DEN), col(X1), AD)
            pre(v.reciprocal(col(RD), col(DEN)))
            pre.wait()
            tt(col(CR), col(LR), col(LRE), M)
            tt(col(X1), col(LI), col(LIM), M)
            tt(col(CR), col(CR), col(X1), AD)
            tt(col(CR), col(CR), col(RD), M)
            tt(col(CI), col(LI), col(LRE), M)
            tt(col(X1), col(LR), col(LIM), M)
            tt(col(CI), col(CI), col(X1), SU)
            tt(col(CI), col(CI), col(RD), M)
            ts(col(S1), col(CR), 2.0, None, M)
            tt(col(S1), col(S1), col(SGN), M)
            ts(col(S2), col(CI), -2.0, None, M)
            tt(col(S3), col(S2), col(SGN), M)
            ts(col(S4), col(CR), -2.0, None, M)
            ts(c_w[:, 0, :], c_T[:, 0, :], col(S1), None, M)
            stt(c_w[:, 0, :], c_T[:, 1, :], col(S2), c_w[:, 0, :], M, AD)
            ts(c_w[:, 1, :], c_T[:, 0, :], col(S3), None, M)
            stt(c_w[:, 1, :], c_T[:, 1, :], col(S4), c_w[:, 1, :], M, AD)
            for b in range(B):
                tt(c_gated[:, b], c_w, gate[:, 0, b, :].unsqueeze(1).to_broadcast([P, 2, D]), M)
            tt(d_gate, m2(4), d_vec.unsqueeze(2).to_broadcast([P, KD, B]), M)
            for b in range(B):
                for k in range(KD):
                    ts(d_diag[:, b, k, :], ident[:, :], d_gate[:, k, b:b + 1], None, M)
            cp(decay, col(MAG).to_broadcast([P, CH]))
            sn = a3(3)
            cs = a3(4)
            e = DH // 2
            ts(lnw[:, 0, :], lnw[:, 0, :], 1.0 / float(np.sqrt(DH)), None, M)
            for z in range(2):
                w = lambda lo: lnw[:, z, lo:lo + e].unsqueeze(1).to_broadcast([P, NT, e])
                pre(v.tensor_tensor(out=ropeA[:, :, z, 0:e], in0=cs, in1=w(0), op=M))
                pre(v.tensor_tensor(out=ropeA[:, :, z, e:DH], in0=cs, in1=w(e), op=M))
                pre(v.tensor_tensor(out=ropeB[:, :, z, e:DH], in0=sn, in1=w(0), op=M))
                pre(v.tensor_tensor(out=ropeB[:, :, z, 0:e], in0=sn, in1=w(e), op=M))
            pre.wait()
            v.tensor_scalar(ropeB[:, :, :, 0:e], ropeB[:, :, :, 0:e], -1.0, None, M).then_inc(s5_w, 1)

            def rsqrt(st, r, a, n):
                vv, y, hv, t0, t1 = (r[:, q, 0:n] for q in range(5))
                st(v.tensor_scalar(hv, vv, -0.5, None, M))
                st(v.tensor_scalar(t0.bitcast(I32), vv.bitcast(I32), 1, None, ALU.logical_shift_right))
                st.wait()
                st(v.tensor_scalar(y.bitcast(I32), t0.bitcast(I32), -1.0, 1597463007.0, M, AD))
                st.wait()
                for q in range(3):
                    st(v.tensor_tensor(out=t0, in0=y, in1=y, op=M))
                    st.wait()
                    st(v.tensor_tensor(out=t1, in0=t0, in1=hv, op=M))
                    st.wait()
                    st(v.scalar_tensor_tensor(out=y, in0=t1, scalar=1.5, in1=y, op0=AD, op1=M))
                    st.wait()

            def norm(c, g, gx, rms):
                st = Steps(dve, nstep, 8 * LN_STEPS + RMS_STEPS * (gx - 8) if rms else LN_STEPS * gx)
                for j in range(TT):
                    st(v.bn_stats(bn6[:, j, :], x_tok[:, bass.ds(TT * c + j, 1), :].rearrange("p a d -> p (a d)")))
                st.wait()
                settle(dve)
                for j in range(TT):
                    st(v.bn_aggr(mv[:, j, :], bn6[:, j, :]))
                st.wait()
                if rms:
                    st(v.tensor_tensor(out=nrm[:, 1, :], in0=mv[:, :, 0], in1=mv[:, :, 0], op=M))
                    st.wait()
                    st(v.scalar_tensor_tensor(out=nrm[:, 0, :], in0=nrm[:, 1, :], scalar=RMS_EPS, in1=mv[:, :, 1], op0=AD, op1=AD))
                else:
                    st(v.tensor_scalar(nrm[:, 0, :], mv[:, :, 1], LN_EPS, None, AD))
                st.wait()
                rsqrt(st, nrm, None, TT)
                dve.wait_ge(tr_ready, g)
                for j in range(TT):
                    src = x_tok[:, bass.ds(TT * c + j, 1), :].rearrange("p a d -> p (a d)")
                    if rms:
                        ins = v.tensor_scalar(xn[:, j, :], src, nrm[:, 1, j:j + 1], None, M)
                    else:
                        ins = v.tensor_scalar(xn[:, j, :], src, mv[:, j, 0:1], nrm[:, 1, j:j + 1], SU, M)
                    ins.then_inc(xn_ready, 1)
                assert st.n == (RMS_STEPS if rms else LN_STEPS), st.n

            def residual(c, b, o, gi, xo):
                for q in range(2):
                    dve.wait_ge(out_ready, 2 * o + q + 1)
                    dve.wait_ge(x_upd, 2 * xo + q)
                    po = P45[:, q * CH:(q + 1) * CH].rearrange("p (a d) -> p a d", a=2)
                    gt = gate[:, gi, bass.ds(b, 1), :].to_broadcast([P, 2, D])
                    xx = x_tok[:, bass.ds(TT * c + 2 * q, 2), :]
                    v.tensor_tensor(out=tmp[q][:, :, :], in0=po, in1=gt, op=M).then_inc(out_used, 1)
                    dve.wait_ge(out_used, 2 * o + q + 2)
                    v.tensor_tensor(out=xx, in0=xx, in1=tmp[q][:, :, :], op=AD).then_inc(x_upd, 1)

            def s5_scan(c, h):
                st = Steps(dve, sstep, SCAN_STEPS * c)
                tb = slice(h * CH, (h + 1) * CH)
                dve.wait_ge(bu_ready, c + 1)
                st(v.tensor_tensor(out=s_cos, in0=P23[:, 0:CH], in1=cosT[:, tb], op=M))
                st(v.tensor_tensor(out=s_sin, in0=P23[:, CH:2 * CH], in1=sinT[:, tb], op=M))
                st.wait()
                st(v.tensor_tensor(out=s_in, in0=s_cos, in1=s_sin, op=AD))
                st.wait()
                init = 0.0 if h == 0 else s_y[:, h - 1, CH - 1:CH]
                st(v.tensor_tensor_scan(s_y[:, h, :], decay, s_in, init, M, AD))
                st.wait()
                dve.wait_ge(out_ready, 2 * c)
                st(v.tensor_tensor(out=s_z[:, 0, :], in0=s_y[:, h, :], in1=cosT[:, tb], op=M))
                v.tensor_tensor(out=s_z[:, 1, :], in0=s_y[:, h, :], in1=sinT[:, tb], op=M).then_inc(z_ready, 1)
                assert st.n == SCAN_STEPS

            dve.sem_inc(out_used, 1)
            dve.wait_ge(ld_x, 16)
            with dve.Fori(0, B) as b:
                for h in range(HC):
                    c = HC * b + h
                    norm(c, c, c, False)
                    s5_scan(c, h)
                    for q in range(2):
                        dve.wait_ge(out_ready, 2 * c + q + 1)
                        xx = x_tok[:, bass.ds(TT * c + 2 * q, 2), :].rearrange("p a d -> p (a d)")
                        v.tensor_tensor(out=xx, in0=xx, in1=P45[:, q * CH:(q + 1) * CH], op=AD).then_inc(out_used, 1)

            with dve.Fori(0, B) as b:
                for h in range(HC):
                    c = HC * b + h
                    dve.wait_ge(out_used, 1 + 2 * B * HC)
                    norm(c, 4 + c, 4 + c, False)
                    residual(c, b, 4 + c, 1, c)

            def qk_norm(b, t):
                i = NT * b + t
                z = t % 2
                st = Steps(dve, qnstep, QN_STEPS * i)
                dve.wait_ge(sq_ready, i + 1)
                st(v.tensor_reduce(out=qnm[:, 3, :], in_=sq[:, z, :].rearrange("p (h d) -> p h d", d=DH), axis=AX.X, op=AD))
                st.wait()
                st(v.tensor_scalar(qnm[:, 0, :], qnm[:, 3, :], 1.0 / DH, RMS_EPS, M, AD))
                st.wait()
                rsqrt(st, qnm, None, 2 * NH)
                bank = P23[:, z * CH:(z + 1) * CH].rearrange("p (h d) -> p h d", d=DH)
                rr = qnm[:, 1, :].unsqueeze(2).to_broadcast([P, 2 * NH, DH])
                if t >= 2:
                    dve.wait_ge(rope_done, 4 * (i - 1))
                v.tensor_tensor(out=qn[:, z, :].rearrange("p (h d) -> p h d", d=DH), in0=bank, in1=rr, op=M).then_inc(qn_done, 1)
                assert st.n == QN_STEPS, st.n

            def qk_split(b, t):
                i = NT * b + t
                st = Steps(dve, qsstep, QS_STEPS * i)
                z = t % 2
                if t >= 2:
                    dve.wait_ge(split_act, 4 * (i - 1))
                dve.wait_ge(rope_done, 4 * i + 4)
                v.tensor_copy(hb[:, z, :], ra[:, z, :]).then_inc(part_ready, 1)
                dve.wait_ge(part_ready, 3 * i + 1)
                st(v.tensor_tensor(out=r1, in0=ra[:, z, :], in1=hb[:, z, :], op=SU))
                st.wait()
                v.tensor_copy(mb[:, z, :], r1).then_inc(part_ready, 1)
                dve.wait_ge(part_ready, 3 * i + 2)
                if t >= 2:
                    dve.wait_ge(stkT_dve, 2 * (i - 1))
                sp = split[:, z, :].rearrange("p (a h r) -> p a h r", a=2, h=NH)
                r4 = r1.rearrange("p (a h d) -> p a h d", a=2, h=NH)
                m4 = mb[:, z, :].rearrange("p (a h d) -> p a h d", a=2, h=NH)
                st(v.tensor_tensor(out=sp[:, 0, :, 5 * DH:6 * DH], in0=r4[:, 0], in1=m4[:, 0], op=SU))
                v.tensor_tensor(out=sp[:, 1, :, 2 * DH:3 * DH], in0=r4[:, 1], in1=m4[:, 1], op=SU).then_inc(part_ready, 1)

            def stack_in(b, t):
                i = NT * b + t
                for a in range(2):
                    dve.wait_ge(stkT_dve, 2 * i + a + 1)
                    dst = stacks[0:SP_ROWS, a, 8:16, t * P:(t + 1) * P]
                    src = P67[0:SP_ROWS, CH:2 * CH].bitcast(BF16).rearrange("p (h q) -> p h q", h=8)
                    v.tensor_copy(dst, src).then_inc(stk_dve, 1)

            def take_max(b, m, k):
                it = 64 * (4 * b + m) + k
                hd, t, half = k // 16, k // 2 % 8, k % 2
                dve.wait_ge(mx_ready, it + 1)
                v.tensor_reduce(out=pmax[:, hd, t, half:half + 1], in_=P67[:, (k % 2) * CH:(k % 2 + 1) * CH], axis=AX.X,
                                op=ALU.max).then_inc(mx_used, 1)

            def shift_split(b, m):
                st = Steps(dve, mstep, SHIFT_STEPS * (4 * b + m))
                dve.wait_ge(mx_used, 64 * (4 * b + m + 1) + 1)
                dve.wait_ge(shT_ready, 4 * b + m)
                w = QD * NT
                st(v.tensor_reduce(out=negm[:, 0, :], in_=pmax[:, :, :, :], axis=AX.X, op=ALU.max, negate=True))
                st.wait()
                st(v.tensor_copy(shift3[:, 0:w], negm[:, 0, :]))
                st.wait()
                st(v.tensor_tensor(out=negm[:, 1, :], in0=negm[:, 0, :], in1=shift3[:, 0:w], op=SU))
                st.wait()
                st(v.tensor_copy(shift3[:, w:2 * w], negm[:, 1, :]))
                st.wait()
                st(v.tensor_tensor(out=negm[:, 2, :], in0=negm[:, 1, :], in1=shift3[:, w:2 * w], op=SU))
                st.wait()
                st(v.tensor_copy(shift3[:, 2 * w:3 * w], negm[:, 2, :]))
                assert st.n == SHIFT_STEPS

            def shift_copy(b, m):
                dve.wait_ge(shT_ready, 4 * b + m + 1)
                dve.wait_ge(shift_dma, 48 * (4 * b + m))
                v.tensor_copy(shiftT[:, :], P67[0:3 * QD * NT, 0:P // 2].bitcast(BF16)).then_inc(shT_copied, 1)

            def pv_copy(b, n):
                dve.wait_ge(pvT_ready, 2 * (4 * b + n))
                dve.wait_ge(pv_step, NT * (4 * b + n + 1) + 1)
                for q in range(2):
                    v.tensor_copy(pv_sb[:, q * CH:(q + 1) * CH], P45[:, q * CH:(q + 1) * CH]).then_inc(pv_copied, 1)

            def attn_out(b, n):
                dve.wait_ge(pvT_ready, 2 * (4 * b + n + 1))
                pt = P67[:, :].rearrange("p (t h d) -> p t h d", t=NT, h=QD)
                v.reciprocal(rden[:, :, :].unsqueeze(3), pt[:, :, :, DH:DH + 1]).then_inc(astep, 1)
                dve.wait_ge(astep, 4 * b + n + 1)
                dst = attn[:, :, bass.ds(QD * DH * n, QD * DH)].rearrange("p t (h d) -> p t h d", h=QD)
                v.tensor_tensor(out=dst, in0=pt[:, :, :, 0:DH], in1=rden[:, :, :].unsqueeze(3).to_broadcast([P, NT, QD, DH]),
                                op=M).then_inc(attn_done, 1)

            dve.sem_inc(qn_done, 1)
            dve.sem_inc(mx_used, 1)
            with dve.Fori(0, B) as b:
                for h in range(HC):
                    dve.wait_ge(x_upd, 2 * (4 + 4 * b))
                    settle(dve)
                    norm(HC * b + h, 8 + 6 * b + h, 8 + 4 * b + h, True)
                    for t in range(TT * h, TT * (h + 1)):
                        qk_norm(b, t)
                        if t >= 1:
                            qk_split(b, t - 1)
                        if t >= 2:
                            stack_in(b, t - 2)
                qk_split(b, NT - 1)
                stack_in(b, NT - 2)
                stack_in(b, NT - 1)
                for k in range(64):
                    take_max(b, 0, k)
                shift_split(b, 0)
                shift_copy(b, 0)
                with dve.Fori(0, NQ - 1) as n:
                    for k in range(64):
                        take_max(b, n + 1, k)
                    shift_split(b, n + 1)
                    shift_copy(b, n + 1)
                    pv_copy(b, n)
                    attn_out(b, n)
                pv_copy(b, NQ - 1)
                attn_out(b, NQ - 1)
                for h in range(HC):
                    c = HC * b + h
                    o = 8 + 4 * b + 2 * h
                    residual(c, b, o, 2, o - 4)
                    dve.wait_ge(x_upd, 2 * (o - 4) + 2)
                    settle(dve)
                    norm(c, 8 + 6 * b + 3 + 2 * h, 8 + 4 * b + 2 + h, True)
                    for m in range(MC):
                        w = min(P, HM - m * P)
                        dve.wait_ge(sil_ready, MC * c + m + 1)
                        v.tensor_tensor(out=gT[0:w, m, :], in0=P67[0:w, (m % 2) * CH:(m % 2 + 1) * CH], in1=sil[0:w, m % 2, :],
                                        op=M).then_inc(gm_done, 1)
                    residual(c, b, o + 1, 3, o + 1 - 4)

        @block.scalar
        def _(act):
            a = nc.scalar
            act.wait_ge(ld_cond, 32)
            a.activation(csilu, condT, ACT.Silu).then_inc(act_silu, 1)
            act.wait_ge(trig_ready, 2)
            two_pi = float(np.float32(2 * np.pi) * np.float32(1 - 2.0 ** -23))
            a.activation(sinT, sinT, ACT.Sin, scale=two_pi).then_inc(act_trig, 1)
            a.activation(cosT, cosT, ACT.Sin, scale=two_pi).then_inc(act_trig, 1)
            for q in (25, 26):
                a.activation(prm[:, q:q + 1], prm[:, q:q + 1], ACT.Sin, scale=two_pi).then_inc(act_trig, 1)
            a.activation(ang[:, 3, :], ang[:, 1, :], ACT.Sin).then_inc(act_trig, 1)
            a.activation(ang[:, 4, :], ang[:, 2, :], ACT.Sin).then_inc(act_trig, 1)

            def evacuate(g, par, b, sc, sh):
                act.wait_ge(tr_ready, g + 1)
                act.wait_ge(u_used, g)
                settle(act)
                for k in range(KD):
                    src = P01[:, k * CH:(k + 1) * CH]
                    if sc is None:
                        ins = a.activation(uT[par][:, k, :], src, ACT.Copy)
                    else:
                        ins = a.activation(uT[par][:, k, :], src, ACT.Identity,
                                           scale=scal[:, sc, k, bass.ds(b, 1)], bias=scal[:, sh, k, bass.ds(b, 1)])
                    ins.then_inc(u_ready, 1)

            act.wait_ge(s5_w, 1)
            with act.Fori(0, B) as b:
                for h in range(HC):
                    evacuate(HC * b + h, h, b, SC_A, SH_A)
            act.wait_ge(ld_ffn, 64)
            with act.Fori(0, B) as b:
                for h in range(HC):
                    c = HC * b + h
                    evacuate(4 + c, h, b, SC_FF, SH_FF)
                    for m in range(FC):
                        act.wait_ge(h_ready, FC * c + m + 1)
                        bank = (P23, P67)[m // 2 % 2][:, (m % 2) * CH:(m % 2 + 1) * CH]
                        a.activation(hT[:, m, :], bank, ACT.Gelu_apprx_tanh, bias=b_ff1[:, m:m + 1]).then_inc(gelu_done, 1)

            act.sem_inc(v_copied, 1)
            act.sem_inc(p_ready, 1)

            def tile_in(b, t):
                i = NT * b + t
                z = t % 2
                act.wait_ge(qk_ready, i + 1)
                a.activation(sq[:, z, :], P23[:, z * CH:(z + 1) * CH], ACT.Square).then_inc(sq_ready, 1)
                act.wait_ge(v_ready, i + 1)
                a.activation(v_tok[:, t, :], P45[:, z * CH:z * CH + D], ACT.Copy).then_inc(v_copied, 1)

            def slots(b, t):
                i = NT * b + t
                z = t % 2
                sp = split[:, z, :].rearrange("p (a h s d) -> p a h s d", a=2, h=NH, s=6)
                if t >= 2:
                    act.wait_ge(stkT_dve, 2 * (i - 1))
                for part, (src, qs, ks) in enumerate(((hb, slice(0, 3), slice(1, 6, 2)), (mb, slice(3, 5), slice(0, 5, 4)))):
                    act.wait_ge(part_ready, 3 * i + part + 1)
                    s4 = src[:, z, :].rearrange("p (a h d) -> p a h d", a=2, h=NH)
                    n = 3 - part
                    for w, sl in ((0, qs), (1, ks)):
                        a.activation(sp[:, w, :, sl, :], s4[:, w].unsqueeze(2).to_broadcast([P, NH, n, DH]), ACT.Copy)\
                         .then_inc(split_act, 1)

            def stack_in(b, t):
                i = NT * b + t
                for w in range(2):
                    act.wait_ge(stkT_act, 2 * i + w + 1)
                    dst = stacks[0:SP_ROWS, w, 0:8, t * P:(t + 1) * P]
                    src = P67[0:SP_ROWS, 0:CH].bitcast(BF16).rearrange("p (h q) -> p h q", h=8)
                    a.activation(dst, src, ACT.Copy).then_inc(stk_act, 1)

            def exps(b, n):
                for u in range(QD * NT):
                    t, hd = u // QD, u % QD
                    act.wait_ge(st_ready, QD * NT * (4 * b + n) + u + 1)
                    if hd == 0:
                        act.wait_ge(pv_step, NT * (4 * b + n) + t)
                    a.activation(probs[:, t % 2, hd, :], (P01, P23)[u % 2][:, :], ACT.Exp).then_inc(p_ready, 1)

            act.wait_ge(ld_blk, 16 * 7)
            with act.Fori(0, B) as b:
                for h in range(HC):
                    evacuate(8 + 6 * b + h, h, b, SC_MSA, SH_MSA)
                    for t in range(TT * h, TT * (h + 1)):
                        tile_in(b, t)
                        if t >= 1:
                            slots(b, t - 1)
                        if t >= 2:
                            stack_in(b, t - 2)
                slots(b, NT - 1)
                stack_in(b, NT - 2)
                stack_in(b, NT - 1)
                with act.Fori(0, NQ) as n:
                    exps(b, n)
                for h in range(HC):
                    c = HC * b + h
                    evacuate(8 + 6 * b + 2 + 2 * h, 0, b, None, None)
                    evacuate(8 + 6 * b + 3 + 2 * h, 1, b, SC_MLP, SH_MLP)
                    for m in range(MC):
                        w = min(P, HM - m * P)
                        act.wait_ge(g_ready, MC * c + m + 1)
                        a.activation(sil[0:w, m % 2, :], P23[0:w, (m % 2) * CH:(m % 2 + 1) * CH], ACT.Silu).then_inc(sil_ready, 1)

        @block.tensor
        def _(pe):
            mm = nc.tensor.matmul

            def transposes(g, gx, src):
                pe.wait_ge(u_ready, 2 * g)
                for j in range(TT):
                    if gx is not None:
                        pe.wait_ge(xn_ready, TT * gx + j + 1)
                    for k in range(KD):
                        ins = nc.tensor.transpose(P01[:, k * CH + j * P:k * CH + (j + 1) * P], src(j)[:, k * P:(k + 1) * P], ident[:, :])
                ins.then_inc(tr_ready, 1)

            norm_src = lambda j: xn[:, j, :]

            pe.wait_ge(ld_adaln, 16 * 10)
            pe.wait_ge(cond_ready, 1)
            chunks = [(w_mod, condT, m) for m in range(12)] + [(w_cond, condT, m) for m in range(4)] + [(w_ada, csilu, m) for m in range(12)]
            for i, (w, r, m) in enumerate(chunks):
                for k in range(KD):
                    ins = mm(P01[:, B * i:B * (i + 1)], w[:, k, m * P:(m + 1) * P], r[:, k, :], start=(k == 0), stop=(k == KD - 1))
            ins.then_inc(mods_mm, 1)
            pe.wait_ge(consts, 8)
            for i, (w, r, lo) in enumerate(((w_mod, cond_b, 2), (w_mod, cond_b, 5), (w_ada, silu_b, 2), (w_ada, silu_b, 5))):
                for b in range(B):
                    dst = (P45, P67)[i // 2][:, ((i % 2) * B + b) * D:((i % 2) * B + b + 1) * D]
                    for k in range(KD):
                        mm(dst, r[:, k, b, :], w[:, k, lo * D:(lo + 1) * D], start=(k == 0), stop=False)
                    ins = mm(dst, ones_row[:, :], row_gate[:, i, :], start=False, stop=True)
            ins.then_inc(gates_mm, 1)
            pe.wait_ge(bneg, 1)
            pe.wait_ge(ld_s5, 16 * 18)
            for z in range(2):
                for k in range(KD):
                    nc.tensor.transpose(P23[:, (z * KD + k) * P:(z * KD + k + 1) * P], b_nat[:, z, k * P:(k + 1) * P], ident[:, :])
            for z in range(2):
                for k in range(KD):
                    ins = nc.tensor.transpose(P23[:, CH + (z * KD + k) * P:CH + (z * KD + k + 1) * P], c_nat[:, z, k, :], ident[:, :])
            ins.then_inc(bc_T, 1)
            pe.sem_inc(u_used, 1)
            pe.sem_inc(pv_step, 1)
            pe.wait_ge(s5_w, 1)

            with pe.Fori(0, B) as b:
                for h in range(HC):
                    c = HC * b + h
                    transposes(c, c, norm_src)
                    pe.wait_ge(u_ready, 2 * c + 2)
                    pe.wait_ge(sstep, SCAN_STEPS * c)
                    for z in range(2):
                        for k in range(KD):
                            ins = mm(P23[:, z * CH:(z + 1) * CH], b_T[:, z, k, :], uT[h][:, k, :], start=(k == 0), stop=(k == KD - 1))
                    ins.then_inc(bu_ready, 1)
                    pe.wait_ge(z_ready, c + 1)
                    for j in range(TT):
                        q = j // 2
                        if j % 2 == 0:
                            pe.wait_ge(out_used, 2 * c + q)
                        dst = P45[:, j * D:(j + 1) * D]
                        tk = slice(j * P, (j + 1) * P)
                        for k in range(KD):
                            ins = mm(dst[:, k * P:(k + 1) * P], uT[h][:, k, tk], d_diag[:, bass.ds(b, 1), k, :].rearrange("p a m -> p (a m)"),
                                     start=(k == 0), stop=False, skip_group_check=True)
                        if j == TT - 1:
                            ins.then_inc(u_used, 1)
                        for z in range(2):
                            ins = mm(dst, s_z[:, z, tk], c_gated[:, bass.ds(b, 1), z, :].rearrange("p a m -> p (a m)"),
                                     start=False, stop=(z == 1), skip_group_check=True)
                        if j % 2 == 1:
                            ins.then_inc(out_ready, 1)

            def to_tokens(o, j, lhs, rhs, nk, bias, used):
                q = j // 2
                if j % 2 == 0:
                    pe.wait_ge(out_used, 2 * o + q)
                dst = P45[:, j * D:(j + 1) * D]
                for k in range(nk):
                    ins = mm(dst, lhs(k, slice(j * P, (j + 1) * P)), rhs(k), start=(k == 0), stop=(bias is None and k == nk - 1))
                    if used == (j, k):
                        ins.then_inc(u_used, 1)
                if bias is not None:
                    ins = mm(dst, ones_row[:, :], bias[:, :], start=False, stop=True)
                if j % 2 == 1:
                    ins.then_inc(out_ready, 1)

            pe.wait_ge(ld_ffn, 64)
            with pe.Fori(0, B) as b:
                for h in range(HC):
                    c = HC * b + h
                    transposes(4 + c, 4 + c, norm_src)
                    pe.wait_ge(u_ready, 2 * (4 + c) + 2)
                    for m in range(FC):
                        if m >= 4:
                            pe.wait_ge(gelu_done, FC * c + m - 3)
                        bank = (P23, P67)[m // 2 % 2][:, (m % 2) * CH:(m % 2 + 1) * CH]
                        for k in range(KD):
                            ins = mm(bank, w_ff1[:, k, m * P:(m + 1) * P], uT[h][:, k, :], start=(k == 0), stop=(k == KD - 1))
                        ins.then_inc(h_ready, 1)
                    pe.wait_ge(gelu_done, FC * c + FC)
                    for j in range(TT):
                        to_tokens(4 + c, j, lambda k, tk: hT[:, k, tk], lambda k: w_ff2[:, k, :], FC, row_b2, (0, 0))

            def qkv(b, t):
                i = NT * b + t
                h, j, z = t // TT, t % TT, t % 2
                tk = slice(j * P, (j + 1) * P)
                if j == 0:
                    pe.wait_ge(u_ready, 2 * (8 + 6 * b + h) + 2)
                pe.wait_ge(qn_done, i)
                for k in range(KD):
                    ins = mm(P23[:, z * CH:(z + 1) * CH], uT[h][:, k, tk], w_qkv[:, k, 0:2 * D], start=(k == 0), stop=(k == KD - 1))
                ins.then_inc(qk_ready, 1)
                pe.wait_ge(v_copied, i)
                for k in range(KD):
                    ins = mm(P45[:, z * CH:z * CH + D], uT[h][:, k, tk], w_qkv[:, k, 2 * D:3 * D], start=(k == 0), stop=(k == KD - 1))
                ins.then_inc(v_ready, 1)

            def stack_T(b, t, tells):
                i = NT * b + t
                pe.wait_ge(split_act, 4 * (i + 1))
                pe.wait_ge(part_ready, 3 * (i + 1))
                sp = split[:, t % 2, :].rearrange("p (a h r) -> p a h r", a=2, h=NH)
                for w in range(2):
                    for e, (freed, ready) in enumerate(((stk_act, stkT_act), (stk_dve, stkT_dve))):
                        pe.wait_ge(freed, 2 * i + w)
                        bank = P67[0:SP_ROWS, e * CH:(e + 1) * CH].bitcast(BF16)
                        for hd in range(8):
                            ins = nc.tensor.transpose(bank[:, hd * P:(hd + 1) * P], sp[:, w, 8 * e + hd, :], ident_bf[:, :])
                            if tells and w == 0 and e == 0 and hd == 0:
                                ins.then_inc(u_used, 1)
                        ins.then_inc(ready, 1)

            def max_item(b, m, k):
                it = 64 * (4 * b + m) + k
                hd, t, half = k // 16, k // 2 % 8, k % 2
                pe.wait_ge(mx_used, it)
                head = bass.ds(QD * m + hd, 1)
                mm(P67[:, (k % 2) * CH:(k % 2 + 1) * CH],
                   q_st[0:SP_ROWS, head, t * P:(t + 1) * P].rearrange("p a q -> p (a q)"),
                   k_st[0:SP_ROWS, head, half * CH:(half + 1) * CH].rearrange("p a q -> p (a q)"),
                   start=True, stop=True).then_inc(mx_ready, 1)

            def shift_T(b, m):
                pe.wait_ge(mstep, SHIFT_STEPS * (4 * b + m + 1))
                nc.tensor.transpose(P67[0:3 * QD * NT, 0:P // 2].bitcast(BF16), shift3[:, :], ident_bf[:, :]).then_inc(shT_ready, 1)

            def p_v(b, n, t):
                pe.wait_ge(p_ready, QD * NT * (4 * b + n) + QD * (t + 1) + 1)
                if t == 0:
                    pe.wait_ge(vq_ready, 4 * b + n + 1)
                    pe.wait_ge(pv_copied, 2 * (4 * b + n))
                for half in range(2):
                    for hd in range(QD):
                        ins = mm(P45[32 * hd:32 * (hd + 1), half * CH:(half + 1) * CH], v_quad[:, t, hd, :],
                                 probs[:, t % 2, hd, half * CH:(half + 1) * CH], start=(t == 0), stop=(t == NT - 1))
                ins.then_inc(pv_step, 1)

            def quad(b, n, with_max):
                pe.wait_ge(shift_dma, 48 * (4 * b + n + 1))
                for u in range(QD * NT):
                    t, hd = u // QD, u % QD
                    ui = QD * NT * (4 * b + n) + u
                    pe.wait_ge(p_ready, ui)
                    head = bass.ds(QD * n + hd, 1)
                    for half in range(2):
                        ins = mm((P01, P23)[u % 2][:, half * CH:(half + 1) * CH],
                                 k_st[0:ST_ROWS, head, t * P:(t + 1) * P].rearrange("p a q -> p (a q)"),
                                 q_st[0:ST_ROWS, head, half * CH:(half + 1) * CH].rearrange("p a q -> p (a q)"),
                                 start=True, stop=True)
                    ins.then_inc(st_ready, 1)
                    if with_max:
                        max_item(b, n + 1, 2 * u)
                        max_item(b, n + 1, 2 * u + 1)
                    if hd == 1 and t >= 1:
                        p_v(b, n, t - 1)
                p_v(b, n, NT - 1)
                if with_max:
                    shift_T(b, n + 1)
                    pe.wait_ge(shT_copied, 4 * b + n + 2)
                pe.wait_ge(pv_copied, 2 * (4 * b + n) + 2)
                for q in range(2):
                    for t in range(4 * q, 4 * q + 4):
                        ins = nc.tensor.transpose(P67[:, t * P:(t + 1) * P], pv_sb[:, t * P:(t + 1) * P], ident[:, :])
                    ins.then_inc(pvT_ready, 1)
                pe.wait_ge(attn_done, 4 * b + n + 1)

            pe.wait_ge(ld_blk, 16 * 7)
            pe.wait_ge(ones_set, 1)
            with pe.Fori(0, B) as b:
                for h in range(HC):
                    transposes(8 + 6 * b + h, 8 + 4 * b + h, norm_src)
                    if h == 0:
                        pe.wait_ge(out_used, 2 * (8 + 4 * b) + 1)
                    for t in range(TT * h, TT * (h + 1)):
                        qkv(b, t)
                        if t >= 2:
                            stack_T(b, t - 2, t % TT == TT - 1)
                stack_T(b, NT - 2, False)
                stack_T(b, NT - 1, False)
                pe.wait_ge(stk_act, 2 * NT * (b + 1))
                pe.wait_ge(stk_dve, 2 * NT * (b + 1))
                for k in range(64):
                    max_item(b, 0, k)
                shift_T(b, 0)
                with pe.Fori(0, NQ - 1) as n:
                    quad(b, n, True)
                quad(b, NQ - 1, False)
                for h in range(HC):
                    c = HC * b + h
                    g, o = 8 + 6 * b + 2 + 2 * h, 8 + 4 * b + 2 * h
                    transposes(g, None, lambda j: attn[:, TT * h + j, :])
                    pe.wait_ge(u_ready, 2 * g + 2)
                    for j in range(TT):
                        to_tokens(o, j, lambda k, tk: uT[0][:, k, tk], lambda k: w_proj[:, k, :], KD, row_pb, (TT - 1, KD - 1))
                    transposes(g + 1, 8 + 4 * b + 2 + h, norm_src)
                    pe.wait_ge(u_ready, 2 * g + 4)
                    for m in range(MC):
                        w = min(P, HM - m * P)
                        if m >= 2:
                            pe.wait_ge(gm_done, MC * c + m - 1)
                        for bank, wt in ((P23, w_g1), (P67, w_g3)):
                            for k in range(KD):
                                ins = mm(bank[0:w, (m % 2) * CH:(m % 2 + 1) * CH], wt[:, k, m * P:m * P + w], uT[1][:, k, :],
                                         start=(k == 0), stop=(k == KD - 1))
                        ins.then_inc(g_ready, 1)
                    pe.wait_ge(gm_done, MC * c + MC)
                    rows = lambda m: min(P, HM - m * P)
                    for j in range(TT):
                        to_tokens(o + 1, j, lambda m, tk: gT[0:rows(m), m, tk], lambda m: w_g2[0:rows(m), m, :], MC, None, (0, 0))


INS = ("x", "cond_1024", "pos_S", "L0_cond_Wm", "L0_cond_bm", "L0_cond_Lam_re", "L0_cond_Lam_im", "L0_cond_B_re",
       "L0_cond_B_im", "L0_cond_C_re", "L0_cond_C_im", "L0_cond_D_diag", "L0_cond_log_step", "L0_cond_Wc", "L0_cond_bc",
       "L0_cond_W1", "L0_cond_b1", "L0_cond_W2", "L0_cond_b2", "L1_cond_adaln_w", "L1_cond_adaln_b", "L1_cond_qkv_w",
       "L1_cond_lnq_w", "L1_cond_lnk_w", "L1_cond_proj_w", "L1_cond_proj_b", "L1_cond_w1_w", "L1_cond_w3_w", "L1_cond_w2_w")


def kernel(**inputs):
    import concourse.bacc as bacc
    from concourse.bass_utils import run_bass_kernel_spmd

    nc = bacc.Bacc("TRN2", target_bir_lowering=False, num_devices=1)
    arrays, aps = {}, {}
    for name in INS:
        a = np.ascontiguousarray(inputs[name])
        if name == "x":
            a = a.reshape(B * T, D)
        arrays[f"in_{name}"] = a
        aps[name] = nc.dram_tensor(f"in_{name}", a.shape, mybir.dt.from_np(a.dtype), kind="ExternalInput").ap()
    aps["out"] = nc.dram_tensor("out", (B * T, D), F32, kind="ExternalOutput").ap()
    build(nc, aps)
    r = run_bass_kernel_spmd(nc, [arrays], core_ids=[0])
    return r.results[0]["out"].reshape(B, T, D)
```

```python
from contextlib import ExitStack

import numpy as np
import concourse.bass as bass
from concourse import mybir

F32 = mybir.dt.float32
BF16 = mybir.dt.bfloat16
I32 = mybir.dt.int32
ACT = mybir.ActivationFunctionType
ALU = mybir.AluOpType
AX = mybir.AxisListType

B, T, D = 2, 1024, 256
P = 128
CH = 512
HC = T // CH
NCH = B * HC
TT = CH // P
NT = T // P
KD = D // P
S = 64
F = 4 * D
FC = F // P
NH, DH = 16, 16
HM = 704
MC = (HM + P - 1) // P
HMP = MC * P
QP = 4
QD = 4
NQ = NH // QD
SP_ROWS = 6 * DH
ST_ROWS = SP_ROWS + 3
LN_EPS, RMS_EPS = 1e-5, 1e-6
MAGIC = 12582912.0
INV2PI = float(np.float32(1.0 / (2 * np.pi)))
TWO_PI_HI = 6.28125
TWO_PI_LO = float(np.float32(2 * np.pi - 6.28125))
LN2_HI = 0.693359375
LN2_LO = float(np.float32(np.log(2.0) - 0.693359375))


def build(nc, A):
    es = ExitStack()
    with es:
        def sb(name, shape, dt=F32):
            return es.enter_context(nc.sbuf_tensor(name, shape, dt))

        def sem(name):
            return es.enter_context(nc.semaphore(name))

        P01, P23, P45, P67 = [es.enter_context(nc.psum_tensor(n, [P, 2 * CH], F32)) for n in ("P01", "P23", "P45", "P67")]

        x_tok = sb("x_tok", [P, B * NT, D])
        xn = sb("xn", [P, TT, D])
        uT = [sb(f"uT{h}", [P, KD, CH]) for h in range(2)]
        w_ff1 = sb("w_ff1", [P, KD, F])
        w_ff2 = sb("w_ff2", [P, FC, D])
        w_qkv = sb("w_qkv", [P, KD, 3 * D])
        w_proj = sb("w_proj", [P, KD, D])
        w_g1 = sb("w_g1", [P, KD, HMP])
        w_g3 = sb("w_g3", [P, KD, HMP])
        w_g2 = sb("w_g2", [P, MC, D])
        b_ff1 = sb("b_ff1", [P, FC])
        bias_rows = sb("bias_rows", [P, 2, D], BF16)
        ones_bf = sb("ones_bf", [P, P], BF16)
        ones_row = sb("ones_row", [1, P])
        ident = sb("ident", [P, P])
        ident_bf = sb("ident_bf", [P, P], BF16)
        gate = sb("gate", [P, 4, B, D])
        scal = sb("scal", [P, 8, KD, B])
        SH_A, SC_A, SC_FF, SH_FF, SH_MSA, SC_MSA, SH_MLP, SC_MLP = range(8)
        tmp = [sb(f"tmp{q}", [P, 2, D]) for q in range(2)]
        qnm = sb("qnm", [P, 5, 2 * NH])
        bn6 = sb("bn6", [P, TT, 6])
        mv = sb("mv", [P, TT, 2])
        nrm = sb("nrm", [P, 5, TT])
        ropeA = sb("ropeA", [P, NT, 2, DH])
        ropeB = sb("ropeB", [P, NT, 2, DH])
        v_tok = sb("v_tok", [P, NT, D])
        v_quad = sb("v_quad", [P, NT, QD, 32])
        attn = sb("attn", [P, NT, D])
        work = sb("work", [P, 8192])
        stacks = sb("stacks", [P, 2, NH, T], BF16)
        q_st = stacks[:, 0]
        k_st = stacks[:, 1]

        def carve(base, at, shape, dt=F32):
            n = int(np.prod(shape[1:])) * (2 if dt == BF16 else 4) // 4
            ap = base[0:shape[0], at:at + n]
            if dt != F32:
                ap = ap.bitcast(dt)
            if len(shape) == 3:
                ap = ap.rearrange("p (a b) -> p a b", a=shape[1])
            if len(shape) == 4:
                ap = ap.rearrange("p (a b c) -> p a b c", a=shape[1], b=shape[2])
            return ap, at + n

        at = 0
        w_mod, at = carve(work, at, [P, KD, 6 * D])
        w_cond, at = carve(work, at, [P, KD, 2 * D])
        w_ada, at = carve(work, at, [P, KD, 6 * D])
        row_gate, at = carve(work, at, [1, 4, D])
        hT, _ = carve(work, 0, [P, FC, CH])
        gT, _ = carve(work, 0, [P, MC, CH])
        sil, _ = carve(work, MC * CH, [P, 2, CH])
        at = 0
        sq, at = carve(work, at, [P, 2, CH])
        qn, at = carve(work, at, [P, 2, CH])
        ra, at = carve(work, at, [P, 2, CH])
        rb, at = carve(work, at, [P, CH])
        r1, at = carve(work, at, [P, CH])
        hb, at = carve(work, at, [P, 2, CH], BF16)
        mb, at = carve(work, at, [P, 2, CH], BF16)
        split, at = carve(work, at, [P, 2, 2 * NH * SP_ROWS], BF16)
        assert at <= 8192
        probs = work[:, :].rearrange("p (s h q) -> p s h q", s=2, h=QD)
        sreg = stacks[:, :, :, :].rearrange("p a h t -> p (a h t)").bitcast(F32)
        at = 0
        cosT, at = carve(sreg, at, [P, T])
        sinT, at = carve(sreg, at, [P, T])
        scr0, at = carve(sreg, at, [P, T])
        scr1, at = carve(sreg, at, [P, T])
        iota, at = carve(sreg, at, [P, T])
        decay, at = carve(sreg, at, [P, CH])
        b_nat, at = carve(sreg, at, [P, 2, D])
        b_T, at = carve(sreg, at, [P, 2, KD, P])
        c_nat, at = carve(sreg, at, [P, 2, KD, P])
        c_T, at = carve(sreg, at, [P, 2, D])
        c_w, at = carve(sreg, at, [P, 2, D])
        c_gated, at = carve(sreg, at, [P, B, 2, D])
        d_diag, at = carve(sreg, at, [P, B, KD, P])
        d_vec, at = carve(sreg, at, [P, KD])
        d_gate, at = carve(sreg, at, [P, KD, B])
        s_cos, at = carve(sreg, at, [P, CH])
        s_sin, at = carve(sreg, at, [P, CH])
        s_in, at = carve(sreg, at, [P, CH])
        s_y, at = carve(sreg, at, [P, 2, CH])
        s_z, at = carve(sreg, at, [P, 2, CH])
        condT, at = carve(sreg, at, [P, KD, B])
        csilu, at = carve(sreg, at, [P, KD, B])
        cond_b, at = carve(sreg, at, [P, KD, B, P])
        silu_b, at = carve(sreg, at, [P, KD, B, P])
        bias28, at = carve(sreg, at, [P, 28])
        mods, at = carve(sreg, at, [P, 28, B])
        prm, at = carve(sreg, at, [P, 48])
        pos_i, at = carve(sreg, at, [P, NT])
        ang, at = carve(sreg, at, [P, 6, NT * 8])
        freq, at = carve(sreg, at, [P, 8])
        lnw, at = carve(sreg, at, [P, 2, DH])
        row_in, at = carve(sreg, at, [1, 2, D])
        row_r = scr0[0:1, 0:2 * D].rearrange("p (a d) -> p a d", a=2)
        row_hml, at = carve(sreg, at, [1, 3, 2 * D], BF16)
        assert at <= NH * T, at
        pmax = sb("pmax", [P, QD, NT, 2])
        negm = sb("negm", [P, 3, QD * NT])
        shift3 = sb("shift3", [P, 3 * QD * NT], BF16)
        shiftT = sb("shiftT", [3 * QD * NT, P], BF16)
        pv_sb = uT[0][:, :, :].rearrange("p k n -> p (k n)")
        rden = sb("rden", [P, NT, QD])

        ld_x = sem("ld_x")
        ld_cond = sem("ld_cond")
        ld_adaln = sem("ld_adaln")
        ld_s5 = sem("ld_s5")
        ld_rows = sem("ld_rows")
        rows_split = sem("rows_split")
        ld_ffn = sem("ld_ffn")
        ld_blk = sem("ld_blk")
        passed = sem("passed")
        ones_set = sem("ones_set")
        consts = sem("consts")
        dve_pre = sem("dve_pre")
        act_silu = sem("act_silu")
        act_trig = sem("act_trig")
        trig_ready = sem("trig_ready")
        cond_ready = sem("cond_ready")
        mods_mm = sem("mods_mm")
        gates_mm = sem("gates_mm")
        bneg = sem("bneg")
        bc_T = sem("bc_T")
        s5_w = sem("s5_w")
        xn_ready = sem("xn_ready")
        tr_ready = sem("tr_ready")
        u_ready = sem("u_ready")
        u_used = sem("u_used")
        out_ready = sem("out_ready")
        out_used = sem("out_used")
        x_upd = sem("x_upd")
        nstep = sem("nstep")
        sstep = sem("sstep")
        bu_ready = sem("bu_ready")
        z_ready = sem("z_ready")
        h_ready = sem("h_ready")
        gelu_done = sem("gelu_done")
        qk_ready = sem("qk_ready")
        v_ready = sem("v_ready")
        sq_ready = sem("sq_ready")
        qn_done = sem("qn_done")
        v_copied = sem("v_copied")
        rope_done = sem("rope_done")
        qnstep = sem("qnstep")
        qsstep = sem("qsstep")
        part_ready = sem("part_ready")
        split_act = sem("split_act")
        stkT_act = sem("stkT_act")
        stkT_dve = sem("stkT_dve")
        stk_act = sem("stk_act")
        stk_dve = sem("stk_dve")
        bank_ready = sem("bank_ready")
        bank_used = sem("bank_used")
        mstep = sem("mstep")
        shift_dma = sem("shift_dma")
        st_ready = sem("st_ready")
        p_ready = sem("p_ready")
        pv_step = sem("pv_step")
        vq_ready = sem("vq_ready")
        pv_copied = sem("pv_copied")
        astep = sem("astep")
        g_ready = sem("g_ready")
        sil_ready = sem("sil_ready")
        gm_done = sem("gm_done")
        st_out = sem("st_out")

        SCAN_STEPS = 5
        START = {id(q): 2 for q in (tr_ready, u_used, out_ready, u_ready, stk_act, v_copied,
                                    p_ready, out_used, x_upd, sstep, qn_done, stk_dve, bank_used, pv_copied, rope_done)}
        START[id(shift_dma)] = 16
        START[id(pv_step)] = 2 * QP
        START[id(sstep)] = SCAN_STEPS + 1

        def start(eng, *sems):
            for q in sems:
                eng.sem_inc(q, START[id(q)])

        def reach(eng, q, n):
            eng.wait_ge(q, n + START.get(id(q), 0))

        class Steps:
            def __init__(self, eng, s, base=0):
                self.eng, self.s, self.base, self.n = eng, s, base, 0

            def __call__(self, ins):
                ins.then_inc(self.s, 1)
                self.n += 1

            def wait(self):
                reach(self.eng, self.s, self.base + self.n)

        LN_STEPS, RMS_STEPS = 21, 22
        QN_STEPS, QS_STEPS = 14, 2
        SHIFT_STEPS = 6

        MAXIMA = QD * NT * HC
        WITH_SHIFT, WITH_OUT = MAXIMA + 1, 2
        A_BATCH = WITH_SHIFT * NQ + WITH_OUT * NQ

        def shift_at(b, m):
            return A_BATCH * b + WITH_SHIFT * 2 + (WITH_SHIFT + WITH_OUT) * (m - 1)

        def before(b, n):
            return shift_at(b, n)

        def entries(u, with_out, with_max):
            todo = []
            if with_max:
                first = [0]
                for w in range(QD * NT):
                    first.append(min(MAXIMA, first[-1] + 2 + (w % 4 == 2)))
                todo = [("max", k) for k in range(first[u], first[u + 1])]
            if with_out and u in (8, 12):
                todo.insert(1, ("out", (u - 8) // 4))
            if with_max and u == 30:
                todo.append(("shift", 0))
            return todo

        def settle(eng):
            eng.sem_inc(passed, 1)

        def tok(c):
            return bass.ds(TT * c, TT)

        es.enter_context(nc.allow_non_contiguous_dma(reason="small vectors, one element a partition"))
        block = es.enter_context(nc.Block())

        @block.sync
        def _(sp):
            d = sp.dma_start
            start(sp, shift_dma)
            d(row_in[:, 0, :], A["L0_cond_b2"].unsqueeze(0)).then_inc(ld_cond, 16)
            d(row_in[:, 1, :], A["L1_cond_proj_b"].unsqueeze(0)).then_inc(ld_cond, 16)
            for k in range(KD):
                d(condT[:, k, :], A["cond_1024"][:, k * P:(k + 1) * P].rearrange("b p -> p b")).then_inc(ld_cond, 16)
            d(w_mod, A["L0_cond_Wm"].rearrange("(k p) n -> p k n", p=P)).then_inc(ld_adaln, 16)
            d(w_cond, A["L0_cond_Wc"].rearrange("(k p) n -> p k n", p=P)).then_inc(ld_adaln, 16)
            d(w_ada, A["L1_cond_adaln_w"].rearrange("(k p) n -> p k n", p=P)).then_inc(ld_adaln, 16)
            for i, (n, lo) in enumerate((("L0_cond_bm", 2), ("L0_cond_bm", 5), ("L1_cond_adaln_b", 2), ("L1_cond_adaln_b", 5))):
                d(row_gate[:, i, :], A[n][lo * D:(lo + 1) * D].unsqueeze(0)).then_inc(ld_adaln, 16)
            for n, lo, w in (("L0_cond_bm", 0, 12), ("L0_cond_bc", 12, 4), ("L1_cond_adaln_b", 16, 12)):
                d(bias28[:, lo:lo + w], A[n].rearrange("(m p) -> p m", p=P)).then_inc(ld_adaln, 16)
            d(x_tok[:, :, :], A["x"].rearrange("(t p) d -> p t d", p=P)).then_inc(ld_x, 16)
            d(w_ff1[:, :, :], A["L0_cond_W1"].rearrange("(k p) n -> p k n", p=P)).then_inc(ld_ffn, 16)
            d(w_ff2[:, :, :], A["L0_cond_W2"].rearrange("(k p) n -> p k n", p=P)).then_inc(ld_ffn, 16)
            d(b_ff1[:, :], A["L0_cond_b1"].rearrange("(m p) -> p m", p=P)).then_inc(ld_ffn, 16)
            d(w_qkv[:, :, :], A["L1_cond_qkv_w"].rearrange("(k p) n -> p k n", p=P)).then_inc(ld_blk, 16)
            d(w_proj[:, :, :], A["L1_cond_proj_w"].rearrange("(k p) n -> p k n", p=P)).then_inc(ld_blk, 16)
            d(w_g1[:, :, 0:HM], A["L1_cond_w1_w"].rearrange("(k p) n -> p k n", p=P)).then_inc(ld_blk, 16)
            d(w_g3[:, :, 0:HM], A["L1_cond_w3_w"].rearrange("(k p) n -> p k n", p=P)).then_inc(ld_blk, 16)
            full = HM // P
            d(w_g2[:, 0:full, :], A["L1_cond_w2_w"][0:full * P].rearrange("(k p) n -> p k n", p=P)).then_inc(ld_blk, 16)
            d(w_g2[0:HM - full * P, full, :], A["L1_cond_w2_w"][full * P:HM]).then_inc(ld_blk, 16)

            sp.wait_ge(rows_split, 1)
            sp.wait_ge(consts, 13)
            for i in range(3):
                d(bias_rows[i:i + 1, :, :].rearrange("p a d -> p (a d)"), row_hml[:, i, :]).then_inc(ld_rows, 16)

            def send_shift(b, m, at):
                reach(sp, bank_used, at)
                for s in range(3):
                    dst = q_st[SP_ROWS + s:SP_ROWS + s + 1, bass.ds(QD * m, QD), :].rearrange("s h (t q) -> s (h t) q", q=P)
                    d(dst, shiftT[QD * NT * s:QD * NT * (s + 1), :]).then_inc(shift_dma, 16)

            with sp.Fori(0, B) as b:
                send_shift(b, 0, A_BATCH * b + WITH_SHIFT)
                with sp.Fori(0, NQ - 1) as n:
                    send_shift(b, n + 1, shift_at(b, n + 1))
                for h in range(HC):
                    c = HC * b + h
                    reach(sp, x_upd, 2 * (4 + 4 * b + 2 + h + 1))
                    d(A["out"].rearrange("(t p) d -> p t d", p=P)[:, tok(c), :], x_tok[:, tok(c), :]).then_inc(st_out, 16)
            sp.wait_ge(st_out, 16 * B * HC)

        @block.gpsimd
        def _(pool):
            d = pool.dma_start
            start(pool, rope_done)
            for i, n in enumerate(("L0_cond_Lam_re", "L0_cond_Lam_im", "L0_cond_log_step")):
                for z in range(2):
                    d(prm[z * S:(z + 1) * S, i:i + 1], A[n].unsqueeze(1)).then_inc(ld_s5, 16)
            for z, (top, bot) in enumerate((("re", "im"), ("im", "re"))):
                d(b_nat[0:S, z, :], A[f"L0_cond_B_{top}"]).then_inc(ld_s5, 16)
                d(b_nat[S:P, z, :], A[f"L0_cond_B_{bot}"]).then_inc(ld_s5, 16)
                d(c_nat[:, z, :, 0:S], A[f"L0_cond_C_{top}"].rearrange("(k p) s -> p k s", p=P)).then_inc(ld_s5, 16)
                d(c_nat[:, z, :, S:P], A[f"L0_cond_C_{bot}"].rearrange("(k p) s -> p k s", p=P)).then_inc(ld_s5, 16)
            d(d_vec, A["L0_cond_D_diag"].rearrange("(k p) -> p k", p=P)).then_inc(ld_s5, 16)
            d(pos_i.bitcast(I32), A["pos_S"].rearrange("(t p) -> p t", p=P)).then_inc(ld_s5, 16)
            d(lnw[:, 0, :], A["L1_cond_lnq_w"].partition_broadcast(P)).then_inc(ld_s5, 16)
            d(lnw[:, 1, :], A["L1_cond_lnk_w"].partition_broadcast(P)).then_inc(ld_s5, 16)

            g = nc.gpsimd
            g.memset(ident[:, :], 0.0).then_inc(consts, 1)
            g.iota(scr1.bitcast(I32), pattern=[[1, T]], base=0, channel_multiplier=0).then_inc(consts, 1)
            pool.wait_ge(consts, 2)
            g.affine_select(out=ident[:, :], in_=ident[:, :], compare_op=ALU.not_equal, fill=1.0,
                            base=0, pattern=[[-1, P]], channel_multiplier=1).then_inc(consts, 1)
            g.tensor_copy(iota, scr1.bitcast(I32)).then_inc(consts, 1)
            pool.wait_ge(consts, 4)
            g.tensor_copy(ident_bf[:, :], ident[:, :]).then_inc(consts, 1)
            g.memset(ones_row[:, :], 1.0).then_inc(consts, 1)
            g.memset(w_g1[:, :, HM:HMP], 0.0).then_inc(consts, 1)
            g.memset(w_g3[:, :, HM:HMP], 0.0).then_inc(consts, 1)
            pool.wait_ge(consts, 8)
            g.memset(w_g2[HM - (MC - 1) * P:P, MC - 1, :], 0.0).then_inc(consts, 1)
            pool.wait_ge(consts, 9)
            g.memset(bias_rows[:, :, :], 0.0).then_inc(consts, 1)
            g.memset(ones_bf[:, :], 1.0).then_inc(consts, 1)
            g.memset(v_quad[:, :, :, :], 0.0).then_inc(consts, 1)
            pool.wait_ge(consts, 12)
            g.memset(v_quad[:, :, :, DH:DH + 1], 1.0).then_inc(consts, 1)

            def rotate(b, t):
                i = NT * b + t
                z = t % 2
                reach(pool, qn_done, i + 1)
                reach(pool, rope_done, 4 * i)
                if t >= 2:
                    pool.wait_ge(part_ready, 3 * (i - 1))
                src = qn[:, z, :].rearrange("p (a h d) -> p a h d", a=2, h=NH)
                dst_a = ra[:, z, :].rearrange("p (a h d) -> p a h d", a=2, h=NH)
                dst_b = rb.rearrange("p (a h d) -> p a h d", a=2, h=NH)
                ca = ropeA[:, t, :, :].unsqueeze(2).to_broadcast([P, 2, NH, DH])
                g.tensor_tensor(out=dst_a, in0=src, in1=ca, op=ALU.mult).then_inc(rope_done, 1)
                e = DH // 2
                for lo, hi in ((0, e), (e, 0)):
                    cb = ropeB[:, t, :, lo:lo + e].unsqueeze(2).to_broadcast([P, 2, NH, e])
                    g.tensor_tensor(out=dst_b[:, :, :, lo:lo + e], in0=src[:, :, :, hi:hi + e], in1=cb,
                                    op=ALU.mult).then_inc(rope_done, 1)
                reach(pool, rope_done, 4 * i + 3)
                g.tensor_tensor(out=ra[:, z, :], in0=ra[:, z, :], in1=rb, op=ALU.add).then_inc(rope_done, 1)

            def stage_v(b, n):
                reach(pool, v_copied, NT * (b + 1))
                reach(pool, pv_step, QP * NT * (4 * b + n))
                g.tensor_copy(v_quad[:, :, :, 0:DH],
                              v_tok[:, :, bass.ds(QD * DH * n, QD * DH)].rearrange("p t (h d) -> p t h d", h=QD))\
                 .then_inc(vq_ready, 1)

            pool.wait_ge(s5_w, 1)
            reach(pool, out_used, 2 * B * HC)
            one_pair = float(np.array([0x3F803F80], np.uint32).view(np.float32)[0])
            g.memset(k_st[SP_ROWS:P, :, :].bitcast(F32), one_pair).then_inc(ones_set, 1)
            with pool.Fori(0, B) as b:
                for t in range(NT):
                    rotate(b, t)
                with pool.Fori(0, NQ) as n:
                    stage_v(b, n)

        @block.vector
        def _(dve):
            v = nc.vector
            start(dve, out_used, x_upd, sstep, qn_done, stk_dve, bank_used)
            pre = Steps(dve, dve_pre)

            def ts(out, in0, s1, s2, op0, op1=None):
                if op1 is None:
                    pre(v.tensor_scalar(out, in0, s1, None, op0))
                else:
                    pre(v.tensor_scalar(out, in0, s1, s2, op0, op1))
                pre.wait()

            def tt(out, a, b, op):
                pre(v.tensor_tensor(out=out, in0=a, in1=b, op=op))
                pre.wait()

            def stt(out, a, s, b, op0, op1):
                pre(v.scalar_tensor_tensor(out=out, in0=a, scalar=s, in1=b, op0=op0, op1=op1))
                pre.wait()

            def cp(out, a):
                pre(v.tensor_copy(out, a))
                pre.wait()

            M, AD, SU = ALU.mult, ALU.add, ALU.subtract

            dve.wait_ge(ld_cond, 64)
            dve.wait_ge(act_silu, 1)
            cp(cond_b, condT.unsqueeze(3).to_broadcast([P, KD, B, P]))
            v.tensor_copy(silu_b, csilu.unsqueeze(3).to_broadcast([P, KD, B, P])).then_inc(cond_ready, 1)

            dve.wait_ge(ld_s5, 16 * 18)
            col = lambda i: prm[:, i:i + 1]
            (LRE, LIM, LS, DT, TH, N_, R_, PO, E_, MAG, PHI, PHH, PHL, LR, LI, DEN, CR, CI, SGN,
             X1, X2, S1, S2, S3, S4, TC, TS_, RD, AR) = range(29)
            pre(v.memset(prm[0:S, SGN:SGN + 1], 1.0))
            pre(v.memset(prm[S:P, SGN:SGN + 1], -1.0))
            v.tensor_scalar(b_nat[S:P, 1, :], b_nat[S:P, 1, :], -1.0, None, M).then_inc(bneg, 1)

            def exp_of(out, x):
                ts(col(X1), col(x), 88.0, -87.0, ALU.min, ALU.max)
                ts(col(N_), col(X1), 1.4426950408889634, MAGIC, M, AD)
                ts(col(N_), col(N_), MAGIC, None, SU)
                stt(col(R_), col(N_), -LN2_HI, col(X1), M, AD)
                stt(col(R_), col(N_), -LN2_LO, col(R_), M, AD)
                pre(v.memset(col(PO), 1.0 / 5040))
                pre.wait()
                for cf in (1.0 / 720, 1.0 / 120, 1.0 / 24, 1.0 / 6, 0.5, 1.0, 1.0):
                    ts(col(PO), col(PO), col(R_), cf, M, AD)
                ts(col(X2), col(N_), 127.0, None, AD)
                cp(col(E_).bitcast(I32), col(X2))
                pre(v.tensor_scalar(col(E_).bitcast(I32), col(E_).bitcast(I32), 23, None, ALU.logical_shift_left))
                pre.wait()
                tt(col(out), col(PO), col(E_), M)

            exp_of(DT, LS)
            tt(col(AR), col(LRE), col(DT), M)
            tt(col(TH), col(LIM), col(DT), M)
            exp_of(MAG, AR)
            ts(col(N_), col(TH), INV2PI, MAGIC, M, AD)
            ts(col(N_), col(N_), MAGIC, None, SU)
            stt(col(R_), col(N_), -TWO_PI_HI, col(TH), M, AD)
            stt(col(R_), col(N_), -TWO_PI_LO, col(R_), M, AD)
            ts(col(PHI), col(R_), INV2PI, None, M)
            ts(col(X1), col(PHI), 4096.0, MAGIC, M, AD)
            ts(col(PHH), col(X1), MAGIC, 1.0 / 4096, SU, M)
            tt(col(PHL), col(PHI), col(PHH), SU)

            dve.wait_ge(consts, 13)
            ts(scr0, iota, col(PHH), None, M)
            ts(scr1, scr0, MAGIC, MAGIC, AD, SU)
            tt(scr0, scr0, scr1, SU)
            stt(scr0, iota, col(PHL), scr0, M, AD)
            ts(scr1, scr0, MAGIC, MAGIC, AD, SU)
            tt(sinT, scr0, scr1, SU)
            ts(scr0, scr0, 0.25, None, AD)
            ts(scr1, scr0, MAGIC, MAGIC, AD, SU)
            tt(cosT, scr0, scr1, SU)
            cp(col(TS_), col(PHI))
            ts(col(X1), col(PHI), 0.25, None, AD)
            ts(col(X2), col(X1), MAGIC, MAGIC, AD, SU)
            tt(col(TC), col(X1), col(X2), SU)
            for i in range(8):
                f = float(np.float32(1.0) / np.float32(10000.0 ** (i / 8)))
                pre(v.memset(freq[:, i:i + 1], f))
            cp(ang[:, 5, 0:NT], pos_i.bitcast(I32))
            a3 = lambda r: ang[:, r, :].rearrange("p (t f) -> p t f", f=8)
            tt(a3(0), ang[:, 5, 0:NT].unsqueeze(2).to_broadcast([P, NT, 8]),
               freq.unsqueeze(1).to_broadcast([P, NT, 8]), M)

            def reduce_angle(out, a, s):
                ts(s, a, INV2PI, MAGIC, M, AD)
                ts(s, s, MAGIC, None, SU)
                stt(out, s, -TWO_PI_HI, a, M, AD)
                stt(out, s, -TWO_PI_LO, out, M, AD)

            reduce_angle(ang[:, 1, :], ang[:, 0, :], ang[:, 3, :])
            ts(ang[:, 2, :], ang[:, 1, :], float(np.pi / 2), None, AD)
            reduce_angle(ang[:, 2, :], ang[:, 2, :], ang[:, 3, :])
            for r in (1, 2):
                v.tensor_scalar(ang[:, r, :], ang[:, r, :], 3.1415925, -3.1415925, ALU.min, ALU.max).then_inc(trig_ready, 1)

            flat = lambda r: r.rearrange("p a d -> p (a d)")
            cp(row_hml[:, 0], flat(row_in))
            tt(flat(row_r), flat(row_in), row_hml[:, 0], SU)
            cp(row_hml[:, 1], flat(row_r))
            v.tensor_tensor(out=row_hml[:, 2], in0=flat(row_r), in1=row_hml[:, 1], op=SU).then_inc(rows_split, 1)

            dve.wait_ge(mods_mm, 1)
            dve.wait_ge(ld_adaln, 16 * 10)
            tt(mods, P01[:, 0:56].rearrange("p (m b) -> p m b", b=B), bias28.unsqueeze(2).to_broadcast([P, 28, B]), AD)
            m2 = lambda i: mods[:, i:i + 2, :]
            pre(v.tensor_copy(scal[:, SH_A], m2(0)))
            pre(v.tensor_scalar(scal[:, SC_A], m2(2), 1.0, None, AD))
            pre(v.tensor_copy(scal[:, SH_MSA], m2(16)))
            pre(v.tensor_scalar(scal[:, SC_MSA], m2(18), 1.0, None, AD))
            pre(v.tensor_copy(scal[:, SH_MLP], m2(22)))
            pre(v.tensor_scalar(scal[:, SC_MLP], m2(24), 1.0, None, AD))
            pre(v.tensor_scalar(m2(8), m2(8), 1.0, None, AD))
            pre.wait()
            stt(scal[:, SC_FF], m2(12), 1.0, m2(8), AD, M)
            tt(scal[:, SH_FF], m2(14), m2(8), M)
            tt(scal[:, SH_FF], scal[:, SH_FF], m2(6), AD)
            dve.wait_ge(gates_mm, 1)
            pre(v.tensor_copy(gate[:, 0:2], P45[:, :].rearrange("p (g b d) -> p g b d", g=2, b=B)))
            pre(v.tensor_copy(gate[:, 2:4], P67[:, :].rearrange("p (g b d) -> p g b d", g=2, b=B)))
            pre.wait()
            dve.wait_ge(bc_T, 1)
            pre(v.tensor_copy(b_T, P23[:, 0:CH].rearrange("p (z k m) -> p z k m", z=2, k=KD)))
            pre(v.tensor_copy(c_T, P23[:, CH:2 * CH].rearrange("p (z m) -> p z m", z=2)))
            dve.wait_ge(act_trig, 6)
            tt(col(LR), col(MAG), col(TC), M)
            ts(col(LR), col(LR), 1.0, None, SU)
            tt(col(LI), col(MAG), col(TS_), M)
            tt(col(DEN), col(LRE), col(LRE), M)
            tt(col(X1), col(LIM), col(LIM), M)
            tt(col(DEN), col(DEN), col(X1), AD)
            pre(v.reciprocal(col(RD), col(DEN)))
            pre.wait()
            tt(col(CR), col(LR), col(LRE), M)
            tt(col(X1), col(LI), col(LIM), M)
            tt(col(CR), col(CR), col(X1), AD)
            tt(col(CR), col(CR), col(RD), M)
            tt(col(CI), col(LI), col(LRE), M)
            tt(col(X1), col(LR), col(LIM), M)
            tt(col(CI), col(CI), col(X1), SU)
            tt(col(CI), col(CI), col(RD), M)
            ts(col(S1), col(CR), 2.0, None, M)
            tt(col(S1), col(S1), col(SGN), M)
            ts(col(S2), col(CI), -2.0, None, M)
            tt(col(S3), col(S2), col(SGN), M)
            ts(col(S4), col(CR), -2.0, None, M)
            ts(c_w[:, 0, :], c_T[:, 0, :], col(S1), None, M)
            stt(c_w[:, 0, :], c_T[:, 1, :], col(S2), c_w[:, 0, :], M, AD)
            ts(c_w[:, 1, :], c_T[:, 0, :], col(S3), None, M)
            stt(c_w[:, 1, :], c_T[:, 1, :], col(S4), c_w[:, 1, :], M, AD)
            for b in range(B):
                tt(c_gated[:, b], c_w, gate[:, 0, b, :].unsqueeze(1).to_broadcast([P, 2, D]), M)
            tt(d_gate, m2(4), d_vec.unsqueeze(2).to_broadcast([P, KD, B]), M)
            for b in range(B):
                for k in range(KD):
                    ts(d_diag[:, b, k, :], ident[:, :], d_gate[:, k, b:b + 1], None, M)
            cp(decay, col(MAG).to_broadcast([P, CH]))
            sn = a3(3)
            cs = a3(4)
            e = DH // 2
            ts(lnw[:, 0, :], lnw[:, 0, :], 1.0 / float(np.sqrt(DH)), None, M)
            for z in range(2):
                w = lambda lo: lnw[:, z, lo:lo + e].unsqueeze(1).to_broadcast([P, NT, e])
                pre(v.tensor_tensor(out=ropeA[:, :, z, 0:e], in0=cs, in1=w(0), op=M))
                pre(v.tensor_tensor(out=ropeA[:, :, z, e:DH], in0=cs, in1=w(e), op=M))
                pre(v.tensor_tensor(out=ropeB[:, :, z, e:DH], in0=sn, in1=w(0), op=M))
                pre(v.tensor_tensor(out=ropeB[:, :, z, 0:e], in0=sn, in1=w(e), op=M))
            pre.wait()
            v.tensor_scalar(ropeB[:, :, :, 0:e], ropeB[:, :, :, 0:e], -1.0, None, M).then_inc(s5_w, 1)

            def rsqrt(st, r, a, n):
                vv, y, hv, t0, t1 = (r[:, q, 0:n] for q in range(5))
                st(v.tensor_scalar(hv, vv, -0.5, None, M))
                st(v.tensor_scalar(t0.bitcast(I32), vv.bitcast(I32), 1, None, ALU.logical_shift_right))
                st.wait()
                st(v.tensor_scalar(y.bitcast(I32), t0.bitcast(I32), -1.0, 1597463007.0, M, AD))
                st.wait()
                for q in range(3):
                    st(v.tensor_tensor(out=t0, in0=y, in1=y, op=M))
                    st.wait()
                    st(v.tensor_tensor(out=t1, in0=t0, in1=hv, op=M))
                    st.wait()
                    st(v.scalar_tensor_tensor(out=y, in0=t1, scalar=1.5, in1=y, op0=AD, op1=M))
                    st.wait()

            def norm(c, g, gx, rms):
                st = Steps(dve, nstep, 8 * LN_STEPS + RMS_STEPS * (gx - 8) if rms else LN_STEPS * gx)
                for j in range(TT):
                    st(v.bn_stats(bn6[:, j, :], x_tok[:, bass.ds(TT * c + j, 1), :].rearrange("p a d -> p (a d)")))
                st.wait()
                settle(dve)
                for j in range(TT):
                    st(v.bn_aggr(mv[:, j, :], bn6[:, j, :]))
                st.wait()
                if rms:
                    st(v.tensor_tensor(out=nrm[:, 1, :], in0=mv[:, :, 0], in1=mv[:, :, 0], op=M))
                    st.wait()
                    st(v.scalar_tensor_tensor(out=nrm[:, 0, :], in0=nrm[:, 1, :], scalar=RMS_EPS, in1=mv[:, :, 1], op0=AD, op1=AD))
                else:
                    st(v.tensor_scalar(nrm[:, 0, :], mv[:, :, 1], LN_EPS, None, AD))
                st.wait()
                rsqrt(st, nrm, None, TT)
                reach(dve, tr_ready, g)
                for j in range(TT):
                    src = x_tok[:, bass.ds(TT * c + j, 1), :].rearrange("p a d -> p (a d)")
                    if rms:
                        ins = v.tensor_scalar(xn[:, j, :], src, nrm[:, 1, j:j + 1], None, M)
                    else:
                        ins = v.tensor_scalar(xn[:, j, :], src, mv[:, j, 0:1], nrm[:, 1, j:j + 1], SU, M)
                    ins.then_inc(xn_ready, 1)
                assert st.n == (RMS_STEPS if rms else LN_STEPS), st.n

            def residual(c, b, o, gi, xo):
                for q in range(2):
                    reach(dve, out_ready, 2 * o + q + 1)
                    reach(dve, x_upd, 2 * xo + q)
                    po = P45[:, q * CH:(q + 1) * CH].rearrange("p (a d) -> p a d", a=2)
                    gt = gate[:, gi, bass.ds(b, 1), :].to_broadcast([P, 2, D])
                    xx = x_tok[:, bass.ds(TT * c + 2 * q, 2), :]
                    v.tensor_tensor(out=tmp[q][:, :, :], in0=po, in1=gt, op=M).then_inc(out_used, 1)
                    reach(dve, out_used, 2 * o + q + 1)
                    v.tensor_tensor(out=xx, in0=xx, in1=tmp[q][:, :, :], op=AD).then_inc(x_upd, 1)

            def s5_scan(c, h):
                st = Steps(dve, sstep, SCAN_STEPS * c)
                tb = slice(h * CH, (h + 1) * CH)
                dve.wait_ge(bu_ready, c + 1)
                bu = (P23, P67)[h]
                st(v.tensor_tensor(out=s_cos, in0=bu[:, 0:CH], in1=cosT[:, tb], op=M))
                st(v.tensor_tensor(out=s_sin, in0=bu[:, CH:2 * CH], in1=sinT[:, tb], op=M))
                st.wait()
                st(v.tensor_tensor(out=s_in, in0=s_cos, in1=s_sin, op=AD))
                st.wait()
                init = 0.0 if h == 0 else s_y[:, h - 1, CH - 1:CH]
                st(v.tensor_tensor_scan(s_y[:, h, :], decay, s_in, init, M, AD))
                st.wait()
                reach(dve, out_ready, 2 * c)
                st(v.tensor_tensor(out=s_z[:, 0, :], in0=s_y[:, h, :], in1=cosT[:, tb], op=M))
                v.tensor_tensor(out=s_z[:, 1, :], in0=s_y[:, h, :], in1=sinT[:, tb], op=M).then_inc(z_ready, 1)
                assert st.n == SCAN_STEPS

            def s5_residual(c):
                for q in range(2):
                    reach(dve, out_ready, 2 * c + q + 1)
                    xx = x_tok[:, bass.ds(TT * c + 2 * q, 2), :].rearrange("p a d -> p (a d)")
                    v.tensor_tensor(out=xx, in0=xx, in1=P45[:, q * CH:(q + 1) * CH], op=AD).then_inc(out_used, 1)

            dve.wait_ge(ld_x, 16)
            norm(0, 0, 0, False)
            norm(1, 1, 1, False)
            s5_scan(0, 0)
            with dve.Fori(0, B - 1) as b:
                for h in range(1, HC + 1):
                    c = HC * b + h
                    norm(c + 1, c + 1, c + 1, False)
                    s5_scan(c, h % HC)
                    s5_residual(c - 1)
            for c in range(NCH - HC + 1, NCH):
                if c == NCH - 1:
                    norm(0, NCH, NCH, False)
                else:
                    norm(c + 1, c + 1, c + 1, False)
                s5_scan(c, c % HC)
                s5_residual(c - 1)
            s5_residual(NCH - 1)

            with dve.Fori(0, NCH - 1) as c:
                reach(dve, out_used, 2 * NCH)
                norm(c + 1, NCH + c + 1, NCH + c + 1, False)
                residual(c, c // HC, NCH + c, 1, c)
            residual(NCH - 1, B - 1, 2 * NCH - 1, 1, NCH - 1)

            def qk_norm(b, t):
                i = NT * b + t
                z = t % 2
                st = Steps(dve, qnstep, QN_STEPS * i)
                dve.wait_ge(sq_ready, i + 1)
                st(v.tensor_reduce(out=qnm[:, 3, :], in_=sq[:, z, :].rearrange("p (h d) -> p h d", d=DH), axis=AX.X, op=AD))
                st.wait()
                st(v.tensor_scalar(qnm[:, 0, :], qnm[:, 3, :], 1.0 / DH, RMS_EPS, M, AD))
                st.wait()
                rsqrt(st, qnm, None, 2 * NH)
                bank = P23[:, z * CH:(z + 1) * CH].rearrange("p (h d) -> p h d", d=DH)
                rr = qnm[:, 1, :].unsqueeze(2).to_broadcast([P, 2 * NH, DH])
                if t >= 2:
                    reach(dve, rope_done, 4 * (i - 1))
                v.tensor_tensor(out=qn[:, z, :].rearrange("p (h d) -> p h d", d=DH), in0=bank, in1=rr, op=M).then_inc(qn_done, 1)
                assert st.n == QN_STEPS, st.n

            def qk_split(b, t):
                i = NT * b + t
                st = Steps(dve, qsstep, QS_STEPS * i)
                z = t % 2
                if t >= 2:
                    dve.wait_ge(split_act, 4 * (i - 1))
                reach(dve, rope_done, 4 * i + 4)
                v.tensor_copy(hb[:, z, :], ra[:, z, :]).then_inc(part_ready, 1)
                dve.wait_ge(part_ready, 3 * i + 1)
                st(v.tensor_tensor(out=r1, in0=ra[:, z, :], in1=hb[:, z, :], op=SU))
                st.wait()
                v.tensor_copy(mb[:, z, :], r1).then_inc(part_ready, 1)
                dve.wait_ge(part_ready, 3 * i + 2)
                if t >= 2:
                    dve.wait_ge(stkT_dve, 2 * (i - 1))
                sp = split[:, z, :].rearrange("p (a h r) -> p a h r", a=2, h=NH)
                r4 = r1.rearrange("p (a h d) -> p a h d", a=2, h=NH)
                m4 = mb[:, z, :].rearrange("p (a h d) -> p a h d", a=2, h=NH)
                st(v.tensor_tensor(out=sp[:, 0, :, 5 * DH:6 * DH], in0=r4[:, 0], in1=m4[:, 0], op=SU))
                v.tensor_tensor(out=sp[:, 1, :, 2 * DH:3 * DH], in0=r4[:, 1], in1=m4[:, 1], op=SU).then_inc(part_ready, 1)

            def stack_in(b, t):
                i = NT * b + t
                for a in range(2):
                    dve.wait_ge(stkT_dve, 2 * i + a + 1)
                    dst = stacks[0:SP_ROWS, a, 8:16, t * P:(t + 1) * P]
                    src = P67[0:SP_ROWS, CH:2 * CH].bitcast(BF16).rearrange("p (h q) -> p h q", h=8)
                    v.tensor_copy(dst, src).then_inc(stk_dve, 1)

            def take_max(k, seq, pos):
                hd, t, half = k // 16, k // 2 % 8, k % 2
                dve.wait_ge(bank_ready, seq + 1)
                v.tensor_reduce(out=pmax[:, hd, t, half:half + 1], in_=P67[:, (pos % 2) * CH:(pos % 2 + 1) * CH], axis=AX.X,
                                op=ALU.max).then_inc(bank_used, 1)

            def shift_split(b, m, seq):
                st = Steps(dve, mstep, SHIFT_STEPS * (4 * b + m))
                reach(dve, bank_used, seq)
                w = QD * NT
                st(v.tensor_reduce(out=negm[:, 0, :], in_=pmax[:, :, :, :], axis=AX.X, op=ALU.max, negate=True))
                st.wait()
                st(v.tensor_copy(shift3[:, 0:w], negm[:, 0, :]))
                st.wait()
                st(v.tensor_tensor(out=negm[:, 1, :], in0=negm[:, 0, :], in1=shift3[:, 0:w], op=SU))
                st.wait()
                st(v.tensor_copy(shift3[:, w:2 * w], negm[:, 1, :]))
                st.wait()
                st(v.tensor_tensor(out=negm[:, 2, :], in0=negm[:, 1, :], in1=shift3[:, w:2 * w], op=SU))
                st.wait()
                st(v.tensor_copy(shift3[:, 2 * w:3 * w], negm[:, 2, :]))
                assert st.n == SHIFT_STEPS

            def shift_copy(b, m, seq, pos):
                dve.wait_ge(bank_ready, seq + 1)
                reach(dve, shift_dma, 48 * (4 * b + m))
                v.tensor_copy(shiftT[:, :], P67[0:3 * QD * NT, (pos % 2) * CH:(pos % 2) * CH + P // 2].bitcast(BF16))\
                 .then_inc(bank_used, 1)

            def attn_out(b, m, half, seq, pos):
                dve.wait_ge(bank_ready, seq + 1)
                pt = P67[:, (pos % 2) * CH:(pos % 2 + 1) * CH].rearrange("p (t h d) -> p t h d", t=TT, h=QD)
                tl = slice(TT * half, TT * (half + 1))
                v.reciprocal(rden[:, tl, :].unsqueeze(3), pt[:, :, :, DH:DH + 1]).then_inc(astep, 1)
                dve.wait_ge(astep, 2 * (4 * b + m) + half + 1)
                dst = attn[:, tl, bass.ds(QD * DH * m, QD * DH)].rearrange("p t (h d) -> p t h d", h=QD)
                v.tensor_tensor(out=dst, in0=pt[:, :, :, 0:DH], in1=rden[:, tl, :].unsqueeze(3).to_broadcast([P, TT, QD, DH]),
                                op=M).then_inc(bank_used, 1)

            def quad(b, n, base, with_out, with_max):
                pos = 0
                for u in range(QD * NT):
                    for kind, k in entries(u, with_out, with_max):
                        if kind == "max":
                            take_max(k, base + pos, pos)
                            if k == MAXIMA - 1:
                                shift_split(b, n + 1, base + pos + 1)
                        elif kind == "shift":
                            shift_copy(b, n + 1, base + pos, pos)
                        else:
                            attn_out(b, n - 1, k, base + pos, pos)
                        pos += 1

            def to_block(b, h):
                reach(dve, x_upd, 2 * (4 + 4 * b))
                settle(dve)
                norm(HC * b + h, 8 + 6 * b + h, 8 + 4 * b + h, True)

            with dve.Fori(0, B) as b:
                for h in range(HC):
                    if h == 0:
                        to_block(b, 0)
                    for t in range(TT * h, TT * (h + 1)):
                        qk_norm(b, t)
                        if t >= 3:
                            stack_in(b, t - 3)
                        if t >= 1:
                            qk_split(b, t - 1)
                        if t == TT - 2:
                            to_block(b, 1)
                stack_in(b, NT - 3)
                qk_split(b, NT - 1)
                stack_in(b, NT - 2)
                stack_in(b, NT - 1)
                for k in range(MAXIMA):
                    take_max(k, A_BATCH * b + k, k)
                shift_split(b, 0, A_BATCH * b + MAXIMA)
                shift_copy(b, 0, A_BATCH * b + MAXIMA, MAXIMA)
                quad(b, 0, A_BATCH * b + WITH_SHIFT, False, True)
                with dve.Fori(1, NQ - 1) as n:
                    quad(b, n, before(b, n), True, True)
                quad(b, NQ - 1, before(b, NQ - 1), True, False)
                for half in range(2):
                    attn_out(b, NQ - 1, half, before(b, NQ - 1) + WITH_OUT + half, half)
                for h in range(HC):
                    c, o = HC * b + h, 8 + 4 * b + h
                    residual(c, b, o, 2, o - 4)
                    reach(dve, x_upd, 2 * (o - 4) + 2)
                    settle(dve)
                    norm(c, 8 + 6 * b + 4 + h, 8 + 4 * b + 2 + h, True)
                for h in range(HC):
                    c, o = HC * b + h, 8 + 4 * b + 2 + h
                    for m in range(MC):
                        dve.wait_ge(sil_ready, MC * c + m + 1)
                        v.tensor_tensor(out=gT[:, m, :], in0=P67[:, (m % 2) * CH:(m % 2 + 1) * CH], in1=sil[:, m % 2, :],
                                        op=M).then_inc(gm_done, 1)
                    residual(c, b, o, 3, o - 4)

        @block.scalar
        def _(act):
            a = nc.scalar
            start(act, u_ready, stk_act, v_copied, p_ready, pv_copied)
            act.wait_ge(ld_cond, 64)
            a.activation(csilu, condT, ACT.Silu).then_inc(act_silu, 1)
            act.wait_ge(trig_ready, 2)
            two_pi = float(np.float32(2 * np.pi) * np.float32(1 - 2.0 ** -23))
            a.activation(sinT, sinT, ACT.Sin, scale=two_pi).then_inc(act_trig, 1)
            a.activation(cosT, cosT, ACT.Sin, scale=two_pi).then_inc(act_trig, 1)
            for q in (25, 26):
                a.activation(prm[:, q:q + 1], prm[:, q:q + 1], ACT.Sin, scale=two_pi).then_inc(act_trig, 1)
            a.activation(ang[:, 3, :], ang[:, 1, :], ACT.Sin).then_inc(act_trig, 1)
            a.activation(ang[:, 4, :], ang[:, 2, :], ACT.Sin).then_inc(act_trig, 1)

            def evacuate(g, par, b, sc, sh):
                reach(act, tr_ready, g + 1)
                reach(act, u_used, g - 1)
                settle(act)
                for k in range(KD):
                    src = P01[:, k * CH:(k + 1) * CH]
                    if sc is None:
                        ins = a.activation(uT[par][:, k, :], src, ACT.Copy)
                    else:
                        ins = a.activation(uT[par][:, k, :], src, ACT.Identity,
                                           scale=scal[:, sc, k, bass.ds(b, 1)], bias=scal[:, sh, k, bass.ds(b, 1)])
                    ins.then_inc(u_ready, 1)

            act.wait_ge(s5_w, 1)
            with act.Fori(0, B) as b:
                for h in range(HC):
                    evacuate(HC * b + h, h, b, SC_A, SH_A)
            evacuate(NCH, 0, 0, SC_FF, SH_FF)
            act.wait_ge(ld_ffn, 48)
            def gelus(c):
                for m in range(FC):
                    act.wait_ge(h_ready, FC * c + m + 1)
                    bank = (P23, P67)[m // 2 % 2][:, (m % 2) * CH:(m % 2 + 1) * CH]
                    a.activation(hT[:, m, :], bank, ACT.Gelu_apprx_tanh, bias=b_ff1[:, m:m + 1]).then_inc(gelu_done, 1)

            gelus(0)
            with act.Fori(0, B - 1) as b:
                for h in range(1, HC + 1):
                    c = HC * b + h
                    evacuate(NCH + c, h % HC, b + h // HC, SC_FF, SH_FF)
                    gelus(c)
            for c in range(NCH - HC + 1, NCH):
                evacuate(NCH + c, c % HC, B - 1, SC_FF, SH_FF)
                gelus(c)

            def tile_in(b, t):
                i = NT * b + t
                z = t % 2
                act.wait_ge(qk_ready, i + 1)
                a.activation(sq[:, z, :], P23[:, z * CH:(z + 1) * CH], ACT.Square).then_inc(sq_ready, 1)
                act.wait_ge(v_ready, i + 1)
                a.activation(v_tok[:, t, :], P45[:, z * CH:z * CH + D], ACT.Copy).then_inc(v_copied, 1)

            def slots(b, t):
                i = NT * b + t
                z = t % 2
                sp = split[:, z, :].rearrange("p (a h s d) -> p a h s d", a=2, h=NH, s=6)
                if t >= 2:
                    act.wait_ge(stkT_dve, 2 * (i - 1))
                for part, (src, qs, ks) in enumerate(((hb, slice(0, 3), slice(1, 6, 2)), (mb, slice(3, 5), slice(0, 5, 4)))):
                    act.wait_ge(part_ready, 3 * i + part + 1)
                    s4 = src[:, z, :].rearrange("p (a h d) -> p a h d", a=2, h=NH)
                    n = 3 - part
                    for w, sl in ((0, qs), (1, ks)):
                        a.activation(sp[:, w, :, sl, :], s4[:, w].unsqueeze(2).to_broadcast([P, NH, n, DH]), ACT.Copy)\
                         .then_inc(split_act, 1)

            def stack_in(b, t):
                i = NT * b + t
                for w in range(2):
                    act.wait_ge(stkT_act, 2 * i + w + 1)
                    dst = stacks[0:SP_ROWS, w, 0:8, t * P:(t + 1) * P]
                    src = P67[0:SP_ROWS, 0:CH].bitcast(BF16).rearrange("p (h q) -> p h q", h=8)
                    a.activation(dst, src, ACT.Copy).then_inc(stk_act, 1)

            def exps(b, n, with_out):
                for u in range(QD * NT):
                    t, hd = u // QD, u % QD
                    act.wait_ge(st_ready, QD * NT * (4 * b + n) + u + 1)
                    if hd == 0:
                        reach(act, pv_step, QP * (NT * (4 * b + n) + t - 1))
                    a.activation(probs[:, t % 2, hd, :], (P01, P23)[u % 2][:, :], ACT.Exp).then_inc(p_ready, 1)
                    if with_out and u in (2, 4):
                        pv_copy(b, n - 1, (u - 2) // 2, before(b, n))

            def pv_copy(b, m, half, seq):
                reach(act, pv_step, QP * NT * (4 * b + m) + QP * (NT - 1) + QP // 2 * (half + 1))
                act.wait_ge(bank_ready, seq)
                a.activation(pv_sb[:, half * CH:(half + 1) * CH], P45[:, half * CH:(half + 1) * CH], ACT.Copy).then_inc(pv_copied, 1)

            act.wait_ge(ld_blk, 16 * 6)
            with act.Fori(0, B) as b:
                for h in range(HC):
                    if h == 0:
                        evacuate(8 + 6 * b, 0, b, SC_MSA, SH_MSA)
                    for t in range(TT * h, TT * (h + 1)):
                        tile_in(b, t)
                        if t == TT - 1:
                            evacuate(8 + 6 * b + 1, 1, b, SC_MSA, SH_MSA)
                        if t >= 2:
                            slots(b, t - 2)
                        if t >= 3:
                            stack_in(b, t - 3)
                slots(b, NT - 2)
                stack_in(b, NT - 3)
                slots(b, NT - 1)
                stack_in(b, NT - 2)
                stack_in(b, NT - 1)
                exps(b, 0, False)
                with act.Fori(1, NQ) as n:
                    exps(b, n, True)
                for half in range(2):
                    pv_copy(b, NQ - 1, half, before(b, NQ - 1) + WITH_OUT)
                for h in range(HC):
                    evacuate(8 + 6 * b + 2 + h, h, b, None, None)
                evacuate(8 + 6 * b + 4, 0, b, SC_MLP, SH_MLP)
                for h in range(HC):
                    for m in range(MC):
                        c = HC * b + h
                        act.wait_ge(g_ready, MC * c + m + 1)
                        a.activation(sil[:, m % 2, :], P23[:, (m % 2) * CH:(m % 2 + 1) * CH], ACT.Silu).then_inc(sil_ready, 1)
                    if h < HC - 1:
                        evacuate(8 + 6 * b + 4 + h + 1, h + 1, b, SC_MLP, SH_MLP)

        @block.tensor
        def _(pe):
            mm = nc.tensor.matmul
            start(pe, tr_ready, u_used, out_ready, pv_step)

            def transposes(g, gx, src):
                reach(pe, u_ready, 2 * g)
                for j in range(TT):
                    if gx is not None:
                        pe.wait_ge(xn_ready, TT * gx + j + 1)
                    for k in range(KD):
                        ins = nc.tensor.transpose(P01[:, k * CH + j * P:k * CH + (j + 1) * P], src(j)[:, k * P:(k + 1) * P], ident[:, :])
                ins.then_inc(tr_ready, 1)

            norm_src = lambda j: xn[:, j, :]

            pe.wait_ge(ld_adaln, 16 * 10)
            pe.wait_ge(cond_ready, 1)
            chunks = [(w_mod, condT, m) for m in range(12)] + [(w_cond, condT, m) for m in range(4)] + [(w_ada, csilu, m) for m in range(12)]
            for i, (w, r, m) in enumerate(chunks):
                for k in range(KD):
                    ins = mm(P01[:, B * i:B * (i + 1)], w[:, k, m * P:(m + 1) * P], r[:, k, :], start=(k == 0), stop=(k == KD - 1))
            ins.then_inc(mods_mm, 1)
            pe.wait_ge(consts, 13)
            for i, (w, r, lo) in enumerate(((w_mod, cond_b, 2), (w_mod, cond_b, 5), (w_ada, silu_b, 2), (w_ada, silu_b, 5))):
                for b in range(B):
                    dst = (P45, P67)[i // 2][:, ((i % 2) * B + b) * D:((i % 2) * B + b + 1) * D]
                    for k in range(KD):
                        mm(dst, r[:, k, b, :], w[:, k, lo * D:(lo + 1) * D], start=(k == 0), stop=False)
                    ins = mm(dst, ones_row[:, :], row_gate[:, i, :], start=False, stop=True)
            ins.then_inc(gates_mm, 1)
            pe.wait_ge(bneg, 1)
            pe.wait_ge(ld_s5, 16 * 18)
            for z in range(2):
                for k in range(KD):
                    nc.tensor.transpose(P23[:, (z * KD + k) * P:(z * KD + k + 1) * P], b_nat[:, z, k * P:(k + 1) * P], ident[:, :])
            for z in range(2):
                for k in range(KD):
                    ins = nc.tensor.transpose(P23[:, CH + (z * KD + k) * P:CH + (z * KD + k + 1) * P], c_nat[:, z, k, :], ident[:, :])
            ins.then_inc(bc_T, 1)
            pe.wait_ge(s5_w, 1)

            def s5_in(c, h):
                reach(pe, u_ready, 2 * c + 2)
                reach(pe, sstep, SCAN_STEPS * (c - 1))
                for z in range(2):
                    for k in range(KD):
                        ins = mm((P23, P67)[h][:, z * CH:(z + 1) * CH], b_T[:, z, k, :], uT[h][:, k, :], start=(k == 0), stop=(k == KD - 1))
                ins.then_inc(bu_ready, 1)

            def s5_out(c, b, h):
                pe.wait_ge(z_ready, c + 1)
                for j in range(TT):
                    q = j // 2
                    if j % 2 == 0:
                        reach(pe, out_used, 2 * c + q - 1)
                    dst = P45[:, j * D:(j + 1) * D]
                    tk = slice(j * P, (j + 1) * P)
                    for k in range(KD):
                        ins = mm(dst[:, k * P:(k + 1) * P], uT[h][:, k, tk], d_diag[:, bass.ds(b, 1), k, :].rearrange("p a m -> p (a m)"),
                                 start=(k == 0), stop=False, skip_group_check=True)
                    if j == TT - 1:
                        ins.then_inc(u_used, 1)
                    for z in range(2):
                        ins = mm(dst, s_z[:, z, tk], c_gated[:, bass.ds(b, 1), z, :].rearrange("p a m -> p (a m)"),
                                 start=False, stop=(z == 1), skip_group_check=True)
                    if j % 2 == 1:
                        ins.then_inc(out_ready, 1)

            transposes(0, 0, norm_src)
            s5_in(0, 0)
            with pe.Fori(0, B - 1) as b:
                for h in range(HC):
                    c = HC * b + h
                    transposes(c + 1, c + 1, norm_src)
                    s5_in(c + 1, (h + 1) % HC)
                    s5_out(c, b, h)
            for c in range(NCH - HC, NCH):
                transposes(c + 1, c + 1, norm_src)
                if c < NCH - 1:
                    s5_in(c + 1, (c + 1) % HC)
                s5_out(c, B - 1, c % HC)

            def to_tokens(o, j, lhs, rhs, nk, bias, used):
                q = j // 2
                if j % 2 == 0:
                    reach(pe, out_used, 2 * o + q - 1)
                dst = P45[:, j * D:(j + 1) * D]
                for k in range(nk):
                    ins = mm(dst, lhs(k, slice(j * P, (j + 1) * P)), rhs(k), start=(k == 0), stop=(bias is None and k == nk - 1))
                    if used == (j, k):
                        ins.then_inc(u_used, 1)
                if bias is not None:
                    ins = mm(dst, ones_bf[:, :], bias_rows[:, bias, :], start=False, stop=True)
                if j % 2 == 1:
                    ins.then_inc(out_ready, 1)

            pe.wait_ge(ld_ffn, 48)
            pe.wait_ge(ld_rows, 48)
            def ffn(c, h, ahead):
                reach(pe, u_ready, 2 * (NCH + c) + 2)
                for m in range(FC):
                    if m >= 4:
                        pe.wait_ge(gelu_done, FC * c + m - 3)
                    bank = (P23, P67)[m // 2 % 2][:, (m % 2) * CH:(m % 2 + 1) * CH]
                    for k in range(KD):
                        ins = mm(bank, w_ff1[:, k, m * P:(m + 1) * P], uT[h][:, k, :], start=(k == 0), stop=(k == KD - 1))
                    ins.then_inc(h_ready, 1)
                if ahead:
                    transposes(NCH + c + 1, NCH + c + 1, norm_src)
                pe.wait_ge(gelu_done, FC * c + FC)
                for j in range(TT):
                    to_tokens(NCH + c, j, lambda k, tk: hT[:, k, tk], lambda k: w_ff2[:, k, :], FC, 0, (0, 0))

            with pe.Fori(0, B - 1) as b:
                for h in range(HC):
                    ffn(HC * b + h, h, True)
            for c in range(NCH - HC, NCH):
                ffn(c, c % HC, c < NCH - 1)

            def qkv(b, t):
                i = NT * b + t
                h, j, z = t // TT, t % TT, t % 2
                tk = slice(j * P, (j + 1) * P)
                if j == 0:
                    reach(pe, u_ready, 2 * (8 + 6 * b + h) + 2)
                reach(pe, qn_done, i - 1)
                for k in range(KD):
                    ins = mm(P23[:, z * CH:(z + 1) * CH], uT[h][:, k, tk], w_qkv[:, k, 0:2 * D], start=(k == 0), stop=(k == KD - 1))
                ins.then_inc(qk_ready, 1)
                reach(pe, v_copied, i - 1)
                for k in range(KD):
                    ins = mm(P45[:, z * CH:z * CH + D], uT[h][:, k, tk], w_qkv[:, k, 2 * D:3 * D], start=(k == 0), stop=(k == KD - 1))
                ins.then_inc(v_ready, 1)

            def stack_T(b, t, tells):
                i = NT * b + t
                pe.wait_ge(split_act, 4 * (i + 1))
                pe.wait_ge(part_ready, 3 * (i + 1))
                sp = split[:, t % 2, :].rearrange("p (a h r) -> p a h r", a=2, h=NH)
                for w in range(2):
                    for e, (freed, ready) in enumerate(((stk_act, stkT_act), (stk_dve, stkT_dve))):
                        reach(pe, freed, 2 * i + w)
                        bank = P67[0:SP_ROWS, e * CH:(e + 1) * CH].bitcast(BF16)
                        for hd in range(8):
                            ins = nc.tensor.transpose(bank[:, hd * P:(hd + 1) * P], sp[:, w, 8 * e + hd, :], ident_bf[:, :])
                            if tells and w == 0 and e == 0 and hd == 0:
                                ins.then_inc(u_used, 1)
                        ins.then_inc(ready, 1)

            def max_item(m, k, pos):
                hd, t, half = k // 16, k // 2 % 8, k % 2
                head = bass.ds(QD * m + hd, 1)
                mm(P67[:, (pos % 2) * CH:(pos % 2 + 1) * CH],
                   q_st[0:SP_ROWS, head, t * P:(t + 1) * P].rearrange("p a q -> p (a q)"),
                   k_st[0:SP_ROWS, head, half * CH:(half + 1) * CH].rearrange("p a q -> p (a q)"),
                   start=True, stop=True).then_inc(bank_ready, 1)

            def bank_free(base, pos):
                reach(pe, bank_used, base + pos - 1 if pos else base)

            def shift_T(b, m, pos):
                pe.wait_ge(mstep, SHIFT_STEPS * (4 * b + m + 1))
                nc.tensor.transpose(P67[0:3 * QD * NT, (pos % 2) * CH:(pos % 2) * CH + P // 2].bitcast(BF16), shift3[:, :],
                                    ident_bf[:, :]).then_inc(bank_ready, 1)

            def out_T(b, m, half, pos):
                reach(pe, pv_copied, 2 * (4 * b + m) + half + 1)
                for j in range(TT):
                    ins = nc.tensor.transpose(P67[:, (pos % 2) * CH + j * P:(pos % 2) * CH + (j + 1) * P],
                                              pv_sb[:, half * CH + j * P:half * CH + (j + 1) * P], ident[:, :])
                ins.then_inc(bank_ready, 1)

            def p_v(b, n, t, part):
                if part == 0:
                    reach(pe, p_ready, QD * NT * (4 * b + n) + QD * (t + 1))
                    if t == 0:
                        pe.wait_ge(vq_ready, 4 * b + n + 1)
                if t == 0 and part % (QP // HC) == 0:
                    reach(pe, pv_copied, 2 * (4 * b + n) - 1 + part // (QP // HC))
                tk = slice(part * T // QP, (part + 1) * T // QP)
                first = part % (QP // HC) == 0
                for hd in range(QD):
                    ins = mm(P45[32 * hd:32 * (hd + 1), tk], v_quad[:, t, hd, :], probs[:, t % 2, hd, tk],
                             start=(t == 0 and first), stop=(t == NT - 1 and not first), skip_group_check=True)
                ins.then_inc(pv_step, 1)

            def quad(b, n, base, with_out, with_max):
                reach(pe, shift_dma, 48 * (4 * b + n + 1))
                pos = 0
                for u in range(QD * NT):
                    t, hd = u // QD, u % QD
                    todo = entries(u, with_out, with_max)
                    for e in range(max(1, len(todo))):
                        if e < len(todo):
                            kind, k = todo[e]
                            bank_free(base, pos)
                            if kind == "max":
                                max_item(n + 1, k, pos)
                            elif kind == "shift":
                                shift_T(b, n + 1, pos)
                            else:
                                out_T(b, n - 1, k, pos)
                            pos += 1
                        if e == 0:
                            reach(pe, p_ready, QD * NT * (4 * b + n) + u - 1)
                            head = bass.ds(QD * n + hd, 1)
                            for half in range(2):
                                ins = mm((P01, P23)[u % 2][:, half * CH:(half + 1) * CH],
                                         k_st[0:ST_ROWS, head, t * P:(t + 1) * P].rearrange("p a q -> p (a q)"),
                                         q_st[0:ST_ROWS, head, half * CH:(half + 1) * CH].rearrange("p a q -> p (a q)"),
                                         start=True, stop=True)
                            ins.then_inc(st_ready, 1)
                    if t >= 1:
                        p_v(b, n, t - 1, hd)
                    elif with_out:
                        p_v(b, n - 1, NT - 1, hd)

            pe.wait_ge(ld_blk, 16 * 6)
            pe.wait_ge(ones_set, 1)
            with pe.Fori(0, B) as b:
                for h in range(HC):
                    if h == 0:
                        transposes(8 + 6 * b, 8 + 4 * b, norm_src)
                        reach(pe, out_used, 2 * (8 + 4 * b))
                    for t in range(TT * h, TT * (h + 1)):
                        qkv(b, t)
                        if t == TT - 1:
                            transposes(8 + 6 * b + 1, 8 + 4 * b + 1, norm_src)
                        if t >= 3:
                            stack_T(b, t - 3, t % TT == TT - 1)
                stack_T(b, NT - 3, False)
                stack_T(b, NT - 2, False)
                stack_T(b, NT - 1, False)
                reach(pe, stk_act, 2 * NT * (b + 1))
                reach(pe, stk_dve, 2 * NT * (b + 1))
                for k in range(MAXIMA):
                    bank_free(A_BATCH * b, k)
                    max_item(0, k, k)
                bank_free(A_BATCH * b, MAXIMA)
                shift_T(b, 0, MAXIMA)
                quad(b, 0, A_BATCH * b + WITH_SHIFT, False, True)
                with pe.Fori(1, NQ - 1) as n:
                    quad(b, n, before(b, n), True, True)
                quad(b, NQ - 1, before(b, NQ - 1), True, False)
                for part in range(QP):
                    p_v(b, NQ - 1, NT - 1, part)
                for half in range(2):
                    bank_free(before(b, NQ - 1) + WITH_OUT, half)
                    out_T(b, NQ - 1, half, half)
                reach(pe, bank_used, A_BATCH * (b + 1))
                for h in range(HC):
                    g, o = 8 + 6 * b + 2 + h, 8 + 4 * b + h
                    transposes(g, None, lambda j: attn[:, TT * h + j, :])
                    reach(pe, u_ready, 2 * g + 2)
                    for j in range(TT):
                        to_tokens(o, j, lambda k, tk: uT[h][:, k, tk], lambda k: w_proj[:, k, :], KD, 1, (TT - 1, KD - 1))
                transposes(8 + 6 * b + 4, 8 + 4 * b + 2, norm_src)
                for h in range(HC):
                    c, g, o = HC * b + h, 8 + 6 * b + 4 + h, 8 + 4 * b + 2 + h
                    reach(pe, u_ready, 2 * g + 2)
                    for m in range(MC):
                        if m >= 2:
                            pe.wait_ge(gm_done, MC * c + m - 1)
                        for bank, wt in ((P23, w_g1), (P67, w_g3)):
                            for k in range(KD):
                                ins = mm(bank[:, (m % 2) * CH:(m % 2 + 1) * CH], wt[:, k, m * P:(m + 1) * P], uT[h][:, k, :],
                                         start=(k == 0), stop=(k == KD - 1))
                        ins.then_inc(g_ready, 1)
                    if h < HC - 1:
                        transposes(g + 1, 8 + 4 * b + 2 + h + 1, norm_src)
                    pe.wait_ge(gm_done, MC * c + MC)
                    for j in range(TT):
                        to_tokens(o, j, lambda m, tk: gT[:, m, tk], lambda m: w_g2[:, m, :], MC, None, (0, 0))


INS = ("x", "cond_1024", "pos_S", "L0_cond_Wm", "L0_cond_bm", "L0_cond_Lam_re", "L0_cond_Lam_im", "L0_cond_B_re",
       "L0_cond_B_im", "L0_cond_C_re", "L0_cond_C_im", "L0_cond_D_diag", "L0_cond_log_step", "L0_cond_Wc", "L0_cond_bc",
       "L0_cond_W1", "L0_cond_b1", "L0_cond_W2", "L0_cond_b2", "L1_cond_adaln_w", "L1_cond_adaln_b", "L1_cond_qkv_w",
       "L1_cond_lnq_w", "L1_cond_lnk_w", "L1_cond_proj_w", "L1_cond_proj_b", "L1_cond_w1_w", "L1_cond_w3_w", "L1_cond_w2_w")


def kernel(**inputs):
    import concourse.bacc as bacc
    from concourse.bass_utils import run_bass_kernel_spmd

    nc = bacc.Bacc("TRN2", target_bir_lowering=False, num_devices=1)
    arrays, aps = {}, {}
    for name in INS:
        a = np.ascontiguousarray(inputs[name])
        if name == "x":
            a = a.reshape(B * T, D)
        arrays[f"in_{name}"] = a
        aps[name] = nc.dram_tensor(f"in_{name}", a.shape, mybir.dt.from_np(a.dtype), kind="ExternalInput").ap()
    aps["out"] = nc.dram_tensor("out", (B * T, D), F32, kind="ExternalOutput").ap()
    build(nc, aps)
    r = run_bass_kernel_spmd(nc, [arrays], core_ids=[0])
    return r.results[0]["out"].reshape(B, T, D)
```

```python
from contextlib import ExitStack

import numpy as np
import concourse.bass as bass
from concourse import mybir

F32 = mybir.dt.float32
BF16 = mybir.dt.bfloat16
I32 = mybir.dt.int32
ACT = mybir.ActivationFunctionType
ALU = mybir.AluOpType
AX = mybir.AxisListType

B, T, D = 2, 1024, 256
P = 128
CH = 512
HC = T // CH
NCH = B * HC
TT = CH // P
NT = T // P
KD = D // P
S = 64
F = 4 * D
FC = F // P
NH, DH = 16, 16
HM = 704
MC = (HM + P - 1) // P
HMP = MC * P
QP = 4
QD = 4
NQ = NH // QD
SP_ROWS = 6 * DH
ST_ROWS = SP_ROWS + 3
LN_EPS, RMS_EPS = 1e-5, 1e-6
MAGIC = 12582912.0
INV2PI = float(np.float32(1.0 / (2 * np.pi)))
TWO_PI_HI = 6.28125
TWO_PI_LO = float(np.float32(2 * np.pi - 6.28125))
LN2_HI = 0.693359375
LN2_LO = float(np.float32(np.log(2.0) - 0.693359375))


def build(nc, A):
    es = ExitStack()
    with es:
        def sb(name, shape, dt=F32):
            return es.enter_context(nc.sbuf_tensor(name, shape, dt))

        def sem(name):
            return es.enter_context(nc.semaphore(name))

        P01, P23, P45, P67 = [es.enter_context(nc.psum_tensor(n, [P, 2 * CH], F32)) for n in ("P01", "P23", "P45", "P67")]

        x_tok = sb("x_tok", [P, B * NT, D])
        xn = sb("xn", [P, TT, D])
        uT = [sb(f"uT{h}", [P, KD, CH]) for h in range(2)]
        w_ff1 = sb("w_ff1", [P, KD, F])
        w_ff2 = sb("w_ff2", [P, FC, D])
        w_qkv = sb("w_qkv", [P, KD, 3 * D])
        w_proj = sb("w_proj", [P, KD, D])
        w_g1 = sb("w_g1", [P, KD, HMP])
        w_g3 = sb("w_g3", [P, KD, HMP])
        w_g2 = sb("w_g2", [P, MC, D])
        b_ff1 = sb("b_ff1", [P, FC])
        bias_rows = sb("bias_rows", [P, 2, D], BF16)
        ones_bf = sb("ones_bf", [P, P], BF16)
        ident = sb("ident", [P, P])
        ident_bf = sb("ident_bf", [P, P], BF16)
        gate = sb("gate", [P, 4, B, D])
        scal = sb("scal", [P, 8, KD, B])
        SH_A, SC_A, SC_FF, SH_FF, SH_MSA, SC_MSA, SH_MLP, SC_MLP = range(8)
        tmp = [sb(f"tmp{q}", [P, 2, D]) for q in range(2)]
        warm = sb("warm", [P, 1])
        minus_half = sb("minus_half", [P, TT])
        epsilons = sb("epsilons", [P, 2, TT])
        qnm = sb("qnm", [P, 3, 2 * NH])
        bn6 = sb("bn6", [P, TT, 6])
        mv = sb("mv", [P, TT, 2])
        nrm = sb("nrm", [P, 3, TT])
        ropeA = sb("ropeA", [P, NT, 2, DH])
        ropeB = sb("ropeB", [P, NT, 2, DH])
        v_tok = sb("v_tok", [P, NT, D])
        v_quad = sb("v_quad", [P, NT, QD, 32])
        attn = sb("attn", [P, NT, D])
        work = sb("work", [P, 8192])
        stacks = sb("stacks", [P, 2, NH, T], BF16)
        q_st = stacks[:, 0]
        k_st = stacks[:, 1]

        def carve(base, at, shape, dt=F32):
            n = int(np.prod(shape[1:])) * (2 if dt == BF16 else 4) // 4
            ap = base[0:shape[0], at:at + n]
            if dt != F32:
                ap = ap.bitcast(dt)
            if len(shape) == 3:
                ap = ap.rearrange("p (a b) -> p a b", a=shape[1])
            if len(shape) == 4:
                ap = ap.rearrange("p (a b c) -> p a b c", a=shape[1], b=shape[2])
            return ap, at + n

        at = 0
        w_mod, at = carve(work, at, [P, KD, 6 * D])
        w_cond, at = carve(work, at, [P, KD, 2 * D])
        w_ada, at = carve(work, at, [P, KD, 6 * D])
        row_gate, at = carve(work, at, [P, 4, D])
        hT, _ = carve(work, 0, [P, FC, CH])
        gT, _ = carve(work, 0, [P, MC, CH])
        sil, _ = carve(work, MC * CH, [P, 2, CH])
        at = 0
        sq, at = carve(work, at, [P, 2, CH])
        qn, at = carve(work, at, [P, 2, CH])
        ra, at = carve(work, at, [P, 2, CH])
        rb, at = carve(work, at, [P, CH])
        r1, at = carve(work, at, [P, CH])
        hb, at = carve(work, at, [P, 2, CH], BF16)
        mb, at = carve(work, at, [P, 2, CH], BF16)
        split, at = carve(work, at, [P, 2, 2 * NH * SP_ROWS], BF16)
        assert at <= 8192
        probs = work[:, :].rearrange("p (s h q) -> p s h q", s=2, h=QD)
        sreg = stacks[:, :, :, :].rearrange("p a h t -> p (a h t)").bitcast(F32)
        at = 0
        cosT, at = carve(sreg, at, [P, T])
        sinT, at = carve(sreg, at, [P, T])
        scr0, at = carve(sreg, at, [P, T])
        scr1, at = carve(sreg, at, [P, T])
        iota, at = carve(sreg, at, [P, T])
        decay, at = carve(sreg, at, [P, CH])
        b_nat, at = carve(sreg, at, [P, 2, D])
        b_T, at = carve(sreg, at, [P, 2, KD, P])
        c_nat, at = carve(sreg, at, [P, 2, KD, P])
        c_T, at = carve(sreg, at, [P, 2, D])
        c_w, at = carve(sreg, at, [P, 2, D])
        c_gated, at = carve(sreg, at, [P, B, 2, D])
        d_diag, at = carve(sreg, at, [P, B, KD, P])
        d_vec, at = carve(sreg, at, [P, KD])
        d_gate, at = carve(sreg, at, [P, KD, B])
        s_cos, at = carve(sreg, at, [P, CH])
        s_sin, at = carve(sreg, at, [P, CH])
        s_in, at = carve(sreg, at, [P, CH])
        s_y, at = carve(sreg, at, [P, 2, CH])
        s_z, at = carve(sreg, at, [P, 2, CH])
        condT, at = carve(sreg, at, [P, KD, B])
        csilu, at = carve(sreg, at, [P, KD, B])
        cond_b, at = carve(sreg, at, [P, KD, B, P])
        silu_b, at = carve(sreg, at, [P, KD, B, P])
        bias22, at = carve(sreg, at, [P, 22])
        mods, at = carve(sreg, at, [P, 22, B])
        prm, at = carve(sreg, at, [P, 48])
        pos_i, at = carve(sreg, at, [P, NT])
        ang, at = carve(sreg, at, [P, 6, NT * 8])
        freq, at = carve(sreg, at, [P, 8])
        lnw, at = carve(sreg, at, [P, 2, DH])
        row_in, at = carve(sreg, at, [1, 2, D])
        row_r = attn[0:1, 0:2, :]
        row_hml, at = carve(sreg, at, [1, 3, 2 * D], BF16)
        assert at <= NH * T, at
        pmax = sb("pmax", [P, QD, NT, 2])
        negm = sb("negm", [P, 3, QD * NT])
        shift3 = sb("shift3", [P, 3 * QD * NT], BF16)
        shiftT = sb("shiftT", [3 * QD * NT, P], BF16)
        pv_sb = uT[0][:, :, :].rearrange("p k n -> p (k n)")
        rden = sb("rden", [P, NT, QD])

        ld_x0 = sem("ld_x0")
        ld_x = sem("ld_x")
        ld_cond = sem("ld_cond")
        ld_adaln = sem("ld_adaln")
        ld_s5 = sem("ld_s5")
        ld_step = sem("ld_step")
        ld_prm = sem("ld_prm")
        ld_mod = sem("ld_mod")
        ld_late = sem("ld_late")
        pre_copied = sem("pre_copied")
        pool_pre = sem("pool_pre")
        rope_args = sem("rope_args")
        rope_w = sem("rope_w")
        ld_rows = sem("ld_rows")
        rows_split = sem("rows_split")
        ld_ffn = sem("ld_ffn")
        ld_blk = sem("ld_blk")
        passed = sem("passed")
        ones_set = sem("ones_set")
        consts = sem("consts")
        dve_pre = sem("dve_pre")
        act_silu = sem("act_silu")
        act_trig = sem("act_trig")
        trig_ready = sem("trig_ready")
        cond_ready = sem("cond_ready")
        mods_mm = sem("mods_mm")
        dgate_ready = sem("dgate_ready")
        gate_a_mm = sem("gate_a_mm")
        gates_done = sem("gates_done")
        mods_used = sem("mods_used")
        gates_mm = sem("gates_mm")
        bneg = sem("bneg")
        bc_T = sem("bc_T")
        s5_w = sem("s5_w")
        xn_ready = sem("xn_ready")
        tr_ready = sem("tr_ready")
        u_ready = sem("u_ready")
        u_used = sem("u_used")
        out_ready = sem("out_ready")
        out_used = sem("out_used")
        x_upd = sem("x_upd")
        rstd_ready = sem("rstd_ready")
        qsum_steps = sem("qsum_steps")
        qrstd_ready = sem("qrstd_ready")
        rpow = sem("rpow")
        nstep = sem("nstep")
        sstep = sem("sstep")
        bu_ready = sem("bu_ready")
        z_ready = sem("z_ready")
        h_ready = sem("h_ready")
        gelu_done = sem("gelu_done")
        qk_ready = sem("qk_ready")
        v_ready = sem("v_ready")
        sq_ready = sem("sq_ready")
        qn_done = sem("qn_done")
        v_copied = sem("v_copied")
        rope_done = sem("rope_done")
        qsstep = sem("qsstep")
        part_ready = sem("part_ready")
        split_act = sem("split_act")
        stkT_act = sem("stkT_act")
        stkT_dve = sem("stkT_dve")
        stk_act = sem("stk_act")
        stk_dve = sem("stk_dve")
        bank_ready = sem("bank_ready")
        bank_used = sem("bank_used")
        mstep = sem("mstep")
        shift_dma = sem("shift_dma")
        st_ready = sem("st_ready")
        p_ready = sem("p_ready")
        pv_step = sem("pv_step")
        vq_ready = sem("vq_ready")
        pv_copied = sem("pv_copied")
        astep = sem("astep")
        g_ready = sem("g_ready")
        sil_ready = sem("sil_ready")
        gm_done = sem("gm_done")
        st_out = sem("st_out")

        SCAN_STEPS = 5
        START = {id(q): 2 for q in (tr_ready, u_used, out_ready, u_ready, stk_act, v_copied,
                                    p_ready, out_used, x_upd, sstep, qn_done, stk_dve, bank_used, pv_copied, rope_done)}
        START[id(shift_dma)] = 16
        START[id(pv_step)] = 2 * QP
        START[id(sstep)] = SCAN_STEPS + 1

        def start(eng, *sems):
            for q in sems:
                eng.sem_inc(q, START[id(q)])

        def reach(eng, q, n):
            eng.wait_ge(q, n + START.get(id(q), 0))

        class Steps:
            def __init__(self, eng, s, base=0):
                self.eng, self.s, self.base, self.n = eng, s, base, 0

            def __call__(self, ins):
                ins.then_inc(self.s, 1)
                self.n += 1

            def wait(self):
                reach(self.eng, self.s, self.base + self.n)

        PRE_COPIES = 2 + B * KD + 1 + 3
        LN_STEPS, RMS_STEPS = 2 * TT, 2 * TT + 2
        QS_STEPS = 2
        SHIFT_STEPS = 6

        MAXIMA, CARRY = QD * NT * HC, 10
        SHIFT_LAG = 3
        WITH_SHIFT, WITH_OUT = MAXIMA + 1, 2
        PROLOGUE = WITH_SHIFT + CARRY
        A_BATCH = PROLOGUE + WITH_SHIFT * (NQ - 1) + WITH_OUT * NQ

        def before(b, n):
            return A_BATCH * b + PROLOGUE + WITH_SHIFT + (WITH_SHIFT + WITH_OUT) * (n - 1)

        def shift_at(b, m):
            return before(b, m) - CARRY + SHIFT_LAG

        def entries(u, with_out, with_max):
            todo = []
            if with_max:
                todo = [("max", k) if k < MAXIMA else ("carry", k - MAXIMA) for k in range(CARRY + 2 * u, CARRY + 2 * u + 2)]
            if with_out and u in (8, 12):
                todo.insert(1, ("out", (u - 8) // 4))
            if ("carry", SHIFT_LAG - 1) in todo:
                todo.insert(todo.index(("carry", SHIFT_LAG - 1)) + 1, ("shift", 0))
            return todo

        def bank_of(pos, wide):
            pair = P45 if wide and pos // 2 % 2 else P67
            return pair[:, (pos % 2) * CH:(pos % 2 + 1) * CH]

        def prologue_entries():
            todo = [("max", k) for k in range(MAXIMA)] + [("carry", k) for k in range(CARRY)]
            todo.insert(MAXIMA + SHIFT_LAG, ("shift", 0))
            return todo

        def settle(eng):
            eng.sem_inc(passed, 1)

        def tok(c):
            return bass.ds(TT * c, TT)

        es.enter_context(nc.allow_non_contiguous_dma(reason="small vectors, one element a partition"))
        block = es.enter_context(nc.Block())

        @block.sync
        def _(sp):
            d = sp.dma_start
            start(sp, shift_dma)
            for i, n, ld in ((2, "L0_cond_log_step", ld_step), (0, "L0_cond_Lam_re", ld_prm), (1, "L0_cond_Lam_im", ld_prm)):
                for z in range(2):
                    d(prm[z * S:(z + 1) * S, i:i + 1], A[n].unsqueeze(1)).then_inc(ld, 16)
            for k in range(KD):
                d(condT[:, k, :], A["cond_1024"][:, k * P:(k + 1) * P].rearrange("b p -> p b")).then_inc(ld_cond, 16)
            def load_x(c):
                d(x_tok[:, tok(c), :], A["x"].rearrange("(t p) d -> p t d", p=P)[:, tok(c), :]).then_inc(ld_x0 if c == 0 else ld_x, 16)

            d(bias22[:, 0:10], A["L0_cond_bm"][0:10 * P].rearrange("(m p) -> p m", p=P)).then_inc(ld_mod, 16)
            d(row_gate[:, 0, :], A["L0_cond_bm"][2 * D:3 * D].partition_broadcast(P)).then_inc(ld_mod, 16)
            d(w_mod, A["L0_cond_Wm"].rearrange("(k p) n -> p k n", p=P)).then_inc(ld_mod, 16)
            for z, (top, bot) in enumerate((("re", "im"), ("im", "re"))):
                d(b_nat[0:S, z, :], A[f"L0_cond_B_{top}"]).then_inc(ld_s5, 16)
                d(b_nat[S:P, z, :], A[f"L0_cond_B_{bot}"]).then_inc(ld_s5, 16)
                d(c_nat[:, z, :, 0:S], A[f"L0_cond_C_{top}"].rearrange("(k p) s -> p k s", p=P)).then_inc(ld_s5, 16)
                d(c_nat[:, z, :, S:P], A[f"L0_cond_C_{bot}"].rearrange("(k p) s -> p k s", p=P)).then_inc(ld_s5, 16)
            d(d_vec, A["L0_cond_D_diag"].rearrange("(k p) -> p k", p=P)).then_inc(ld_s5, 16)
            d(w_cond, A["L0_cond_Wc"].rearrange("(k p) n -> p k n", p=P)).then_inc(ld_adaln, 16)
            d(w_ada, A["L1_cond_adaln_w"].rearrange("(k p) n -> p k n", p=P)).then_inc(ld_adaln, 16)
            load_x(0)
            for i, (n, lo) in enumerate((("L0_cond_bm", 5), ("L1_cond_adaln_b", 2), ("L1_cond_adaln_b", 5))):
                d(row_gate[:, 1 + i, :], A[n][lo * D:(lo + 1) * D].partition_broadcast(P)).then_inc(ld_adaln, 16)
            for n, first, lo in (("L0_cond_bc", 0, 10), ("L1_cond_adaln_b", 0, 14), ("L1_cond_adaln_b", 6, 18)):
                d(bias22[:, lo:lo + 4], A[n][first * P:(first + 4) * P].rearrange("(m p) -> p m", p=P)).then_inc(ld_adaln, 16)
            for c in range(1, NCH):
                load_x(c)
            d(w_ff1[:, :, :], A["L0_cond_W1"].rearrange("(k p) n -> p k n", p=P)).then_inc(ld_ffn, 16)
            d(w_ff2[:, :, :], A["L0_cond_W2"].rearrange("(k p) n -> p k n", p=P)).then_inc(ld_ffn, 16)
            d(b_ff1[:, :], A["L0_cond_b1"].rearrange("(m p) -> p m", p=P)).then_inc(ld_ffn, 16)
            d(w_qkv[:, :, :], A["L1_cond_qkv_w"].rearrange("(k p) n -> p k n", p=P)).then_inc(ld_blk, 16)
            d(w_proj[:, :, :], A["L1_cond_proj_w"].rearrange("(k p) n -> p k n", p=P)).then_inc(ld_blk, 16)
            d(w_g1[:, :, 0:HM], A["L1_cond_w1_w"].rearrange("(k p) n -> p k n", p=P)).then_inc(ld_blk, 16)
            d(w_g3[:, :, 0:HM], A["L1_cond_w3_w"].rearrange("(k p) n -> p k n", p=P)).then_inc(ld_blk, 16)
            full = HM // P
            d(w_g2[:, 0:full, :], A["L1_cond_w2_w"][0:full * P].rearrange("(k p) n -> p k n", p=P)).then_inc(ld_blk, 16)
            d(w_g2[0:HM - full * P, full, :], A["L1_cond_w2_w"][full * P:HM]).then_inc(ld_blk, 16)

            sp.wait_ge(rows_split, 1)
            sp.wait_ge(consts, 15)
            for i in range(3):
                d(bias_rows[i:i + 1, :, :].rearrange("p a d -> p (a d)"), row_hml[:, i, :]).then_inc(ld_rows, 16)

            def send_shift(b, m, at):
                reach(sp, bank_used, at)
                for s in range(3):
                    dst = q_st[SP_ROWS + s:SP_ROWS + s + 1, bass.ds(QD * m, QD), :].rearrange("s h (t q) -> s (h t) q", q=P)
                    d(dst, shiftT[QD * NT * s:QD * NT * (s + 1), :]).then_inc(shift_dma, 16)

            with sp.Fori(0, B) as b:
                send_shift(b, 0, A_BATCH * b + WITH_SHIFT + SHIFT_LAG)
                with sp.Fori(0, NQ - 1) as n:
                    send_shift(b, n + 1, shift_at(b, n + 1))
                for h in range(HC):
                    c = HC * b + h
                    reach(sp, x_upd, 2 * (NCH + 4 * b + 2 + h + 1))
                    d(A["out"].rearrange("(t p) d -> p t d", p=P)[:, tok(c), :], x_tok[:, tok(c), :]).then_inc(st_out, 16)
            sp.wait_ge(st_out, 16 * B * HC)

        @block.gpsimd
        def _(pool):
            d = pool.dma_start
            start(pool, rope_done)
            g = nc.gpsimd
            g.iota(scr1.bitcast(I32), pattern=[[1, T]], base=0, channel_multiplier=0).then_inc(consts, 1)
            pool.wait_ge(consts, 1)
            g.tensor_copy(iota, scr1.bitcast(I32)).then_inc(consts, 1)
            pool.wait_ge(consts, 2)
            g.memset(ident[:, :], 0.0).then_inc(consts, 1)
            pool.wait_ge(consts, 3)
            g.affine_select(out=ident[:, :], in_=ident[:, :], compare_op=ALU.not_equal, fill=1.0,
                            base=0, pattern=[[-1, P]], channel_multiplier=1).then_inc(consts, 1)
            pool.wait_ge(consts, 4)
            g.tensor_copy(ident_bf[:, :], ident[:, :]).then_inc(consts, 1)
            d(pos_i.bitcast(I32), A["pos_S"].rearrange("(t p) -> p t", p=P)).then_inc(ld_late, 16)
            d(lnw[:, 0, :], A["L1_cond_lnq_w"].partition_broadcast(P)).then_inc(ld_late, 16)
            d(lnw[:, 1, :], A["L1_cond_lnk_w"].partition_broadcast(P)).then_inc(ld_late, 16)
            d(row_in[:, 0, :], A["L0_cond_b2"].unsqueeze(0)).then_inc(ld_late, 16)
            d(row_in[:, 1, :], A["L1_cond_proj_b"].unsqueeze(0)).then_inc(ld_late, 16)

            g.memset(minus_half[:, :], -0.5).then_inc(consts, 1)
            for i, eps in enumerate((LN_EPS, RMS_EPS)):
                g.memset(epsilons[:, i, :], eps).then_inc(consts, 1)
            g.memset(w_g1[:, :, HM:HMP], 0.0).then_inc(consts, 1)
            g.memset(w_g3[:, :, HM:HMP], 0.0).then_inc(consts, 1)
            pool.wait_ge(consts, 10)
            g.memset(w_g2[HM - (MC - 1) * P:P, MC - 1, :], 0.0).then_inc(consts, 1)
            pool.wait_ge(consts, 11)
            g.memset(bias_rows[:, :, :], 0.0).then_inc(consts, 1)
            g.memset(ones_bf[:, :], 1.0).then_inc(consts, 1)
            g.memset(v_quad[:, :, :, :], 0.0).then_inc(consts, 1)
            pool.wait_ge(consts, 14)
            g.memset(v_quad[:, :, :, DH:DH + 1], 1.0).then_inc(consts, 1)

            pre = Steps(pool, pool_pre)

            def rstd(gx, rms):
                pool.wait_ge(nstep, 8 * LN_STEPS + RMS_STEPS * (gx - 7) if rms else LN_STEPS * (gx + 1))
                var, eps = (nrm[:, 0, :], 1) if rms else (mv[:, :, 1], 0)
                g.tensor_tensor(out=nrm[:, 1, :], in0=var, in1=epsilons[:, eps, :], op=ALU.add).then_inc(rpow, 1)
                pool.wait_ge(rpow, gx + 1)
                g.tensor_tensor(out=nrm[:, 2, :], in0=nrm[:, 1, :], in1=minus_half[:, :], op=ALU.pow).then_inc(rstd_ready, 1)

            def ts(out, in0, s1, s2, op0, op1=None):
                pre(g.tensor_scalar(out, in0, s1, s2, op0) if op1 is None else g.tensor_scalar(out, in0, s1, s2, op0, op1))
                pre.wait()

            def tt(out, a, b, op):
                pre(g.tensor_tensor(out=out, in0=a, in1=b, op=op))
                pre.wait()

            def cp(out, a):
                pre(g.tensor_copy(out, a))
                pre.wait()

            M, AD, SU = ALU.mult, ALU.add, ALU.subtract
            rstd(0, False)
            pool.wait_ge(ld_late, 16 * 5)
            for i in range(8):
                f = float(np.float32(1.0) / np.float32(10000.0 ** (i / 8)))
                pre(g.memset(freq[:, i:i + 1], f))
            cp(ang[:, 5, 0:NT], pos_i.bitcast(I32))
            a3 = lambda r: ang[:, r, :].rearrange("p (t f) -> p t f", f=8)
            tt(a3(0), ang[:, 5, 0:NT].unsqueeze(2).to_broadcast([P, NT, 8]),
               freq.unsqueeze(1).to_broadcast([P, NT, 8]), M)

            def reduce_angle(out, a, s):
                ts(s, a, INV2PI, MAGIC, M, AD)
                ts(s, s, MAGIC, None, SU)
                ts(ang[:, 4, :], s, -TWO_PI_HI, None, M)
                tt(out, ang[:, 4, :], a, AD)
                ts(ang[:, 4, :], s, -TWO_PI_LO, None, M)
                tt(out, ang[:, 4, :], out, AD)

            reduce_angle(ang[:, 1, :], ang[:, 0, :], ang[:, 3, :])
            ts(ang[:, 2, :], ang[:, 1, :], float(np.pi / 2), None, AD)
            reduce_angle(ang[:, 2, :], ang[:, 2, :], ang[:, 3, :])
            for r in (1, 2):
                g.tensor_scalar(ang[:, r, :], ang[:, r, :], 3.1415925, -3.1415925, ALU.min, ALU.max).then_inc(rope_args, 1)

            with pool.Fori(1, NCH + 1) as gx:
                rstd(gx, False)
            flat = lambda r: r.rearrange("p a d -> p (a d)")
            cp(row_hml[:, 0], flat(row_in))
            tt(flat(row_r), flat(row_in), row_hml[:, 0], SU)
            cp(row_hml[:, 1], flat(row_r))
            g.tensor_tensor(out=row_hml[:, 2], in0=flat(row_r), in1=row_hml[:, 1], op=SU).then_inc(rows_split, 1)

            pool.wait_ge(act_trig, 6)
            sn = a3(3)
            cs = a3(4)
            e = DH // 2
            ts(lnw[:, 0, :], lnw[:, 0, :], 1.0 / float(np.sqrt(DH)), None, M)
            for z in range(2):
                w = lambda lo: lnw[:, z, lo:lo + e].unsqueeze(1).to_broadcast([P, NT, e])
                pre(g.tensor_tensor(out=ropeA[:, :, z, 0:e], in0=cs, in1=w(0), op=M))
                pre(g.tensor_tensor(out=ropeA[:, :, z, e:DH], in0=cs, in1=w(e), op=M))
                pre(g.tensor_tensor(out=ropeB[:, :, z, e:DH], in0=sn, in1=w(0), op=M))
                pre(g.tensor_tensor(out=ropeB[:, :, z, 0:e], in0=sn, in1=w(e), op=M))
            pre.wait()
            g.tensor_scalar(ropeB[:, :, :, 0:e], ropeB[:, :, :, 0:e], -1.0, None, M).then_inc(rope_w, 1)

            def rotate(b, t):
                i = NT * b + t
                z = t % 2
                reach(pool, qn_done, i + 1)
                reach(pool, rope_done, 4 * i)
                if t >= 2:
                    pool.wait_ge(part_ready, 3 * (i - 1))
                src = qn[:, z, :].rearrange("p (a h d) -> p a h d", a=2, h=NH)
                dst_a = ra[:, z, :].rearrange("p (a h d) -> p a h d", a=2, h=NH)
                dst_b = rb.rearrange("p (a h d) -> p a h d", a=2, h=NH)
                ca = ropeA[:, t, :, :].unsqueeze(2).to_broadcast([P, 2, NH, DH])
                g.tensor_tensor(out=dst_a, in0=src, in1=ca, op=ALU.mult).then_inc(rope_done, 1)
                e = DH // 2
                for lo, hi in ((0, e), (e, 0)):
                    cb = ropeB[:, t, :, lo:lo + e].unsqueeze(2).to_broadcast([P, 2, NH, e])
                    g.tensor_tensor(out=dst_b[:, :, :, lo:lo + e], in0=src[:, :, :, hi:hi + e], in1=cb,
                                    op=ALU.mult).then_inc(rope_done, 1)
                reach(pool, rope_done, 4 * i + 3)
                g.tensor_tensor(out=ra[:, z, :], in0=ra[:, z, :], in1=rb, op=ALU.add).then_inc(rope_done, 1)

            pool.wait_ge(rope_w, 1)
            pool.wait_ge(pre_copied, PRE_COPIES)
            for i in range(1, 4):
                g.tensor_tensor(out=gate[:, i], in0=gate[:, i], in1=row_gate[:, i, :].unsqueeze(1).to_broadcast([P, B, D]), op=AD)\
                 .then_inc(gates_done, 1)
            pool.wait_ge(gates_done, 3)
            reach(pool, out_used, 2 * B * HC)
            one_pair = float(np.array([0x3F803F80], np.uint32).view(np.float32)[0])
            g.memset(k_st[SP_ROWS:P, :, :].bitcast(F32), one_pair).then_inc(ones_set, 1)
            pool.wait_ge(ones_set, 1)
            with pool.Fori(NCH + 1, 2 * NCH) as gx:
                rstd(gx, False)
            rstd(8, True)
            with pool.Fori(0, B) as b:
                for t in range(NT):
                    if t == 0:
                        rstd(2 * NCH + 4 * b + 1, True)
                    rotate(b, t)
                for h in range(HC):
                    rstd(2 * NCH + 4 * b + 2 + h, True)
                rstd(2 * NCH + 4 * (b + 1), True)

        @block.vector
        def _(dve):
            v = nc.vector
            start(dve, out_used, x_upd, sstep, qn_done, stk_dve, bank_used)
            pre = Steps(dve, dve_pre)

            def ts(out, in0, s1, s2, op0, op1=None):
                if op1 is None:
                    pre(v.tensor_scalar(out, in0, s1, None, op0))
                else:
                    pre(v.tensor_scalar(out, in0, s1, s2, op0, op1))
                pre.wait()

            def tt(out, a, b, op):
                pre(v.tensor_tensor(out=out, in0=a, in1=b, op=op))
                pre.wait()

            def stt(out, a, s, b, op0, op1):
                pre(v.scalar_tensor_tensor(out=out, in0=a, scalar=s, in1=b, op0=op0, op1=op1))
                pre.wait()

            def cp(out, a):
                pre(v.tensor_copy(out, a))
                pre.wait()

            M, AD, SU = ALU.mult, ALU.add, ALU.subtract

            def norm_stats(c, gx, rms):
                st = Steps(dve, nstep, 8 * LN_STEPS + RMS_STEPS * (gx - 8) if rms else LN_STEPS * gx)
                for j in range(TT):
                    st(v.bn_stats(bn6[:, j, :], x_tok[:, bass.ds(TT * c + j, 1), :].rearrange("p a d -> p (a d)")))
                st.wait()
                settle(dve)
                for j in range(TT):
                    st(v.bn_aggr(mv[:, j, :], bn6[:, j, :]))
                if rms:
                    st.wait()
                    st(v.tensor_tensor(out=nrm[:, 1, :], in0=mv[:, :, 0], in1=mv[:, :, 0], op=M))
                    st.wait()
                    st(v.tensor_tensor(out=nrm[:, 0, :], in0=nrm[:, 1, :], in1=mv[:, :, 1], op=AD))
                assert st.n == (RMS_STEPS if rms else LN_STEPS), st.n

            def norm_apply(c, g, gx, rms):
                dve.wait_ge(rstd_ready, gx + 1)
                reach(dve, tr_ready, g)
                for j in range(TT):
                    src = x_tok[:, bass.ds(TT * c + j, 1), :].rearrange("p a d -> p (a d)")
                    if rms:
                        ins = v.tensor_scalar(xn[:, j, :], src, nrm[:, 2, j:j + 1], None, M)
                    else:
                        ins = v.tensor_scalar(xn[:, j, :], src, mv[:, j, 0:1], nrm[:, 2, j:j + 1], SU, M)
                    ins.then_inc(xn_ready, 1)

            def norm(c, g, gx, rms):
                norm_stats(c, gx, rms)
                norm_apply(c, g, gx, rms)

            def residual(c, b, o, gi, xo):
                for q in range(2):
                    reach(dve, out_ready, 2 * o + q + 1)
                    reach(dve, x_upd, 2 * xo + q)
                    po = P45[:, q * CH:(q + 1) * CH].rearrange("p (a d) -> p a d", a=2)
                    gt = gate[:, gi, bass.ds(b, 1), :].to_broadcast([P, 2, D])
                    xx = x_tok[:, bass.ds(TT * c + 2 * q, 2), :]
                    v.tensor_tensor(out=tmp[q][:, :, :], in0=po, in1=gt, op=M).then_inc(out_used, 1)
                    reach(dve, out_used, 2 * o + q + 1)
                    v.tensor_tensor(out=xx, in0=xx, in1=tmp[q][:, :, :], op=AD).then_inc(x_upd, 1)

            def s5_scan(c, h):
                st = Steps(dve, sstep, SCAN_STEPS * c)
                tb = slice(h * CH, (h + 1) * CH)
                dve.wait_ge(bu_ready, c + 1)
                bu = (P23, P67)[h]
                st(v.tensor_tensor(out=s_cos, in0=bu[:, 0:CH], in1=cosT[:, tb], op=M))
                st(v.tensor_tensor(out=s_sin, in0=bu[:, CH:2 * CH], in1=sinT[:, tb], op=M))
                st.wait()
                st(v.tensor_tensor(out=s_in, in0=s_cos, in1=s_sin, op=AD))
                st.wait()
                init = 0.0 if h == 0 else s_y[:, h - 1, CH - 1:CH]
                st(v.tensor_tensor_scan(s_y[:, h, :], decay, s_in, init, M, AD))
                st.wait()
                reach(dve, out_ready, 2 * c)
                st(v.tensor_tensor(out=s_z[:, 0, :], in0=s_y[:, h, :], in1=cosT[:, tb], op=M))
                v.tensor_tensor(out=s_z[:, 1, :], in0=s_y[:, h, :], in1=sinT[:, tb], op=M).then_inc(z_ready, 1)
                assert st.n == SCAN_STEPS

            dve.wait_ge(ld_step, 16 * 2)
            col = lambda i: prm[:, i:i + 1]
            (LRE, LIM, LS, DT, TH, N_, R_, PO, E_, MAG, PHI, PHH, PHL, LR, LI, DEN, CR, CI, SGN,
             X1, X2, S1, S2, S3, S4, TC, TS_, RD, AR) = range(29)
            pre(v.memset(prm[0:S, SGN:SGN + 1], 1.0))
            pre(v.memset(prm[S:P, SGN:SGN + 1], -1.0))
            def exp_of(out, x):
                ts(col(X1), col(x), 88.0, -87.0, ALU.min, ALU.max)
                ts(col(N_), col(X1), 1.4426950408889634, MAGIC, M, AD)
                ts(col(N_), col(N_), MAGIC, None, SU)
                stt(col(R_), col(N_), -LN2_HI, col(X1), M, AD)
                stt(col(R_), col(N_), -LN2_LO, col(R_), M, AD)
                pre(v.memset(col(PO), 1.0 / 5040))
                pre.wait()
                for cf in (1.0 / 720, 1.0 / 120, 1.0 / 24, 1.0 / 6, 0.5, 1.0, 1.0):
                    ts(col(PO), col(PO), col(R_), cf, M, AD)
                ts(col(X2), col(N_), 127.0, None, AD)
                cp(col(E_).bitcast(I32), col(X2))
                pre(v.tensor_scalar(col(E_).bitcast(I32), col(E_).bitcast(I32), 23, None, ALU.logical_shift_left))
                pre.wait()
                tt(col(out), col(PO), col(E_), M)

            exp_of(DT, LS)
            dve.wait_ge(ld_prm, 16 * 4)
            tt(col(AR), col(LRE), col(DT), M)
            tt(col(TH), col(LIM), col(DT), M)
            exp_of(MAG, AR)
            ts(col(N_), col(TH), INV2PI, MAGIC, M, AD)
            ts(col(N_), col(N_), MAGIC, None, SU)
            stt(col(R_), col(N_), -TWO_PI_HI, col(TH), M, AD)
            stt(col(R_), col(N_), -TWO_PI_LO, col(R_), M, AD)
            ts(col(PHI), col(R_), INV2PI, None, M)
            ts(col(X1), col(PHI), 4096.0, MAGIC, M, AD)
            ts(col(PHH), col(X1), MAGIC, 1.0 / 4096, SU, M)
            tt(col(PHL), col(PHI), col(PHH), SU)

            dve.wait_ge(consts, 2)
            ts(scr0, iota, col(PHH), None, M)
            ts(scr1, scr0, MAGIC, MAGIC, AD, SU)
            tt(scr0, scr0, scr1, SU)
            stt(scr0, iota, col(PHL), scr0, M, AD)
            ts(scr1, scr0, MAGIC, MAGIC, AD, SU)
            tt(sinT, scr0, scr1, SU)
            ts(scr0, scr0, 0.25, None, AD)
            ts(scr1, scr0, MAGIC, MAGIC, AD, SU)
            tt(cosT, scr0, scr1, SU)
            cp(col(TS_), col(PHI))
            ts(col(X1), col(PHI), 0.25, None, AD)
            ts(col(X2), col(X1), MAGIC, MAGIC, AD, SU)
            v.tensor_tensor(out=col(TC), in0=col(X1), in1=col(X2), op=SU).then_inc(trig_ready, 1)

            dve.wait_ge(ld_x0, 16)
            norm_stats(0, 0, False)

            m2 = lambda i: mods[:, i:i + 2, :]

            def take_mods(lo, hi, at, col0):
                dve.wait_ge(mods_mm, at)
                v.tensor_tensor(out=mods[:, lo:hi, :], in0=P01[:, col0 + B * lo:col0 + B * hi].rearrange("p (m b) -> p m b", b=B),
                                in1=bias22[:, lo:hi].unsqueeze(2).to_broadcast([P, hi - lo, B]), op=AD).then_inc(mods_used, 1)
                dve.wait_ge(mods_used, at)

            take_mods(0, 6, 1, 0)
            pre(v.tensor_copy(scal[:, SH_A], m2(0)))
            pre(v.tensor_scalar(scal[:, SC_A], m2(2), 1.0, None, AD))
            dve.wait_ge(ld_s5, 16 * 9)
            v.tensor_tensor(out=d_gate, in0=m2(4), in1=d_vec.unsqueeze(2).to_broadcast([P, KD, B]), op=M).then_inc(dgate_ready, 1)
            dve.wait_ge(act_trig, 4)
            tt(col(LR), col(MAG), col(TC), M)
            ts(col(LR), col(LR), 1.0, None, SU)
            tt(col(LI), col(MAG), col(TS_), M)
            tt(col(DEN), col(LRE), col(LRE), M)
            tt(col(X1), col(LIM), col(LIM), M)
            tt(col(DEN), col(DEN), col(X1), AD)
            pre(v.reciprocal(col(RD), col(DEN)))
            pre.wait()
            tt(col(CR), col(LR), col(LRE), M)
            tt(col(X1), col(LI), col(LIM), M)
            tt(col(CR), col(CR), col(X1), AD)
            tt(col(CR), col(CR), col(RD), M)
            tt(col(CI), col(LI), col(LRE), M)
            tt(col(X1), col(LR), col(LIM), M)
            tt(col(CI), col(CI), col(X1), SU)
            tt(col(CI), col(CI), col(RD), M)
            ts(col(S1), col(CR), 2.0, None, M)
            tt(col(S1), col(S1), col(SGN), M)
            ts(col(S2), col(CI), -2.0, None, M)
            tt(col(S3), col(S2), col(SGN), M)
            ts(col(S4), col(CR), -2.0, None, M)
            norm_apply(0, 0, 0, False)
            dve.wait_ge(ld_x, 16 * (NCH - 1))
            norm_stats(1, 1, False)
            dve.wait_ge(gate_a_mm, 1)
            dve.wait_ge(ld_mod, 16 * 3)
            tt(gate[:, 0], P45[:, 0:CH].rearrange("p (b d) -> p b d", b=B), row_gate[:, 0, :].unsqueeze(1).to_broadcast([P, B, D]), AD)
            dve.wait_ge(pre_copied, 2)
            ts(c_w[:, 0, :], c_T[:, 0, :], col(S1), None, M)
            stt(c_w[:, 0, :], c_T[:, 1, :], col(S2), c_w[:, 0, :], M, AD)
            ts(c_w[:, 1, :], c_T[:, 0, :], col(S3), None, M)
            stt(c_w[:, 1, :], c_T[:, 1, :], col(S4), c_w[:, 1, :], M, AD)
            for b in range(B):
                tt(c_gated[:, b], c_w, gate[:, 0, b, :].unsqueeze(1).to_broadcast([P, 2, D]), M)
            dve.wait_ge(ld_adaln, 16 * 8)
            take_mods(6, 22, 2, CH)
            pre(v.tensor_copy(scal[:, SH_MSA], m2(14)))
            pre(v.tensor_scalar(scal[:, SC_MSA], m2(16), 1.0, None, AD))
            pre(v.tensor_copy(scal[:, SH_MLP], m2(18)))
            pre(v.tensor_scalar(scal[:, SC_MLP], m2(20), 1.0, None, AD))
            pre(v.tensor_scalar(m2(8), m2(8), 1.0, None, AD))
            pre.wait()
            stt(scal[:, SC_FF], m2(10), 1.0, m2(8), AD, M)
            tt(scal[:, SH_FF], m2(12), m2(8), M)
            v.tensor_tensor(out=scal[:, SH_FF], in0=scal[:, SH_FF], in1=m2(6), op=AD).then_inc(s5_w, 1)

            dve.wait_ge(pre_copied, PRE_COPIES - 3)

            def s5_residual(c):
                for q in range(2):
                    reach(dve, out_ready, 2 * c + q + 1)
                    xx = x_tok[:, bass.ds(TT * c + 2 * q, 2), :].rearrange("p a d -> p (a d)")
                    v.tensor_tensor(out=xx, in0=xx, in1=P45[:, q * CH:(q + 1) * CH], op=AD).then_inc(out_used, 1)

            norm_apply(1, 1, 1, False)
            norm_stats(2, 2, False)
            s5_scan(0, 0)
            with dve.Fori(0, B - 1) as b:
                for h in range(1, HC + 1):
                    c = HC * b + h
                    norm_apply(c + 1, c + 1, c + 1, False)
                    s5_residual(c - 1)
                    reach(dve, out_used, 2 * c)
                    settle(dve)
                    norm_stats((c + 2) % NCH, c + 2, False)
                    s5_scan(c, h % HC)
            for c in range(NCH - HC + 1, NCH):
                norm_apply((c + 1) % NCH, c + 1, c + 1, False)
                s5_residual(c - 1)
                s5_scan(c, c % HC)
            s5_residual(NCH - 1)

            dve.wait_ge(gates_done, 3)
            with dve.Fori(0, NCH - 1) as c:
                reach(dve, out_used, 2 * NCH)
                norm(c + 1, NCH + c + 1, NCH + c + 1, False)
                residual(c, c // HC, NCH + c, 1, c)
            reach(dve, x_upd, 2)
            norm(0, 2 * NCH, 2 * NCH, True)
            residual(NCH - 1, B - 1, 2 * NCH - 1, 1, NCH - 1)

            def qk_sums(b, t):
                z = t % 2
                dve.wait_ge(sq_ready, NT * b + t + 1)
                st = Steps(dve, qsum_steps, 3 * (NT * b + t))
                st(v.tensor_reduce(out=qnm[:, 0, :], in_=sq[:, z, :].rearrange("p (h d) -> p h d", d=DH), axis=AX.X, op=AD))
                st.wait()
                st(v.tensor_scalar(qnm[:, 1, :], qnm[:, 0, :], 1.0 / DH, RMS_EPS, M, AD))
                st.wait()
                st(v.reciprocal(qnm[:, 0, :], qnm[:, 1, :]))

            def qk_scale(b, t):
                i = NT * b + t
                z = t % 2
                dve.wait_ge(qrstd_ready, i + 1)
                bank = P23[:, z * CH:(z + 1) * CH].rearrange("p (h d) -> p h d", d=DH)
                rr = qnm[:, 2, :].unsqueeze(2).to_broadcast([P, 2 * NH, DH])
                if t >= 2:
                    reach(dve, rope_done, 4 * (i - 1))
                v.tensor_tensor(out=qn[:, z, :].rearrange("p (h d) -> p h d", d=DH), in0=bank, in1=rr, op=M).then_inc(qn_done, 1)

            def qk_split(b, t):
                i = NT * b + t
                st = Steps(dve, qsstep, QS_STEPS * i)
                z = t % 2
                if t >= 2:
                    dve.wait_ge(split_act, 4 * (i - 1))
                reach(dve, rope_done, 4 * i + 4)
                v.tensor_copy(hb[:, z, :], ra[:, z, :]).then_inc(part_ready, 1)
                dve.wait_ge(part_ready, 3 * i + 1)
                st(v.tensor_tensor(out=r1, in0=ra[:, z, :], in1=hb[:, z, :], op=SU))
                st.wait()
                v.tensor_copy(mb[:, z, :], r1).then_inc(part_ready, 1)
                dve.wait_ge(part_ready, 3 * i + 2)
                if t >= 2:
                    dve.wait_ge(stkT_dve, 2 * (i - 1))
                sp = split[:, z, :].rearrange("p (a h r) -> p a h r", a=2, h=NH)
                r4 = r1.rearrange("p (a h d) -> p a h d", a=2, h=NH)
                m4 = mb[:, z, :].rearrange("p (a h d) -> p a h d", a=2, h=NH)
                st(v.tensor_tensor(out=sp[:, 0, :, 5 * DH:6 * DH], in0=r4[:, 0], in1=m4[:, 0], op=SU))
                v.tensor_tensor(out=sp[:, 1, :, 2 * DH:3 * DH], in0=r4[:, 1], in1=m4[:, 1], op=SU).then_inc(part_ready, 1)

            def stack_in(b, t):
                i = NT * b + t
                for a in range(2):
                    dve.wait_ge(stkT_dve, 2 * i + a + 1)
                    dst = stacks[0:SP_ROWS, a, 8:16, t * P:(t + 1) * P]
                    src = (P67, P01)[a][0:SP_ROWS, CH:2 * CH].bitcast(BF16).rearrange("p (h q) -> p h q", h=8)
                    v.tensor_copy(dst, src).then_inc(stk_dve, 1)

            def take_max(k, seq, bank):
                hd, t, half = k // 16, k // 2 % 8, k % 2
                dve.wait_ge(bank_ready, seq + 1)
                v.tensor_reduce(out=pmax[:, hd, t, half:half + 1], in_=bank, axis=AX.X,
                                op=ALU.max).then_inc(bank_used, 1)

            def shift_split(b, m, seq):
                st = Steps(dve, mstep, SHIFT_STEPS * (4 * b + m))
                reach(dve, bank_used, seq)
                w = QD * NT
                st(v.tensor_reduce(out=negm[:, 0, :], in_=pmax[:, :, :, :], axis=AX.X, op=ALU.max, negate=True))
                st.wait()
                st(v.tensor_copy(shift3[:, 0:w], negm[:, 0, :]))
                st.wait()
                st(v.tensor_tensor(out=negm[:, 1, :], in0=negm[:, 0, :], in1=shift3[:, 0:w], op=SU))
                st.wait()
                st(v.tensor_copy(shift3[:, w:2 * w], negm[:, 1, :]))
                st.wait()
                st(v.tensor_tensor(out=negm[:, 2, :], in0=negm[:, 1, :], in1=shift3[:, w:2 * w], op=SU))
                st.wait()
                st(v.tensor_copy(shift3[:, 2 * w:3 * w], negm[:, 2, :]))
                assert st.n == SHIFT_STEPS

            def shift_copy(b, m, seq, bank):
                dve.wait_ge(bank_ready, seq + 1)
                reach(dve, shift_dma, 48 * (4 * b + m))
                v.tensor_copy(shiftT[:, :], bank[0:3 * QD * NT, 0:P // 2].bitcast(BF16))\
                 .then_inc(bank_used, 1)

            def attn_out(b, m, half, seq, bank):
                dve.wait_ge(bank_ready, seq + 1)
                pt = bank.rearrange("p (t h d) -> p t h d", t=TT, h=QD)
                tl = slice(TT * half, TT * (half + 1))
                v.reciprocal(rden[:, tl, :].unsqueeze(3), pt[:, :, :, DH:DH + 1]).then_inc(astep, 1)
                dve.wait_ge(astep, 2 * (4 * b + m) + half + 1)
                dst = attn[:, tl, bass.ds(QD * DH * m, QD * DH)].rearrange("p t (h d) -> p t h d", h=QD)
                v.tensor_tensor(out=dst, in0=pt[:, :, :, 0:DH], in1=rden[:, tl, :].unsqueeze(3).to_broadcast([P, TT, QD, DH]),
                                op=M).then_inc(bank_used, 1)

            def stream(b, n, base, pos, todo):
                for kind, k in todo:
                    bank = bank_of(pos, isinstance(n, int) and n < 0)
                    if kind in ("max", "carry"):
                        take_max(k, base + pos, bank)
                        if kind == "max" and k == MAXIMA - 1:
                            shift_split(b, n + 1, base + pos + 1)
                    elif kind == "shift":
                        shift_copy(b, n + 1, base + pos, bank)
                    else:
                        attn_out(b, n - 1, k, base + pos, bank)
                    pos += 1
                return pos

            def quad(b, n, base, with_out, with_max):
                pos = 0
                for u in range(QD * NT):
                    pos = stream(b, n, base, pos, entries(u, with_out, with_max))

            with dve.Fori(0, B) as b:
                for h in range(HC):
                    if h == 0:
                        reach(dve, x_upd, 2 * (NCH + 4 * b))
                    for t in range(TT * h, TT * (h + 1)):
                        qk_sums(b, t)
                        if t >= 2:
                            qk_split(b, t - 2)
                        if t == 0:
                            norm_stats(HC * b + 1, 2 * NCH + 4 * b + 1, True)
                        qk_scale(b, t)
                        if t >= 3:
                            stack_in(b, t - 3)
                        if t == 0:
                            norm_apply(HC * b + 1, 2 * NCH + 6 * b + 1, 2 * NCH + 4 * b + 1, True)
                qk_split(b, NT - 2)
                stack_in(b, NT - 3)
                qk_split(b, NT - 1)
                stack_in(b, NT - 2)
                stack_in(b, NT - 1)
                stream(b, -1, A_BATCH * b, 0, prologue_entries())
                quad(b, 0, A_BATCH * b + PROLOGUE, False, True)
                with dve.Fori(1, NQ - 1) as n:
                    quad(b, n, before(b, n), True, True)
                quad(b, NQ - 1, before(b, NQ - 1), True, False)
                for half in range(2):
                    attn_out(b, NQ - 1, half, before(b, NQ - 1) + WITH_OUT + half, bank_of(half, False))
                for h in range(HC):
                    c, o = HC * b + h, 2 * NCH + 4 * b + h
                    residual(c, b, o, 2, o - 4)
                    reach(dve, x_upd, 2 * (o - 4) + 2)
                    settle(dve)
                    norm(c, 2 * NCH + 6 * b + 4 + h, 2 * NCH + 4 * b + 2 + h, True)
                for h in range(HC):
                    c, o = HC * b + h, 2 * NCH + 4 * b + 2 + h
                    for m in range(MC):
                        dve.wait_ge(sil_ready, MC * c + m + 1)
                        v.tensor_tensor(out=gT[:, m, :], in0=P67[:, (m % 2) * CH:(m % 2 + 1) * CH], in1=sil[:, m % 2, :],
                                        op=M).then_inc(gm_done, 1)
                        ahead = HC * ((b + 1) % B)
                        if h == HC - 1 and m == 1:
                            reach(dve, x_upd, 2 * (o - 4))
                            settle(dve)
                            norm_stats(ahead, 2 * NCH + 4 * (b + 1), True)
                        if h == HC - 1 and m == 3:
                            norm_apply(ahead, 2 * NCH + 6 * (b + 1), 2 * NCH + 4 * (b + 1), True)
                    residual(c, b, o, 3, o - 4)

        @block.scalar
        def _(act):
            a = nc.scalar
            start(act, u_ready, stk_act, v_copied, p_ready, pv_copied)
            act.wait_ge(ld_cond, 32)
            a.activation(csilu, condT, ACT.Silu).then_inc(act_silu, 1)
            act.wait_ge(act_silu, 1)
            a.activation(cond_b, condT.unsqueeze(3).to_broadcast([P, KD, B, P]), ACT.Copy).then_inc(cond_ready, 1)
            a.activation(silu_b, csilu.unsqueeze(3).to_broadcast([P, KD, B, P]), ACT.Copy).then_inc(cond_ready, 1)
            act.wait_ge(ld_s5, 16 * 9)
            a.activation(b_nat[S:P, 1, :], b_nat[S:P, 1, :], ACT.Copy, scale=-1.0).then_inc(bneg, 1)
            act.wait_ge(bc_T, 1)
            a.activation(b_T, P23[:, 0:CH].rearrange("p (z k m) -> p z k m", z=2, k=KD), ACT.Copy).then_inc(pre_copied, 1)
            a.activation(c_T, P23[:, CH:2 * CH].rearrange("p (z m) -> p z m", z=2), ACT.Copy).then_inc(pre_copied, 1)
            act.wait_ge(trig_ready, 1)
            two_pi = float(np.float32(2 * np.pi) * np.float32(1 - 2.0 ** -23))
            a.activation(sinT, sinT, ACT.Sin, scale=two_pi).then_inc(act_trig, 1)
            a.activation(cosT, cosT, ACT.Sin, scale=two_pi).then_inc(act_trig, 1)
            for q in (25, 26):
                a.activation(prm[:, q:q + 1], prm[:, q:q + 1], ACT.Sin, scale=two_pi).then_inc(act_trig, 1)
            act.wait_ge(dgate_ready, 1)
            for b in range(B):
                for k in range(KD):
                    a.activation(d_diag[:, b, k, :], ident[:, :], ACT.Copy, scale=d_gate[:, k, b:b + 1]).then_inc(pre_copied, 1)
            a.activation(decay, prm[:, 9:10].to_broadcast([P, CH]), ACT.Copy).then_inc(pre_copied, 1)
            def evacuate(g, par, b, sc, sh):
                reach(act, tr_ready, g + 1)
                reach(act, u_used, g - 1)
                settle(act)
                for k in range(KD):
                    src = P01[:, k * CH:(k + 1) * CH]
                    if sc is None:
                        ins = a.activation(uT[par][:, k, :], src, ACT.Copy)
                    else:
                        ins = a.activation(uT[par][:, k, :], src, ACT.Identity,
                                           scale=scal[:, sc, k, bass.ds(b, 1)], bias=scal[:, sh, k, bass.ds(b, 1)])
                    ins.then_inc(u_ready, 1)

            act.wait_ge(s5_w, 1)
            evacuate(0, 0, 0, SC_A, SH_A)
            act.wait_ge(gates_mm, 1)
            for i in range(1, 4):
                bank = (P45, P67)[i // 2][:, i % 2 * CH:(i % 2 + 1) * CH]
                a.activation(gate[:, i], bank.rearrange("p (b d) -> p b d", b=B), ACT.Copy).then_inc(pre_copied, 1)
            with act.Fori(0, B - 1) as b:
                for h in range(1, HC + 1):
                    evacuate(HC * b + h, h % HC, b + h // HC, SC_A, SH_A)
            for h in range(1, HC):
                evacuate(NCH - HC + h, h, B - 1, SC_A, SH_A)
            evacuate(NCH, 0, 0, SC_FF, SH_FF)
            act.wait_ge(rope_args, 2)
            a.activation(ang[:, 3, :], ang[:, 1, :], ACT.Sin).then_inc(act_trig, 1)
            a.activation(ang[:, 4, :], ang[:, 2, :], ACT.Sin).then_inc(act_trig, 1)
            act.wait_ge(ld_ffn, 48)
            def gelus(c):
                for m in range(FC):
                    act.wait_ge(h_ready, FC * c + m + 1)
                    bank = (P23, P67)[m // 2 % 2][:, (m % 2) * CH:(m % 2 + 1) * CH]
                    a.activation(hT[:, m, :], bank, ACT.Gelu_apprx_tanh, bias=b_ff1[:, m:m + 1]).then_inc(gelu_done, 1)

            gelus(0)
            with act.Fori(0, B - 1) as b:
                for h in range(1, HC + 1):
                    c = HC * b + h
                    evacuate(NCH + c, h % HC, b + h // HC, SC_FF, SH_FF)
                    gelus(c)
            for c in range(NCH - HC + 1, NCH):
                evacuate(NCH + c, c % HC, B - 1, SC_FF, SH_FF)
                gelus(c)

            def tile_in(b, t):
                i = NT * b + t
                z = t % 2
                act.wait_ge(qk_ready, i + 1)
                a.activation(sq[:, z, :], P23[:, z * CH:(z + 1) * CH], ACT.Square).then_inc(sq_ready, 1)
                act.wait_ge(v_ready, i + 1)
                a.activation(v_tok[:, t, :], P45[:, z * CH:z * CH + D], ACT.Copy).then_inc(v_copied, 1)

            def roots(b, t):
                act.wait_ge(qsum_steps, 3 * (NT * b + t + 1))
                a.activation(qnm[:, 2, :], qnm[:, 0, :], ACT.Sqrt).then_inc(qrstd_ready, 1)

            def slots(b, t):
                i = NT * b + t
                z = t % 2
                sp = split[:, z, :].rearrange("p (a h s d) -> p a h s d", a=2, h=NH, s=6)
                if t >= 2:
                    act.wait_ge(stkT_dve, 2 * (i - 1))
                for part, (src, qs, ks) in enumerate(((hb, slice(0, 3), slice(1, 6, 2)), (mb, slice(3, 5), slice(0, 5, 4)))):
                    act.wait_ge(part_ready, 3 * i + part + 1)
                    s4 = src[:, z, :].rearrange("p (a h d) -> p a h d", a=2, h=NH)
                    n = 3 - part
                    for w, sl in ((0, qs), (1, ks)):
                        a.activation(sp[:, w, :, sl, :], s4[:, w].unsqueeze(2).to_broadcast([P, NH, n, DH]), ACT.Copy)\
                         .then_inc(split_act, 1)

            def stack_in(b, t, w):
                act.wait_ge(stkT_act, 2 * (NT * b + t) + w + 1)
                dst = stacks[0:SP_ROWS, w, 0:8, t * P:(t + 1) * P]
                src = (P67, P01)[w][0:SP_ROWS, 0:CH].bitcast(BF16).rearrange("p (h q) -> p h q", h=8)
                a.activation(dst, src, ACT.Copy).then_inc(stk_act, 1)

            def stage_v(b, n):
                reach(act, v_copied, NT * (b + 1))
                reach(act, pv_step, QP * NT * (4 * b + n))
                settle(act)
                a.activation(v_quad[:, :, :, 0:DH], v_tok[:, :, bass.ds(QD * DH * n, QD * DH)].rearrange("p t (h d) -> p t h d", h=QD),
                             ACT.Copy).then_inc(vq_ready, 1)

            def exps(b, n, with_out):
                for u in range(QD * NT):
                    t, hd = u // QD, u % QD
                    act.wait_ge(st_ready, QD * NT * (4 * b + n) + u + 1)
                    if hd == 0:
                        reach(act, pv_step, QP * (NT * (4 * b + n) + t - 1))
                    a.activation(probs[:, t % 2, hd, :], (P01, P23)[u % 2][:, :], ACT.Exp).then_inc(p_ready, 1)
                    if u == 3:
                        stage_v(b, n)
                    if with_out and u in (2, 4):
                        pv_copy(b, n - 1, (u - 2) // 2, before(b, n))

            def pv_copy(b, m, half, seq):
                reach(act, pv_step, QP * NT * (4 * b + m) + QP * (NT - 1) + QP // 2 * (half + 1))
                act.wait_ge(bank_ready, seq)
                a.activation(pv_sb[:, half * CH:(half + 1) * CH], P45[:, half * CH:(half + 1) * CH], ACT.Copy).then_inc(pv_copied, 1)

            evacuate(2 * NCH, 0, 0, SC_MSA, SH_MSA)
            with act.Fori(0, B) as b:
                for h in range(HC):
                    for t in range(TT * h, TT * (h + 1)):
                        tile_in(b, t)
                        if t == 1:
                            evacuate(2 * NCH + 6 * b + 1, 1, b, SC_MSA, SH_MSA)
                        if t >= 3:
                            stack_in(b, t - 3, 0)
                        roots(b, t)
                        if t >= 3:
                            stack_in(b, t - 3, 1)
                        if t >= 2:
                            slots(b, t - 2)
                for t in range(NT - 3, NT):
                    if t < NT - 1:
                        slots(b, t + 1)
                    for w in range(2):
                        stack_in(b, t, w)
                a.activation(warm[:, :], ones_bf[:, 0:1], ACT.Exp)
                exps(b, 0, False)
                with act.Fori(1, NQ) as n:
                    exps(b, n, True)
                for half in range(2):
                    pv_copy(b, NQ - 1, half, before(b, NQ - 1) + WITH_OUT)
                for h in range(HC):
                    evacuate(2 * NCH + 6 * b + 2 + h, h, b, None, None)
                evacuate(2 * NCH + 6 * b + 4, 0, b, SC_MLP, SH_MLP)
                for h in range(HC):
                    for m in range(MC):
                        c = HC * b + h
                        act.wait_ge(g_ready, MC * c + m + 1)
                        a.activation(sil[:, m % 2, :], P23[:, (m % 2) * CH:(m % 2 + 1) * CH], ACT.Silu).then_inc(sil_ready, 1)
                    if h < HC - 1:
                        evacuate(2 * NCH + 6 * b + 4 + h + 1, h + 1, b, SC_MLP, SH_MLP)
                evacuate(2 * NCH + 6 * (b + 1), 0, (b + 1) % B, SC_MSA, SH_MSA)

        @block.tensor
        def _(pe):
            mm = nc.tensor.matmul
            start(pe, tr_ready, u_used, out_ready, pv_step)

            def transposes(g, gx, src):
                reach(pe, u_ready, 2 * g)
                for j in range(TT):
                    if gx is not None:
                        pe.wait_ge(xn_ready, TT * gx + j + 1)
                    for k in range(KD):
                        ins = nc.tensor.transpose(P01[:, k * CH + j * P:k * CH + (j + 1) * P], src(j)[:, k * P:(k + 1) * P], ident[:, :])
                ins.then_inc(tr_ready, 1)

            norm_src = lambda j: xn[:, j, :]

            def vectors(chunks, first, at):
                for i, (w, r, m) in enumerate(chunks):
                    for k in range(KD):
                        ins = mm(P01[:, at + B * (first + i):at + B * (first + i + 1)], w[:, k, m * P:(m + 1) * P], r[:, k, :],
                                 start=(k == 0), stop=(k == KD - 1))
                ins.then_inc(mods_mm, 1)

            def gate_rows(i, w, r, lo):
                for b in range(B):
                    dst = (P45, P67)[i // 2][:, ((i % 2) * B + b) * D:((i % 2) * B + b + 1) * D]
                    for k in range(KD):
                        ins = mm(dst, r[:, k, b, :], w[:, k, lo * D:(lo + 1) * D], start=(k == 0), stop=(k == KD - 1))
                return ins

            pe.wait_ge(ld_mod, 16 * 3)
            pe.wait_ge(cond_ready, 2)
            vectors([(w_mod, condT, m) for m in range(6)], 0, 0)
            gate_rows(0, w_mod, cond_b, 2).then_inc(gate_a_mm, 1)
            pe.wait_ge(consts, 4)
            pe.wait_ge(bneg, 1)
            pe.wait_ge(ld_s5, 16 * 9)
            for z in range(2):
                for k in range(KD):
                    nc.tensor.transpose(P23[:, (z * KD + k) * P:(z * KD + k + 1) * P], b_nat[:, z, k * P:(k + 1) * P], ident[:, :])
            for z in range(2):
                for k in range(KD):
                    ins = nc.tensor.transpose(P23[:, CH + (z * KD + k) * P:CH + (z * KD + k + 1) * P], c_nat[:, z, k, :], ident[:, :])
            ins.then_inc(bc_T, 1)
            pe.wait_ge(ld_adaln, 16 * 8)
            vectors([(w_mod, condT, m) for m in range(6, 10)] + [(w_cond, condT, m) for m in range(4)]
                    + [(w_ada, csilu, m) for m in (0, 1, 2, 3, 6, 7, 8, 9)], 6, CH)
            gate_rows(1, w_mod, cond_b, 5)
            pe.wait_ge(mods_used, 2)
            transposes(0, 0, norm_src)
            gate_rows(2, w_ada, silu_b, 2)
            pe.wait_ge(pre_copied, PRE_COPIES - 3)

            def s5_in(c, h):
                reach(pe, u_ready, 2 * c + 2)
                reach(pe, sstep, SCAN_STEPS * (c - 1))
                for z in range(2):
                    for k in range(KD):
                        ins = mm((P23, P67)[h][:, z * CH:(z + 1) * CH], b_T[:, z, k, :], uT[h][:, k, :], start=(k == 0), stop=(k == KD - 1))
                ins.then_inc(bu_ready, 1)

            def s5_direct(c, b, h):
                for j in range(TT):
                    if j % 2 == 0:
                        reach(pe, out_used, 2 * c + j // 2 - 1)
                    for k in range(KD):
                        ins = mm(P45[:, j * D + k * P:j * D + (k + 1) * P], uT[h][:, k, j * P:(j + 1) * P],
                                 d_diag[:, bass.ds(b, 1), k, :].rearrange("p a m -> p (a m)"),
                                 start=(j % 2 == 0 and k == 0), stop=False, skip_group_check=True)
                ins.then_inc(u_used, 1)

            def s5_out(c, b, h):
                pe.wait_ge(z_ready, c + 1)
                for j in range(TT):
                    for z in range(2):
                        ins = mm(P45[:, j * D:(j + 1) * D], s_z[:, z, j * P:(j + 1) * P],
                                 c_gated[:, bass.ds(b, 1), z, :].rearrange("p a m -> p (a m)"),
                                 start=False, stop=(z == 1 and j % 2 == 1), skip_group_check=True)
                    if j % 2 == 1:
                        ins.then_inc(out_ready, 1)

            s5_in(0, 0)
            gate_rows(3, w_ada, silu_b, 5).then_inc(gates_mm, 1)
            with pe.Fori(0, B - 1) as b:
                for h in range(HC):
                    c = HC * b + h
                    transposes(c + 1, c + 1, norm_src)
                    pe.wait_ge(pre_copied, PRE_COPIES)
                    s5_direct(c, b, h)
                    s5_in(c + 1, (h + 1) % HC)
                    s5_out(c, b, h)
            for c in range(NCH - HC, NCH):
                transposes(c + 1, c + 1, norm_src)
                s5_direct(c, B - 1, c % HC)
                if c < NCH - 1:
                    s5_in(c + 1, (c + 1) % HC)
                s5_out(c, B - 1, c % HC)

            def to_tokens(o, j, lhs, rhs, nk, bias, used):
                q = j // 2
                if j % 2 == 0:
                    reach(pe, out_used, 2 * o + q - 1)
                dst = P45[:, j * D:(j + 1) * D]
                for k in range(nk):
                    ins = mm(dst, lhs(k, slice(j * P, (j + 1) * P)), rhs(k), start=(k == 0), stop=(bias is None and k == nk - 1))
                    if used == (j, k):
                        ins.then_inc(u_used, 1)
                if bias is not None:
                    ins = mm(dst, ones_bf[:, :], bias_rows[:, bias, :], start=False, stop=True)
                if j % 2 == 1:
                    ins.then_inc(out_ready, 1)

            pe.wait_ge(ld_ffn, 48)
            pe.wait_ge(ld_rows, 48)
            def ffn(c, h):
                reach(pe, u_ready, 2 * (NCH + c) + 2)
                for m in range(FC):
                    if m >= 4:
                        pe.wait_ge(gelu_done, FC * c + m - 3)
                    bank = (P23, P67)[m // 2 % 2][:, (m % 2) * CH:(m % 2 + 1) * CH]
                    for k in range(KD):
                        ins = mm(bank, w_ff1[:, k, m * P:(m + 1) * P], uT[h][:, k, :], start=(k == 0), stop=(k == KD - 1))
                    ins.then_inc(h_ready, 1)
                transposes(NCH + c + 1, NCH + c + 1, norm_src)
                pe.wait_ge(gelu_done, FC * c + FC)
                for j in range(TT):
                    to_tokens(NCH + c, j, lambda k, tk: hT[:, k, tk], lambda k: w_ff2[:, k, :], FC, 0, (0, 0))

            with pe.Fori(0, B - 1) as b:
                for h in range(HC):
                    ffn(HC * b + h, h)
            for c in range(NCH - HC, NCH):
                ffn(c, c % HC)

            def qkv(b, t):
                i = NT * b + t
                h, j, z = t // TT, t % TT, t % 2
                tk = slice(j * P, (j + 1) * P)
                if j == 0:
                    reach(pe, u_ready, 2 * (2 * NCH + 6 * b + h) + 2)
                reach(pe, qn_done, i - 1)
                for k in range(KD):
                    ins = mm(P23[:, z * CH:(z + 1) * CH], uT[h][:, k, tk], w_qkv[:, k, 0:2 * D], start=(k == 0), stop=(k == KD - 1))
                ins.then_inc(qk_ready, 1)
                reach(pe, v_copied, i - 1)
                for k in range(KD):
                    ins = mm(P45[:, z * CH:z * CH + D], uT[h][:, k, tk], w_qkv[:, k, 2 * D:3 * D], start=(k == 0), stop=(k == KD - 1))
                ins.then_inc(v_ready, 1)

            def stack_T(b, t, tells):
                i = NT * b + t
                pe.wait_ge(split_act, 4 * (i + 1))
                pe.wait_ge(part_ready, 3 * (i + 1))
                sp = split[:, t % 2, :].rearrange("p (a h r) -> p a h r", a=2, h=NH)
                for w in range(2):
                    for e, (freed, ready) in enumerate(((stk_act, stkT_act), (stk_dve, stkT_dve))):
                        reach(pe, freed, 2 * (i - 1) + w + 1)
                        if w == 1:
                            reach(pe, u_ready, 2 * (2 * NCH + 6 * b) + 4)
                        bank = (P67, P01)[w][0:SP_ROWS, e * CH:(e + 1) * CH].bitcast(BF16)
                        for hd in range(8):
                            ins = nc.tensor.transpose(bank[:, hd * P:(hd + 1) * P], sp[:, w, 8 * e + hd, :], ident_bf[:, :])
                            if tells and w == 0 and e == 0 and hd == 0:
                                ins.then_inc(u_used, 1)
                        ins.then_inc(ready, 1)

            def max_item(m, k, bank):
                hd, t, half = k // 16, k // 2 % 8, k % 2
                head = bass.ds(QD * m + hd, 1)
                mm(bank,
                   q_st[0:SP_ROWS, head, t * P:(t + 1) * P].rearrange("p a q -> p (a q)"),
                   k_st[0:SP_ROWS, head, half * CH:(half + 1) * CH].rearrange("p a q -> p (a q)"),
                   start=True, stop=True).then_inc(bank_ready, 1)

            def bank_free(base, pos, wide):
                reach(pe, bank_used, base + max(pos - (3 if wide else 1), 0))

            def shift_T(b, m, bank):
                pe.wait_ge(mstep, SHIFT_STEPS * (4 * b + m + 1))
                nc.tensor.transpose(bank[0:3 * QD * NT, 0:P // 2].bitcast(BF16), shift3[:, :],
                                    ident_bf[:, :]).then_inc(bank_ready, 1)

            def out_T(b, m, half, bank):
                reach(pe, pv_copied, 2 * (4 * b + m) + half + 1)
                for j in range(TT):
                    ins = nc.tensor.transpose(bank[:, j * P:(j + 1) * P],
                                              pv_sb[:, half * CH + j * P:half * CH + (j + 1) * P], ident[:, :])
                ins.then_inc(bank_ready, 1)

            def p_v(b, n, t, part):
                if part == 0:
                    reach(pe, p_ready, QD * NT * (4 * b + n) + QD * (t + 1))
                    if t == 0:
                        pe.wait_ge(vq_ready, 4 * b + n + 1)
                if t == 0 and part % (QP // HC) == 0:
                    reach(pe, pv_copied, 2 * (4 * b + n) - 1 + part // (QP // HC))
                tk = slice(part * T // QP, (part + 1) * T // QP)
                first = part % (QP // HC) == 0
                for hd in range(QD):
                    ins = mm(P45[32 * hd:32 * (hd + 1), tk], v_quad[:, t, hd, :], probs[:, t % 2, hd, tk],
                             start=(t == 0 and first), stop=(t == NT - 1 and not first), skip_group_check=True)
                ins.then_inc(pv_step, 1)

            def entry(b, n, base, pos, kind, k):
                wide = isinstance(n, int) and n < 0
                bank = bank_of(pos, wide)
                bank_free(base, pos, wide)
                if kind == "max":
                    max_item(n + 1, k, bank)
                elif kind == "carry":
                    max_item((n + 2) % NQ, k, bank)
                elif kind == "shift":
                    shift_T(b, n + 1, bank)
                else:
                    out_T(b, n - 1, k, bank)

            def quad(b, n, base, with_out, with_max):
                reach(pe, shift_dma, 48 * (4 * b + n + 1))
                pos = 0
                for u in range(QD * NT):
                    t, hd = u // QD, u % QD
                    todo = entries(u, with_out, with_max)
                    for e in range(max(1, len(todo))):
                        if e < len(todo):
                            entry(b, n, base, pos, *todo[e])
                            pos += 1
                        if e == 0:
                            reach(pe, p_ready, QD * NT * (4 * b + n) + u - 1)
                            head = bass.ds(QD * n + hd, 1)
                            for half in range(2):
                                ins = mm((P01, P23)[u % 2][:, half * CH:(half + 1) * CH],
                                         k_st[0:ST_ROWS, head, t * P:(t + 1) * P].rearrange("p a q -> p (a q)"),
                                         q_st[0:ST_ROWS, head, half * CH:(half + 1) * CH].rearrange("p a q -> p (a q)"),
                                         start=True, stop=True)
                            ins.then_inc(st_ready, 1)
                    if t >= 1:
                        p_v(b, n, t - 1, hd)
                    elif with_out:
                        p_v(b, n - 1, NT - 1, hd)

            pe.wait_ge(ld_blk, 16 * 6)
            pe.wait_ge(ones_set, 1)
            with pe.Fori(0, B) as b:
                for h in range(HC):
                    if h == 0:
                        reach(pe, out_used, 2 * (2 * NCH + 4 * b))
                    for t in range(TT * h, TT * (h + 1)):
                        qkv(b, t)
                        if t == 1:
                            transposes(2 * NCH + 6 * b + 1, 2 * NCH + 4 * b + 1, norm_src)
                        if t >= 3:
                            stack_T(b, t - 3, t % TT == TT - 1)
                stack_T(b, NT - 3, False)
                stack_T(b, NT - 2, False)
                stack_T(b, NT - 1, False)
                reach(pe, stk_act, 2 * NT * (b + 1))
                reach(pe, stk_dve, 2 * NT * (b + 1))
                reach(pe, v_copied, NT * (b + 1))
                for pos, (kind, k) in enumerate(prologue_entries()):
                    entry(b, -1, A_BATCH * b, pos, kind, k)
                quad(b, 0, A_BATCH * b + PROLOGUE, False, True)
                with pe.Fori(1, NQ - 1) as n:
                    quad(b, n, before(b, n), True, True)
                quad(b, NQ - 1, before(b, NQ - 1), True, False)
                for part in range(QP):
                    p_v(b, NQ - 1, NT - 1, part)
                for half in range(2):
                    bank_free(before(b, NQ - 1) + WITH_OUT, half, False)
                    out_T(b, NQ - 1, half, bank_of(half, False))
                reach(pe, bank_used, A_BATCH * (b + 1))
                for h in range(HC):
                    g, o = 2 * NCH + 6 * b + 2 + h, 2 * NCH + 4 * b + h
                    transposes(g, None, lambda j: attn[:, TT * h + j, :])
                    reach(pe, u_ready, 2 * g + 2)
                    for j in range(TT):
                        to_tokens(o, j, lambda k, tk: uT[h][:, k, tk], lambda k: w_proj[:, k, :], KD, 1, (TT - 1, KD - 1))
                transposes(2 * NCH + 6 * b + 4, 2 * NCH + 4 * b + 2, norm_src)
                for h in range(HC):
                    c, g, o = HC * b + h, 2 * NCH + 6 * b + 4 + h, 2 * NCH + 4 * b + 2 + h
                    reach(pe, u_ready, 2 * g + 2)
                    for m in range(MC):
                        if m >= 2:
                            pe.wait_ge(gm_done, MC * c + m - 1)
                        for bank, wt in ((P23, w_g1), (P67, w_g3)):
                            for k in range(KD):
                                ins = mm(bank[:, (m % 2) * CH:(m % 2 + 1) * CH], wt[:, k, m * P:(m + 1) * P], uT[h][:, k, :],
                                         start=(k == 0), stop=(k == KD - 1))
                        ins.then_inc(g_ready, 1)
                    transposes(g + 1, 2 * NCH + 4 * b + 2 + h + 1, norm_src)
                    pe.wait_ge(gm_done, MC * c + MC)
                    for j in range(TT):
                        to_tokens(o, j, lambda m, tk: gT[:, m, tk], lambda m: w_g2[:, m, :], MC, None, (0, 0))


INS = ("x", "cond_1024", "pos_S", "L0_cond_Wm", "L0_cond_bm", "L0_cond_Lam_re", "L0_cond_Lam_im", "L0_cond_B_re",
       "L0_cond_B_im", "L0_cond_C_re", "L0_cond_C_im", "L0_cond_D_diag", "L0_cond_log_step", "L0_cond_Wc", "L0_cond_bc",
       "L0_cond_W1", "L0_cond_b1", "L0_cond_W2", "L0_cond_b2", "L1_cond_adaln_w", "L1_cond_adaln_b", "L1_cond_qkv_w",
       "L1_cond_lnq_w", "L1_cond_lnk_w", "L1_cond_proj_w", "L1_cond_proj_b", "L1_cond_w1_w", "L1_cond_w3_w", "L1_cond_w2_w")


def kernel(**inputs):
    import concourse.bacc as bacc
    from concourse.bass_utils import run_bass_kernel_spmd

    nc = bacc.Bacc("TRN2", target_bir_lowering=False, num_devices=1)
    arrays, aps = {}, {}
    for name in INS:
        a = np.ascontiguousarray(inputs[name])
        if name == "x":
            a = a.reshape(B * T, D)
        arrays[f"in_{name}"] = a
        aps[name] = nc.dram_tensor(f"in_{name}", a.shape, mybir.dt.from_np(a.dtype), kind="ExternalInput").ap()
    aps["out"] = nc.dram_tensor("out", (B * T, D), F32, kind="ExternalOutput").ap()
    build(nc, aps)
    r = run_bass_kernel_spmd(nc, [arrays], core_ids=[0])
    return r.results[0]["out"].reshape(B, T, D)
```
